# Optimizing a Trainium2 kernel written in Bass

```python
import numpy as np
import jax
import jax.numpy as jnp

def _softmax(x, axis=-1):
    return jax.nn.softmax(x, axis=axis)

def _gelu(x):
    return jax.nn.gelu(x, approximate=True)

def _silu(x):
    return jax.nn.silu(x)

def _sigmoid(x):
    return jax.nn.sigmoid(x)

def _layernorm(x, axis=-1, eps=1e-05):
    m = jnp.mean(x, axis=axis, keepdims=True)
    v = jnp.var(x, axis=axis, keepdims=True)
    return (x - m) / jnp.sqrt(v + eps)

def _scatter_add(tgt, idx, src, axis=0):
    return tgt.at[idx].add(src)

def _segment_sum(src, seg, n):
    return jax.ops.segment_sum(src, seg, n)
kernel_name = 'mk_perceiver_d1_seqx_r4_608c2c'

def setup_inputs(seed: int=0):
    np.random.seed(seed)
    _w = jnp.asarray

    def _rec_inputs():
        import jax
        import jax.numpy as jnp
        _rk = jax.random.key(seed)
        x = -0.0002928 + 1 * jax.random.normal(jax.random.fold_in(_rk, 1), (64, 32, 256), jnp.float32)
        _lenS = 32 - jax.random.randint(jax.random.fold_in(_rk, 7), (64,), 0, max(1, 32 // 4) + 1, jnp.int32)
        _lenS2 = 257 - jax.random.randint(jax.random.fold_in(_rk, 8), (64,), 0, max(1, 257 // 4) + 1, jnp.int32)
        _ctx_1024P = jax.random.normal(jax.random.fold_in(_rk, 11), (64, 16, 256), jnp.float32)
        _ctx_1024c = jax.random.dirichlet(jax.random.fold_in(_rk, 511), 0.3 * jnp.ones((16,), jnp.float32), (64, 257))
        _ctx_1024t = jnp.einsum('bsk,bkd->bsd', _ctx_1024c, _ctx_1024P)
        _ctx_1024t = _ctx_1024t * jax.lax.rsqrt(jnp.mean(jnp.square(_ctx_1024t)) + 1e-12) * 0.953939
        ctx_1024 = -1.39393e-06 + 0.999914 * (_ctx_1024t + 0.3 * jax.random.normal(jax.random.fold_in(_rk, 611), (64, 257, 256), jnp.float32))
        return (x, ctx_1024)
    x, ctx_1024 = _rec_inputs()

    def _L0_xattn_setup():
        import jax, jax.numpy as jnp
        import numpy as np
        EMBED_DIM = 256
        NUM_HEADS = 16
        HEAD_DIM = EMBED_DIM // NUM_HEADS
        SCALE_BASE = EMBED_DIM

        def xpos_apply(x, downscale):
            L, D = (x.shape[1], x.shape[2])
            half = D // 2
            base = (jnp.arange(0, D, 2, dtype=jnp.float32) + 0.4 * D) / (1.4 * D)
            pos = jnp.arange(L, dtype=jnp.float32)
            scale = base[None, :] ** (pos[:, None] / SCALE_BASE)
            inv_freq = 1.0 / 10000.0 ** (jnp.arange(half, dtype=jnp.float32) / half)
            sinusoid = pos[:, None] * inv_freq[None, :]
            sin, cos = (jnp.sin(sinusoid), jnp.cos(sinusoid))
            if downscale:
                scale = 1.0 / scale
            sin_s = jnp.repeat(sin * scale, 2, axis=-1)
            cos_s = jnp.repeat(cos * scale, 2, axis=-1)
            x1, x2 = (x[..., ::2], x[..., 1::2])
            rot = jnp.stack([-x2, x1], axis=-1).reshape(x.shape)
            return x * cos_s + rot * sin_s
        key = jax.random.key(seed)
        ks = jax.random.split(key, 12)
        B, L, E = (2, 512, EMBED_DIM)
        s = 1.0 / np.sqrt(E)
        inp = {'query': jax.random.normal(ks[0], (B, L, E), jnp.float32), 'key': jax.random.normal(ks[1], (B, L, E), jnp.float32), 'value': jax.random.normal(ks[2], (B, L, E), jnp.float32), 'Wq': jax.random.normal(ks[3], (E, E), jnp.float32) * s, 'bq': jax.random.normal(ks[4], (E,), jnp.float32) * 0.01, 'Wk': jax.random.normal(ks[5], (E, E), jnp.float32) * s, 'bk': jax.random.normal(ks[6], (E,), jnp.float32) * 0.01, 'Wv': jax.random.normal(ks[7], (E, E), jnp.float32) * s, 'bv': jax.random.normal(ks[8], (E,), jnp.float32) * 0.01, 'Wo': jax.random.normal(ks[9], (E, E), jnp.float32) * s, 'bo': jax.random.normal(ks[10], (E,), jnp.float32) * 0.01}
        return inp
    _L0_xattn_all = _L0_xattn_setup()
    _L0_xattn_in = {k: v for k, v in _L0_xattn_all.items() if k in ('Wq', 'bq', 'Wk', 'bk', 'Wv', 'bv', 'Wo', 'bo')}
    del _L0_xattn_all

    def _L0_attn_setup():
        import jax, jax.numpy as jnp
        import numpy as np
        B, S, D, H, FACTOR = (1, 512, 256, 16, 16)
        HD = D // H
        key = jax.random.key(seed)
        ks = jax.random.split(key, 9)
        s = 1.0 / np.sqrt(D)
        u = lambda k, shape: jax.random.uniform(k, shape, jnp.float32, -s, s)
        return {'x': jax.random.normal(ks[0], (B, S, D), jnp.float32), 'Wq': u(ks[1], (D, D)), 'bq': u(ks[2], (D,)), 'Wk': u(ks[3], (D, D)), 'bk': u(ks[4], (D,)), 'Wv': u(ks[5], (D, D)), 'bv': u(ks[6], (D,)), 'Wo': u(ks[7], (D, D)), 'bo': u(ks[8], (D,))}
    _L0_attn_all = _L0_attn_setup()
    _L0_attn_in = {k: v for k, v in _L0_attn_all.items() if k in ('Wq', 'bq', 'Wk', 'bk', 'Wv', 'bv', 'Wo', 'bo')}
    del _L0_attn_all

    def _L0_ffn_setup():
        import jax, jax.numpy as jnp
        import numpy as np
        B, S, D, F, E = (2, 512, 256, 1024, 8)
        LN_EPS = 1e-05

        def _layer_norm(x, gamma, beta):
            mu = jnp.mean(x, axis=-1, keepdims=True)
            var = jnp.mean(jnp.square(x - mu), axis=-1, keepdims=True)
            return (x - mu) * jax.lax.rsqrt(var + LN_EPS) * gamma + beta
        key = jax.random.key(seed)
        ks = jax.random.split(key, 8)

        def xavier(k, shape):
            fan_in, fan_out = (shape[-1], shape[-2])
            a = jnp.sqrt(6.0 / (fan_in + fan_out))
            return jax.random.uniform(k, shape, jnp.float32, -a, a)
        return {'tgt': jax.random.normal(ks[0], (B, S, D), jnp.float32), 'Wr': xavier(ks[1], (E, D)), 'br': jnp.zeros((E,), jnp.float32), 'W1': xavier(ks[2], (E, F, D)), 'b1': jnp.zeros((E, F), jnp.float32), 'W2': xavier(ks[3], (E, D, F)), 'b2': jnp.zeros((E, D), jnp.float32), 'gamma': jnp.ones((D,), jnp.float32), 'beta': jnp.zeros((D,), jnp.float32)}
    _L0_ffn_all = _L0_ffn_setup()
    _L0_ffn_in = {k: v for k, v in _L0_ffn_all.items() if k in ('Wr', 'br', 'W1', 'b1', 'W2', 'b2', 'gamma', 'beta')}
    del _L0_ffn_all
    return {'x': x, 'ctx_1024': ctx_1024, 'L0_xattn_Wq': _L0_xattn_in['Wq'], 'L0_xattn_bq': _L0_xattn_in['bq'], 'L0_xattn_Wk': _L0_xattn_in['Wk'], 'L0_xattn_bk': _L0_xattn_in['bk'], 'L0_xattn_Wv': _L0_xattn_in['Wv'], 'L0_xattn_bv': _L0_xattn_in['bv'], 'L0_xattn_Wo': _L0_xattn_in['Wo'], 'L0_xattn_bo': _L0_xattn_in['bo'], 'L0_attn_Wq': _L0_attn_in['Wq'], 'L0_attn_bq': _L0_attn_in['bq'], 'L0_attn_Wk': _L0_attn_in['Wk'], 'L0_attn_bk': _L0_attn_in['bk'], 'L0_attn_Wv': _L0_attn_in['Wv'], 'L0_attn_bv': _L0_attn_in['bv'], 'L0_attn_Wo': _L0_attn_in['Wo'], 'L0_attn_bo': _L0_attn_in['bo'], 'L0_ffn_Wr': _L0_ffn_in['Wr'], 'L0_ffn_br': _L0_ffn_in['br'], 'L0_ffn_W1': _L0_ffn_in['W1'], 'L0_ffn_b1': _L0_ffn_in['b1'], 'L0_ffn_W2': _L0_ffn_in['W2'], 'L0_ffn_b2': _L0_ffn_in['b2'], 'L0_ffn_gamma': _L0_ffn_in['gamma'], 'L0_ffn_beta': _L0_ffn_in['beta']}

def reference(x, ctx_1024, L0_xattn_Wq, L0_xattn_bq, L0_xattn_Wk, L0_xattn_bk, L0_xattn_Wv, L0_xattn_bv, L0_xattn_Wo, L0_xattn_bo, L0_attn_Wq, L0_attn_bq, L0_attn_Wk, L0_attn_bk, L0_attn_Wv, L0_attn_bv, L0_attn_Wo, L0_attn_bo, L0_ffn_Wr, L0_ffn_br, L0_ffn_W1, L0_ffn_b1, L0_ffn_W2, L0_ffn_b2, L0_ffn_gamma, L0_ffn_beta):
    import jax
    import jax.numpy as jnp

    def _L0_xattn_ref(query, key, value, Wq, bq, Wk, bk, Wv, bv, Wo, bo):
        import jax, jax.numpy as jnp
        import numpy as np
        EMBED_DIM = 256
        NUM_HEADS = 16
        HEAD_DIM = EMBED_DIM // NUM_HEADS
        SCALE_BASE = EMBED_DIM

        def xpos_apply(x, downscale):
            L, D = (x.shape[1], x.shape[2])
            half = D // 2
            base = (jnp.arange(0, D, 2, dtype=jnp.float32) + 0.4 * D) / (1.4 * D)
            pos = jnp.arange(L, dtype=jnp.float32)
            scale = base[None, :] ** (pos[:, None] / SCALE_BASE)
            inv_freq = 1.0 / 10000.0 ** (jnp.arange(half, dtype=jnp.float32) / half)
            sinusoid = pos[:, None] * inv_freq[None, :]
            sin, cos = (jnp.sin(sinusoid), jnp.cos(sinusoid))
            if downscale:
                scale = 1.0 / scale
            sin_s = jnp.repeat(sin * scale, 2, axis=-1)
            cos_s = jnp.repeat(cos * scale, 2, axis=-1)
            x1, x2 = (x[..., ::2], x[..., 1::2])
            rot = jnp.stack([-x2, x1], axis=-1).reshape(x.shape)
            return x * cos_s + rot * sin_s
        B, T, E = query.shape
        S = key.shape[1]
        H, D = (NUM_HEADS, HEAD_DIM)
        scaling = D ** (-0.5)
        q = (query @ Wq.T + bq) * scaling
        k = key @ Wk.T + bk
        v = value @ Wv.T + bv

        def split_heads(x, L):
            return x.reshape(B, L, H, D).transpose(0, 2, 1, 3).reshape(B * H, L, D)
        q = split_heads(q, T)
        k = split_heads(k, S)
        v = split_heads(v, S)
        k = xpos_apply(k, downscale=True)
        q = xpos_apply(q, downscale=False)
        attn_weights = jnp.einsum('btd,bsd->bts', q, k)
        attn_weights = jax.nn.softmax(attn_weights.astype(jnp.float32), axis=-1).astype(q.dtype)
        attn = jnp.einsum('bts,bsd->btd', attn_weights, v)
        attn = attn.reshape(B, H, T, D).transpose(0, 2, 1, 3).reshape(B, T, E)
        return attn @ Wo.T + bo

    def _L0_attn_ref(x, Wq, bq, Wk, bk, Wv, bv, Wo, bo):
        import jax, jax.numpy as jnp
        import numpy as np
        B, S, D, H, FACTOR = (1, 512, 256, 16, 16)
        HD = D // H
        b, s, d = x.shape
        h, hd = (H, HD)
        q = (x @ Wq + bq).reshape(b, s, h, hd).transpose(0, 2, 1, 3)
        k = (x @ Wk + bk).reshape(b, s, h, hd).transpose(0, 2, 1, 3)
        v = (x @ Wv + bv).reshape(b, s, h, hd).transpose(0, 2, 1, 3)
        scores = jnp.einsum('bhqd,bhkd->bhqk', q, k) / np.sqrt(hd).astype(np.float32)
        vals, idx = jax.lax.top_k(scores, FACTOR)
        flat_scores = scores.reshape(-1, s)
        rows = jnp.arange(flat_scores.shape[0])[:, None]
        sparse = jnp.zeros_like(flat_scores).at[rows, idx.reshape(-1, FACTOR)].set(vals.reshape(-1, FACTOR)).reshape(scores.shape)
        attn = jax.nn.softmax(sparse, axis=-1)
        out = jnp.einsum('bhqk,bhkd->bhqd', attn, v)
        out = out.transpose(0, 2, 1, 3).reshape(b, s, d)
        return out @ Wo + bo

    def _L0_ffn_ref(tgt, Wr, br, W1, b1, W2, b2, gamma, beta):
        import jax, jax.numpy as jnp
        import numpy as np
        B, S, D, F, E = (2, 512, 256, 1024, 8)
        LN_EPS = 1e-05

        def _layer_norm(x, gamma, beta):
            mu = jnp.mean(x, axis=-1, keepdims=True)
            var = jnp.mean(jnp.square(x - mu), axis=-1, keepdims=True)
            return (x - mu) * jax.lax.rsqrt(var + LN_EPS) * gamma + beta
        logits = jnp.einsum('bsd,ed->bse', tgt, Wr) + br
        top_v, top_i = jax.lax.top_k(logits, 2)
        top_w = jax.nn.softmax(top_v, axis=-1)
        n_exp = logits.shape[-1]
        router_w = jnp.sum(jax.nn.one_hot(top_i, n_exp, dtype=top_w.dtype) * top_w[..., None], axis=-2)
        h = jnp.einsum('bsd,efd->bsef', tgt, W1) + b1
        h = jax.nn.relu(h)
        o = jnp.einsum('bsef,edf->bsed', h, W2) + b2
        tgt2 = jnp.einsum('bsed,bse->bsd', o, router_w)
        return _layer_norm(tgt + tgt2, gamma, beta)
    x = x + _L0_xattn_ref(_layernorm(x, axis=-1), ctx_1024, ctx_1024, L0_xattn_Wq, L0_xattn_bq, L0_xattn_Wk, L0_xattn_bk, L0_xattn_Wv, L0_xattn_bv, L0_xattn_Wo, L0_xattn_bo)
    x = x + _L0_attn_ref(_layernorm(x, axis=-1), L0_attn_Wq, L0_attn_bq, L0_attn_Wk, L0_attn_bk, L0_attn_Wv, L0_attn_bv, L0_attn_Wo, L0_attn_bo)
    x = x + _L0_ffn_ref(_layernorm(x, axis=-1), L0_ffn_Wr, L0_ffn_br, L0_ffn_W1, L0_ffn_b1, L0_ffn_W2, L0_ffn_b2, L0_ffn_gamma, L0_ffn_beta)
    return x

_drawn_inputs = setup_inputs


def setup_inputs(seed=0):
    import zlib

    import numpy as np

    out = dict(_drawn_inputs(seed))
    spreads = {'L0_ffn_br': (0.0, 0.1),
     'L0_ffn_b1': (0.0, 0.267),
     'L0_ffn_b2': (0.0, 0.1),
     'L0_ffn_gamma': (1.0, 0.2),
     'L0_ffn_beta': (0.0, 0.1)}
    factors = {'L0_xattn_bq': 6.935,
     'L0_xattn_bk': 7.343,
     'L0_xattn_bv': 3.429,
     'L0_xattn_bo': 3.935,
     'L0_attn_Wq': 3.453,
     'L0_attn_bq': 8.0,
     'L0_attn_Wk': 3.64,
     'L0_attn_bk': 50.347}
    for name, (base, spread) in spreads.items():
        noise = np.random.default_rng([zlib.crc32(name.encode()), seed]).standard_normal(out[name].shape)
        drawn = base * np.exp(spread * noise) if base else spread * noise
        out[name] = jnp.asarray(drawn.astype(out[name].dtype))
    for name, factor in factors.items():
        out[name] = (out[name] * factor).astype(out[name].dtype)
    return out
```

```python
from contextlib import ExitStack

import numpy as np

import concourse.bass as bass
from concourse import mybir

P = 128
B, T, D, S = 64, 32, 256, 257
SP = S + 1
H, HD = 16, 16
TOK = B * T
NT = TOK // P
C = D // P
BLK = 4
NB = NT // BLK
HH = H // C
TOPK = 16
E, F = 8, 1024
FC = F // P
LN_EPS = 1e-5
TAKEN = -3.0e38

F32 = mybir.dt.float32
F32R = mybir.dt.float32r
U32 = mybir.dt.uint32
ALU = mybir.AluOpType
ACT = mybir.ActivationFunctionType
AX = mybir.AxisListType.X
ds = bass.ds

CONSTS = {}


def build_consts():
    cols = {}
    p = np.arange(P)
    cols["ident"] = np.eye(P)
    cols["delta"] = (p[:, None] % T == np.arange(T)[None, :])
    chan = np.arange(P)
    for gl in range(2):
        cols[f"pick{gl}"] = (chan[None, :] // 64 == gl) & (chan[None, :] % 64 // HD == p[:, None] // T)
    cols["parity"] = np.stack([p // HD % 2 == 0, p // HD % 2 == 1], 1)
    cols["iota"] = np.tile(np.arange(E), (P, 1))
    half = HD // 2
    base = ((np.arange(0, HD, 2, dtype=np.float32) + np.float32(0.4 * HD)) / np.float32(1.4 * HD)).astype(np.float32)
    inv_freq = (1.0 / np.float32(10000.0) ** (np.arange(half, dtype=np.float32) / half)).astype(np.float32)
    for name, length, down, factor in (("k", S, True, 1.0), ("q", T, False, HD ** -0.5)):
        pos = np.arange(length, dtype=np.float32)
        scale = base[None, :] ** (pos[:, None] / np.float32(D))
        if down:
            scale = np.float32(1.0) / scale
        angle = pos[:, None] * inv_freq[None, :]
        pair = p % HD // 2
        cos = (np.cos(angle) * scale * factor)[:, pair].T
        sin = (np.sin(angle) * scale * factor)[:, pair].T * np.where(p % 2 == 0, 1.0, -1.0)[:, None]
        if length % 2:
            cos, sin = np.pad(cos, ((0, 0), (0, 1))), np.pad(sin, ((0, 0), (0, 1)))
        cols[name + "cos"], cols[name + "sin"] = cos, sin
    at = 0
    for name, a in cols.items():
        CONSTS[name] = (at, a.shape[1])
        at += a.shape[1]
    return np.ascontiguousarray(np.concatenate([np.asarray(a, np.float32) for a in cols.values()], 1))


build_consts()
NCONST = sum(n for _, n in CONSTS.values())
QX, KX, VX, QA, KA, VA = range(6)
BOX, BOA, GAMMA, BETA = range(4)


def perceiver(nc, x, ctx_t, ctx_last, w_x, w_a, bias_cols, bias_rows, w_r, b_r, w_1, b_1, w_2, b_2, consts, out):
    with ExitStack() as stack:
        def sb(name, shape, dt=F32):
            return stack.enter_context(nc.sbuf_tensor(name, shape, dt))

        def sem(name):
            return stack.enter_context(nc.semaphore(name))

        cst = sb("cst", [P, NCONST])
        wx = sb("wx", [P, 4, C, D])
        wa = sb("wa", [P, 4, C, D])
        bcol = sb("bcol", [P, 6, C])
        brow = sb("brow", [P, 4, D])
        wr = sb("wr", [P, C, E])
        br = sb("br", [P, E])
        xs = sb("xs", [P, NT, D])
        xnrm = sb("xnrm", [P, BLK, D])
        stats = sb("stats", [P, BLK, 6])
        mv = sb("mv", [P, BLK, 2])
        rstd = sb("rstd", [P, BLK])
        vareps = sb("vareps", [P, BLK])
        nhalf = sb("nhalf", [P, BLK])
        bvb = sb("bvb", [P, 2, C, P])
        ocorr = sb("ocorr", [P, 2, D])
        ps = stack.enter_context(nc.psum_tensor("ps", [P, 8, 512], F32))

        def const(name):
            at, n = CONSTS[name]
            return cst[:, at:at + n]

        ident, delta, parity = const("ident"), const("delta"), const("parity")

        s_load = sem("s_load")
        s_set = sem("s_set")
        s_pset = sem("s_pset")
        s_corr_mm = sem("s_corr_mm")
        s_vlast_mm = sem("s_vlast_mm")
        s_st = sem("s_st")
        s_rstd = sem("s_rstd")
        s_xn = sem("s_xn")
        s_tr = sem("s_tr")
        s_xta = sem("s_xta")
        s_xtd = sem("s_xtd")
        s_block = sem("s_block")
        s_done = sem("s_done")

        NLOAD = 9

        def wait_apart(eng, semaphore, value):
            value = value if isinstance(value, int) else eng.to_reg(value)
            eng.wait_ge(s_load, 16 * NLOAD)
            eng.wait_ge(semaphore, value)

        def ln_stats(v, tile_of, n):
            for t in range(BLK):
                nc.vector.bn_stats(stats[:, t, :], tile_of(t)).then_inc(s_st, 1)
            wait_apart(v, s_st, 8 * n + 4)
            for t in range(BLK):
                nc.vector.bn_aggr(mv[:, t, :], stats[:, t, :]).then_inc(s_st, 1)

        def ln_apply(v, tile_of, n):
            v.wait_ge(s_rstd, 2 * n + 2)
            for t in range(BLK):
                nc.vector.tensor_scalar(xnrm[:, t, :], tile_of(t), mv[:, t, 0:1], rstd[:, t:t + 1],
                                        ALU.subtract, ALU.mult).then_inc(s_xn, 1)

        def ln_rstd(g, n):
            wait_apart(g, s_st, 8 * n + 8)
            nc.gpsimd.tensor_scalar(vareps[:], mv[:, :, 1], LN_EPS, None, ALU.add).then_inc(s_rstd, 1)
            g.wait_ge(s_rstd, 2 * n + 1)
            nc.gpsimd.tensor_tensor(rstd[:], vareps[:], nhalf[:], ALU.pow).then_inc(s_rstd, 1)

        def transpose_block(pe, n):
            for t in range(BLK):
                pe.wait_ge(s_xn, 4 * n + t + 1)
                for c in range(C):
                    ins = nc.tensor.transpose(ps[:, c, t * P:(t + 1) * P], xnrm[:, t, c * P:(c + 1) * P], ident)
                    if t == BLK - 1:
                        ins.then_inc(s_tr, 1)

        late = ExitStack()
        xT = late.enter_context(nc.sbuf_tensor("xT", [P, C, BLK * P], F32))

        a_ = ExitStack()

        def asb(name, shape, dt=F32):
            return a_.enter_context(nc.sbuf_tensor(name, shape, dt))

        attn_t = late.enter_context(nc.sbuf_tensor("attn_t", [P, C, TOK], F32))
        wk_hl = asb("wk_hl", [P, 2, C, D], F32R)
        wv_hl = asb("wv_hl", [P, 2, C, D], F32R)
        q_hl = asb("q_hl", [P, 2, C, TOK], F32R)
        clast = asb("clast", [P, C, B])
        vlast = asb("vlast", [P, C, B])
        raw = asb("raw", [P, 2, C, SP])
        cx = asb("cx", [P, 2, 2, C, SP], F32R)
        kb = asb("kb", [P, 2, C, SP])
        kc = asb("kc", [P, 2, C, SP])
        ks = asb("ks", [P, 2, C, SP])
        kw = asb("kw", [P, 2, C, SP])
        kt = asb("kt", [P, 2, C, SP])
        khl = asb("khl", [P, 2, 2, C, SP], F32R)
        vv = asb("vv", [P, 4, 2, D])
        qbd = asb("qbd", [P, 2, 2, C, HH, 2 * T], F32R)
        room = asb("room", [P, 4 * 4 * SP])
        qb, qc, qs, qw = (room[:, 1024 * i:1024 * (i + 1)].rearrange("p (c t) -> p c t", c=C) for i in range(4))
        pexp = room[:].rearrange("p (s g k) -> p s g k", s=4, g=4)
        negmax = asb("negmax", [P, 4, 4])
        rsum = asb("rsum", [P, 4, 4])
        rrec = asb("rrec", [P, 2, 2, 4])
        pt = asb("pt", [P, 2, 2, 512])
        dg = asb("dg", [P, 2, 4, 2, 2, T])
        f1 = asb("f1", [P, 2, C, T])
        f2 = asb("f2", [P, 2, C, T])
        f3 = asb("f3", [P, C, 2, T])
        f4 = asb("f4", [P, C, 2, T])

        s_q = sem("s_q")
        s_qb = sem("s_qb")
        s_qd = sem("s_qd")
        ctx_in = [sem(f"ctx_in{i}") for i in range(2)]
        kw_in = [sem(f"kw_in{i}") for i in range(2)]
        qbd_in = [sem(f"qbd_in{i}") for i in range(2)]
        s_split = sem("s_split")
        s_K = sem("s_K")
        s_V = sem("s_V")
        s_kev = sem("s_kev")
        s_vev = sem("s_vev")
        s_kc = sem("s_kc")
        s_ks = sem("s_ks")
        s_kadd = sem("s_kadd")
        s_khl = sem("s_khl")
        s_S = sem("s_S")
        s_max = sem("s_max")
        s_exp = sem("s_exp")
        s_T = sem("s_T")
        s_pt0 = sem("s_pt0")
        s_pt1 = sem("s_pt1")
        s_pv = sem("s_pv")
        s_rec = sem("s_rec")
        s_dg = sem("s_dg")
        s_L = sem("s_L")
        s_f = sem("s_f")
        s_fin = sem("s_fin")

        J0, J1 = 1, 14

        def has(j, u, k):
            return not isinstance(j, int) or 0 <= 4 * j + u + k < B

        def cross_steps(eng, step):
            for b in range(-6, 4 * J0):
                step(b // 4, b % 4)
            with eng.Fori(J0, J1) as j:
                for u in range(4):
                    step(j, u)
            for b in range(4 * J1, B):
                step(b // 4, b % 4)

        def nth(j, m, slots, per):
            return (4 // slots * j + m // slots + 1) * per

        a_.close()

        b_ = ExitStack()

        def bsb(name, shape, dt=F32):
            return b_.enter_context(nc.sbuf_tensor(name, shape, dt))

        x2n = bsb("x2n", [P, NT, D])
        x2t = bsb("x2t", [P, C, TOK])
        logits = bsb("logits", [P, NT, E])
        ast = bsb("ast", [P, C, BLK * P])
        qt_all = bsb("qt_all", [P, C, TOK])
        kt_all = bsb("kt_all", [P, C, TOK])
        v_all = bsb("v_all", [P, NT, D])
        bq4 = bsb("bq4", [P, C])
        kbd = bsb("kbd", [P, 2, C, HH, P])
        qst = bsb("qst", [P, 2, C, P])
        vst = bsb("vst", [P, 2, D])
        top_a = bsb("top_a", [P, 2, H, 8])
        top_b = bsb("top_b", [P, H, 8])
        left_a = bsb("left_a", [P, H, T])
        left_b = bsb("left_b", [P, H, T])
        kept = bsb("kept", [P, 2, H, T])
        rmax = bsb("rmax", [P, 2, H])
        shifted = bsb("shifted", [P, 2, H, T])
        pr = bsb("pr", [P, 2, H, T])
        prs = bsb("prs", [P, H])
        prr = bsb("prr", [P, H])
        prn = bsb("prn", [P, H, T])
        prt = bsb("prt", [P, 2, H, T])
        g1 = bsb("g1", [P, C, 4, T])
        at2 = bsb("at2", [P, 2, C, P])
        st2 = bsb("st2", [P, 8])
        xn2 = bsb("xn2", [P, 2, D])
        xt2 = bsb("xt2", [P, 2, C, P])

        ast_in = sem("ast_in")
        s_wo = sem("s_wo")
        s_x1 = sem("s_x1")
        s_corr2 = sem("s_corr2")
        s_qk = sem("s_qk")
        s_qkev = sem("s_qkev")
        s_v2 = sem("s_v2")
        s_v2ev = sem("s_v2ev")
        s_b0 = sem("s_b0")
        kq_in = [sem(f"kq_in{i}") for i in range(2)]
        v_in = [sem(f"v_in{i}") for i in range(2)]
        s_S2 = sem("s_S2")
        s_top = sem("s_top")
        s_kept = sem("s_kept")
        s_sub = sem("s_sub")
        s_e2 = sem("s_e2")
        s_red = sem("s_red")
        s_prt = sem("s_prt")
        s_pv2 = sem("s_pv2")
        s_g = sem("s_g")
        s_wo2 = sem("s_wo2")
        s_x2 = sem("s_x2")
        s_st2 = sem("s_st2")
        s_rs2 = sem("s_rs2")
        s_xn2 = sem("s_xn2")
        s_tr2 = sem("s_tr2")
        s_xt2 = sem("s_xt2")
        s_rt = sem("s_rt")
        s_lg = sem("s_lg")
        x2n_in = sem("x2n_in")

        M0, M1 = 1, 6

        def has2(m, u, k):
            return not isinstance(m, int) or 0 <= 2 * m + u + k < NT

        def self_steps(eng, step):
            for j in range(-3, 2 * M0):
                step(j // 2, j % 2)
            with eng.Fori(M0, M1) as m:
                for u in range(2):
                    step(m, u)
            for j in range(2 * M1, NT):
                step(j // 2, j % 2)

        def nth2(m, u, k, per):
            return (m + (u + k) // 2 + 1) * per

        def blocks(eng, body):
            body(0)
            with eng.Fori(1, NB) as k:
                body(k)

        def later(k):
            return not isinstance(k, int) or k > 0

        b_.close()

        c_ = ExitStack()

        def csb(name, shape, dt=F32):
            return c_.enter_context(nc.sbuf_tensor(name, shape, dt))

        x2n_ = csb("x2n_c", [P, NT, D])
        x2t_ = csb("x2t_c", [P, C, TOK])
        logits_ = csb("logits_c", [P, NT, E])
        acc = csb("acc", [P, NT, D])
        w1s = csb("w1s", [P, 2, C, F])
        w2s = csb("w2s", [P, 2, FC, D])
        hid = csb("hid", [P, FC, 512])
        b1s = csb("b1s", [P, E, FC])
        b2s = csb("b2s", [E, D])
        rank = csb("rank", [P, NT, 8])
        rix = csb("rix", [P, NT, 8], U32)
        rixf = csb("rixf", [P, NT, 2])
        rdiff = csb("rdiff", [P, NT])
        rexp = csb("rexp", [P, NT])
        rtmp = csb("rtmp", [P, NT])
        rwt = csb("rwt", [P, NT, 2])
        hot = csb("hot", [P, 2, NT, E])
        rw = csb("rw", [P, NT, E])
        rwT = csb("rwT", [E, NT, P])
        yo = csb("yo", [P, 2, BLK, D])

        w_in = [sem(f"w_in{i}") for i in range(2)]
        s_ix = sem("s_ix")
        s_r = sem("s_r")
        s_rexp = sem("s_rexp")
        s_rwT = sem("s_rwT")
        s_rwTs = sem("s_rwTs")
        s_acc0 = sem("s_acc0")
        s_acc1 = sem("s_acc1")
        s_hid = sem("s_hid")
        s_relu = sem("s_relu")
        s_o = sem("s_o")
        s_acc = sem("s_acc")
        s_y = sem("s_y")
        s_yy = sem("s_yy")
        s_r0 = sem("s_r0")
        c_.close()

        stack.enter_context(late)
        block = stack.enter_context(nc.Block())

        @block.sync
        def _(sp):
            sp.dma_start(cst[:], consts).then_inc(s_load, 16)
            sp.dma_start(wx[:], w_x).then_inc(s_load, 16)
            sp.dma_start(xs[:], x.rearrange("(j p) c -> p j c", p=P)).then_inc(s_load, 16)
            sp.dma_start(wa[:], w_a).then_inc(s_load, 16)
            sp.dma_start(bcol[:], bias_cols).then_inc(s_load, 16)
            sp.dma_start(brow[:], bias_rows).then_inc(s_load, 16)
            sp.dma_start(clast[:], ctx_last).then_inc(s_load, 16)
            sp.dma_start(wr[:], w_r).then_inc(s_load, 16)
            sp.dma_start(br[:], b_r).then_inc(s_load, 16)

            def fill_queries(slot, first):
                for h in range(HH):
                    rows = slice(HD * h, HD * (h + 1))
                    sp.dma_start(qbd[rows, slot, :, :, h, :].bitcast(F32), q_hl[rows, :, :, ds(first, 2 * T)].bitcast(F32)).then_inc(qbd_in[slot], 16)

            def step(j, u):
                if has(j, u, 2):
                    m, slot = u + 2, (u + 2) % 2
                    wait_apart(sp, s_ks, 4 * j + m + 1)
                    if has(j, u, 0):
                        sp.wait_ge(s_kadd, 4 * j + u + 1)
                    sp.dma_start(kw[0:P:2, slot], ks[1:P:2, slot]).then_inc(kw_in[slot], 16)
                    sp.dma_start(kw[1:P:2, slot], ks[0:P:2, slot]).then_inc(kw_in[slot], 16)
                if has(j, u, 6):
                    m, slot = u + 6, (u + 6) % 2
                    if has(j, u, 4):
                        wait_apart(sp, s_split, 2 * (4 * j + u + 5))
                    sp.dma_start(raw[:, slot], ctx_t[ds(4 * j + m, 1)].rearrange("a p c s -> p (a c) s")).then_inc(ctx_in[slot], 16)
                if u % 2 == 0 and has(j, u, 1) and has(j, u, 5):
                    wait_apart(sp, s_S, 2 * (4 * j + u + 2))
                    fill_queries((u // 2) % 2, 128 * j + 32 * u + 4 * T)

            for b in range(-6, -2):
                step(b // 4, b % 4)
            sp.wait_ge(s_qd, 6 * NB)
            fill_queries(0, 0)
            fill_queries(1, 2 * T)
            for b in range(-2, 4 * J0):
                step(b // 4, b % 4)
            with sp.Fori(J0, J1) as j:
                for u in range(4):
                    step(j, u)
            for b in range(4 * J1, B):
                step(b // 4, b % 4)
            sp.wait_ge(s_fin, B // 2)
            def stage(k):
                if later(k):
                    wait_apart(sp, s_wo, 4 * k)
                sp.dma_start(ast[:], attn_t[:, :, ds(512 * k, 512)]).then_inc(ast_in, 16)

            blocks(sp, stage)
            sp.wait_ge(s_v2ev, 2 * NB)
            sp.wait_ge(s_qkev, 4 * NB)
            sp.wait_ge(s_b0, 2)

            def step2(m, u):
                if has2(m, u, 3):
                    slot = (u + 3) % 2
                    if has2(m, u, 1):
                        wait_apart(sp, s_S2, 2 * m + u + 2)
                    first = 256 * m + 128 * (u + 3)
                    sp.dma_start(qst[:, slot], qt_all[:, :, ds(first, P)]).then_inc(kq_in[slot], 16)
                    for h in range(HH):
                        rows = slice(HD * h, HD * (h + 1))
                        sp.dma_start(kbd[rows, slot, :, h, :], kt_all[rows, :, ds(first, P)]).then_inc(kq_in[slot], 16)
                if has2(m, u, 1):
                    slot = (u + 1) % 2
                    if has2(m, u, -1):
                        wait_apart(sp, s_pv2, 2 * m + u)
                    sp.dma_start(vst[:, slot], v_all[:, ds(2 * m + u + 1, 1), :].rearrange("p a d -> p (a d)")).then_inc(v_in[slot], 16)
                if has2(m, u, 0):
                    wait_apart(sp, s_xn2, 2 * m + u + 1)
                    sp.dma_start(x2n[:, ds(2 * m + u, 1), :].rearrange("p a d -> p (a d)"), xn2[:, u]).then_inc(x2n_in, 16)

            self_steps(sp, step2)
            sp.wait_ge(s_lg, NT)
            sp.wait_ge(x2n_in, 16 * NT)
            sp.dma_start(b1s[:], b_1).then_inc(s_ix, 16)
            sp.dma_start(b2s[:], b_2).then_inc(s_ix, 16)
            for e in range(E):
                if e >= 2:
                    sp.wait_ge(s_acc, NT * (e - 1))
                sp.dma_start(w1s[:, e % 2], w_1[e]).then_inc(w_in[e % 2], 16)
                sp.dma_start(w2s[:, e % 2], w_2[e]).then_inc(w_in[e % 2], 16)
            out_v = out.rearrange("(j p) c -> p j c", p=P)

            def store(k):
                wait_apart(sp, s_y, k + 1)
                sp.dma_start(out_v[:, ds(4 * k, 4), :], yo[:, 0]).then_inc(s_done, 16)

            blocks(sp, store)
            sp.wait_ge(s_done, 16 * NB)

        @block.gpsimd
        def _(g):
            nc.gpsimd.memset(nhalf[:], -0.5).then_inc(s_pset, 1)
            g.wait_ge(s_pset, 1)
            with g.Fori(0, NB) as k:
                ln_rstd(g, k)
            g.wait_ge(s_xn, NT)
            g.wait_ge(s_set, 9)
            nc.gpsimd.tensor_tensor(xs[:], xs[:], ocorr[:, 0, :].unsqueeze(1).to_broadcast([P, NT, D]), ALU.add).then_inc(s_pset, 1)

            def step(j, u):
                if has(j, u, 2):
                    m, slot = u + 2, (u + 2) % 2
                    g.wait_ge(s_kev, 2 * (4 * j + m + 1))
                    if has(j, u, 0):
                        g.wait_ge(kw_in[slot], nth(j, u, 2, 32))
                    nc.gpsimd.tensor_tensor(ks[:, slot], kb[:, slot], const("ksin").unsqueeze(1).to_broadcast([P, C, SP]),
                                            ALU.mult).then_inc(s_ks, 1)
                if has(j, u, 4):
                    m, slot = u + 4, (u + 4) % 2
                    wait_apart(g, ctx_in[slot], nth(j, m, 2, 16))
                    if has(j, u, 2):
                        g.wait_ge(s_V, 4 * j + u + 3)
                    nc.gpsimd.tensor_scalar(cx[:, slot, 0], raw[:, slot], 1.0, None, ALU.mult).then_inc(s_split, 1)
                    g.wait_ge(s_split, 2 * (4 * j + m) + 1)
                    nc.gpsimd.tensor_tensor(cx[:, slot, 1], raw[:, slot], cx[:, slot, 0].bitcast(F32), ALU.subtract).then_inc(s_split, 1)
                if u % 2 == 1 and has(j, u, 0):
                    pair, slot = 2 * j + u // 2, u // 2
                    g.wait_ge(s_exp, 4 * (4 * j + u + 1))
                    g.wait_ge(s_rec, pair + 1)
                    if has(j, u, -4):
                        g.wait_ge(s_L, pair - 1)
                    dl = delta.unsqueeze(1).unsqueeze(1).to_broadcast([P, 2, 4, T])
                    nc.gpsimd.tensor_tensor(dg[:, slot, :, 0].rearrange("p g b t -> p b g t"),
                                            pexp[:, u - 1:u + 1, :, S - 1:S].to_broadcast([P, 2, 4, T]), dl, ALU.mult).then_inc(s_dg, 1)
                    nc.gpsimd.tensor_tensor(dg[:, slot, :, 1].rearrange("p g b t -> p b g t"),
                                            rrec[:, slot].unsqueeze(3).to_broadcast([P, 2, 4, T]), dl, ALU.mult).then_inc(s_dg, 1)

            cross_steps(g, step)
            g.wait_ge(s_fin, B // 2)
            nc.gpsimd.memset(kbd[:], 0.0).then_inc(s_b0, 1)

            def block2(k):
                ln_rstd(g, k + NB)
                wait_apart(g, s_xn, 4 * (k + NB) + 4)
                rows = xs[:, ds(4 * k, 4), :]
                nc.gpsimd.tensor_tensor(rows, rows, ocorr[:, 1, :].unsqueeze(1).to_broadcast([P, BLK, D]), ALU.add).then_inc(s_corr2, 1)

            blocks(g, block2)

            def step2(m, u):
                if has2(m, u, 0):
                    n = 2 * m + u
                    wait_apart(g, s_st2, 2 * n + 2)
                    nc.gpsimd.tensor_scalar(st2[:, 2:3], st2[:, 1:2], LN_EPS, None, ALU.add).then_inc(s_rs2, 1)
                    g.wait_ge(s_rs2, 2 * n + 1)
                    nc.gpsimd.tensor_tensor(rstd[:, 0:1], st2[:, 2:3], nhalf[:, 0:1], ALU.pow).then_inc(s_rs2, 1)
                if has2(m, u, 1):
                    n, slot = 2 * m + u + 1, (u + 1) % 2
                    g.wait_ge(s_kept, 2 * n + 2)
                    if has2(m, u, -1):
                        g.wait_ge(s_e2, n - 1)
                    nc.gpsimd.tensor_tensor(shifted[:, slot], kept[:, slot], rmax[:, slot].unsqueeze(2).to_broadcast([P, H, T]),
                                            ALU.subtract).then_inc(s_sub, 1)

            self_steps(g, step2)
            for k in range(NB):
                ln_rstd(g, 2 * NB + k)

        @block.scalar
        def _(act):
            act.wait_ge(s_load, 16 * NLOAD)
            with act.Fori(0, NB) as k:
                act.wait_ge(s_tr, 2 * k + 1)
                nc.scalar.copy(xT[:, 0, :], ps[:, 0, :]).then_inc(s_xta, 1)
                for hf in range(C):
                    act.wait_ge(s_q, 2 * k + hf + 1)
                    nc.scalar.activation(qb[:, hf, :], ps[:, 2 + hf, :], ACT.Identity, bias=bcol[:, QX, hf:hf + 1]).then_inc(s_qb, 1)

            def step(j, u):
                if has(j, u, 0):
                    act.wait_ge(s_T, 2 * (4 * j + u) + 1)
                    if has(j, u, -2):
                        act.wait_ge(s_pv, 4 * j + u - 1)
                    nc.scalar.copy(pt[:, u % 2, 0], ps[:, 0, :]).then_inc(s_pt0, 1)
                if has(j, u, 1):
                    m, slot = u + 1, (u + 1) % 4
                    if has(j, u, -3):
                        act.wait_ge(s_T, 2 * (4 * j + u - 2))
                        act.wait_ge(s_dg, 2 * (2 * j + (u - 3) // 2 + 1))
                    for g in range(4):
                        if g % 2 == 0:
                            act.wait_ge(s_max, 2 * (4 * j + m) + g // 2 + 1)
                        nc.scalar.activation(pexp[:, slot, g, 0:S], ps[:, 3 + g, 0:S], ACT.Exp, bias=negmax[:, slot, g:g + 1],
                                             accum_out=rsum[:, slot, g:g + 1]).then_inc(s_exp, 1)
                if has(j, u, 3):
                    m, slot = u + 3, (u + 3) % 2
                    if has(j, u, 1):
                        act.wait_ge(s_kc, 4 * j + u + 2)
                        act.wait_ge(s_ks, 4 * j + u + 2)
                    for hf in range(C):
                        act.wait_ge(s_K, 2 * (4 * j + m) + hf + 1)
                        nc.scalar.activation(kb[:, slot, hf, :], ps[:, hf, 0:SP], ACT.Identity, bias=bcol[:, KX, hf:hf + 1]).then_inc(s_kev, 1)
                    act.wait_ge(s_V, 4 * j + m + 1)
                    if has(j, u, -1):
                        act.wait_ge(s_pv, 4 * j + u)
                    nc.scalar.copy(vv[:, m % 4].rearrange("p c d -> p (c d)"), ps[:, 2, :]).then_inc(s_vev, 1)

            cross_steps(act, step)
            act.wait_ge(s_b0, 2)

            def block2(k):
                n = k + NB
                act.wait_ge(s_tr, 2 * n + 1)
                nc.scalar.copy(xT[:, 0, :], ps[:, 0, :]).then_inc(s_xta, 1)
                for i, (dst, bias, scale, hf) in enumerate(((qt_all, bq4, HD ** -0.5, 0), (qt_all, bq4, HD ** -0.5, 1),
                                                            (kt_all, bcol[:, KA], 1.0, 0), (kt_all, bcol[:, KA], 1.0, 1))):
                    act.wait_ge(s_qk, 4 * k + i + 1)
                    nc.scalar.activation(dst[:, hf, ds(512 * k, 512)], ps[:, (2, 3, 6, 7)[i], :], ACT.Identity, bias=bias[:, hf:hf + 1],
                                         scale=scale).then_inc(s_qkev, 1)

            blocks(act, block2)

            def step2(m, u):
                if has2(m, u, 0):
                    n = 2 * m + u
                    act.wait_ge(s_tr2, n + 1)
                    if has2(m, u, -2):
                        act.wait_ge(s_rt, n - 1)
                    src = ps[:, 7, 0:D].rearrange("p (c t) -> p c t", c=C)
                    nc.scalar.copy(xt2[:, u], src).then_inc(s_xt2, 1)
                    nc.scalar.copy(x2t[:, :, ds(256 * m + 128 * u, P)], src).then_inc(s_xt2, 1)
                if has2(m, u, 1):
                    n, slot = 2 * m + u + 1, (u + 1) % 2
                    act.wait_ge(s_sub, n + 1)
                    if has2(m, u, -1):
                        act.wait_ge(s_red, 3 * (n - 1))
                    nc.scalar.activation(pr[:, slot], shifted[:, slot], ACT.Exp).then_inc(s_e2, 1)

            self_steps(act, step2)
            act.wait_ge(s_r, 1)
            nc.scalar.activation(rexp[:], rdiff[:], ACT.Exp).then_inc(s_rexp, 1)
            for e in range(E):
                def chunk(i):
                    for f in range(FC):
                        act.wait_ge(s_hid, FC * (NB * e + i) + f + 1)
                        if f == 0 and (e or later(i)):
                            act.wait_ge(s_o, NB * (NB * e + i))
                        nc.scalar.activation(hid[:, f, :], ps[:, f % 4, :], ACT.Relu, bias=b1s[:, e, f:f + 1]).then_inc(s_relu, 1)
                blocks(act, chunk)

        @block.vector
        def _(v):
            nc.vector.memset(qbd[:].bitcast(F32), 0.0).then_inc(s_set, 1)
            v.wait_ge(s_load, 16 * NLOAD)
            for w, src in ((wk_hl, wx[:, 1]), (wv_hl, wx[:, 2])):
                nc.vector.tensor_copy(w[:, 0], src).then_inc(s_set, 1)
            v.wait_ge(s_set, 3)
            for w, src in ((wk_hl, wx[:, 1]), (wv_hl, wx[:, 2])):
                nc.vector.tensor_tensor(w[:, 1], src, w[:, 0].bitcast(F32), ALU.subtract).then_inc(s_set, 1)
            for i, col in enumerate((VX, VA)):
                nc.vector.tensor_copy(bvb[:, i], bcol[:, col, :].unsqueeze(2).to_broadcast([P, C, P])).then_inc(s_set, 1)
            v.wait_ge(s_corr_mm, 1)
            for i, row in enumerate((BOX, BOA)):
                nc.vector.tensor_tensor(ocorr[:, i, :], ps[:, 4, i * D:(i + 1) * D], brow[:, row, :], ALU.add).then_inc(s_set, 1)
            v.wait_ge(s_vlast_mm, 1)
            nc.vector.tensor_copy(vlast[:], ps[:, 5, 0:C * B].rearrange("p (c b) -> p c b", c=C)).then_inc(s_set, 1)

            with v.Fori(0, NB) as k:
                def tile_of(t):
                    return xs[:, ds(4 * k + t, 1), :].rearrange("p a d -> p (a d)")
                ln_stats(v, tile_of, k)
                ln_apply(v, tile_of, k)
                v.wait_ge(s_tr, 2 * k + 2)
                nc.vector.tensor_copy(xT[:, 1, :], ps[:, 1, :]).then_inc(s_xtd, 1)
                v.wait_ge(s_qb, 2 * k + 2)
                by_pos = lambda a: a.rearrange("p c (b t) -> p (c b) t", t=T)
                by_pair = lambda a: a.rearrange("p c (i b t) -> p (c i) b t", b=2, t=T)
                by_latent = lambda a: a.rearrange("p c (i t b) -> p (c i) b t", b=2, t=T)
                for dst, tab in ((qc, "qcos"), (qs, "qsin")):
                    nc.vector.tensor_tensor(by_pos(dst), by_pos(qb), const(tab).unsqueeze(1).to_broadcast([P, C * BLK * 4, T]),
                                            ALU.mult).then_inc(s_qd, 1)
                wait_apart(v, s_qd, 6 * k + 2)
                nc.vector.stream_shuffle(qw, qs, [i ^ 1 for i in range(32)]).then_inc(s_qd, 1)
                v.wait_ge(s_qd, 6 * k + 3)
                nc.vector.tensor_tensor(by_latent(qb), by_pair(qc), by_pair(qw), ALU.add).then_inc(s_qd, 1)
                v.wait_ge(s_qd, 6 * k + 4)
                nc.vector.tensor_copy(q_hl[:, 0, :, ds(512 * k, 512)], qb).then_inc(s_qd, 1)
                v.wait_ge(s_qd, 6 * k + 5)
                nc.vector.tensor_tensor(q_hl[:, 1, :, ds(512 * k, 512)], qb, q_hl[:, 0, :, ds(512 * k, 512)].bitcast(F32),
                                        ALU.subtract).then_inc(s_qd, 1)

            def step(j, u):
                if has(j, u, 0):
                    v.wait_ge(s_T, 2 * (4 * j + u) + 2)
                    if has(j, u, -2):
                        v.wait_ge(s_pv, 4 * j + u - 1)
                    nc.vector.tensor_copy(pt[:, u % 2, 1], ps[:, 1, :]).then_inc(s_pt1, 1)
                if has(j, u, 1):
                    m, slot = u + 1, (u + 1) % 4
                    if has(j, u, -3):
                        v.wait_ge(s_exp, 4 * (4 * j + u - 2))
                    for hf in range(C):
                        v.wait_ge(s_S, 2 * (4 * j + m) + hf + 1)
                        nc.vector.tensor_reduce(negmax[:, slot, 2 * hf:2 * hf + 2], ps[:, 3 + 2 * hf:5 + 2 * hf, 0:S], axis=AX,
                                                op=ALU.max, negate=True).then_inc(s_max, 1)
                if u % 2 == 1 and has(j, u, 0):
                    pair, slot = 2 * j + u // 2, u // 2
                    v.wait_ge(s_exp, 4 * (4 * j + u + 1))
                    if has(j, u, -4):
                        v.wait_ge(s_dg, 2 * (pair - 1))
                    nc.vector.reciprocal(rrec[:, slot], rsum[:, u - 1:u + 1]).then_inc(s_rec, 1)
                if has(j, u, 2):
                    m, slot = u + 2, (u + 2) % 2
                    n = 4 * j + m
                    v.wait_ge(s_kev, 2 * (n + 1))
                    nc.vector.tensor_tensor(kc[:, slot], kb[:, slot], const("kcos").unsqueeze(1).to_broadcast([P, C, SP]),
                                            ALU.mult).then_inc(s_kc, 1)
                    v.wait_ge(kw_in[slot], nth(j, m, 2, 32))
                    v.wait_ge(s_kc, n + 1)
                    if has(j, u, 0):
                        v.wait_ge(s_khl, 2 * (4 * j + u + 1))
                    nc.vector.tensor_tensor(kt[:, slot], kc[:, slot], kw[:, slot], ALU.add).then_inc(s_kadd, 1)
                    v.wait_ge(s_kadd, n + 1)
                    if has(j, u, 0):
                        v.wait_ge(s_S, 2 * (4 * j + u + 1))
                    nc.vector.tensor_copy(khl[:, slot, 0], kt[:, slot]).then_inc(s_khl, 1)
                    v.wait_ge(s_khl, 2 * n + 1)
                    nc.vector.tensor_tensor(khl[:, slot, 1], kt[:, slot], khl[:, slot, 0].bitcast(F32), ALU.subtract).then_inc(s_khl, 1)
                if u % 2 == 1 and has(j, u, 0):
                    pair = 2 * j + u // 2
                    both = ps[:, 7, 0:256].rearrange("p (b c r t) -> p b c r t", b=2, c=C, r=2)
                    sel = ps[:, 7, 256:512].rearrange("p (c w b t) -> p c w b t", c=C, w=2, b=2)
                    v.wait_ge(s_L, pair + 1)
                    nc.vector.tensor_scalar(f1[:].rearrange("p b c t -> p (b c) t"), both[:, :, :, 0, :].rearrange("p b c t -> p (b c) t"),
                                            parity[:, 0:1], None, ALU.mult).then_inc(s_f, 1)
                    nc.vector.tensor_tensor(f3[:], sel[:, :, 0], vlast[:, :, ds(4 * j + u - 1, 2)].unsqueeze(3).to_broadcast([P, C, 2, T]),
                                            ALU.mult).then_inc(s_f, 1)
                    v.wait_ge(s_f, 4 * pair + 1)
                    nc.vector.scalar_tensor_tensor(f2[:].rearrange("p b c t -> p (b c) t"), both[:, :, :, 1, :].rearrange("p b c t -> p (b c) t"),
                                                   parity[:, 1:2], f1[:].rearrange("p b c t -> p (b c) t"), ALU.mult, ALU.add).then_inc(s_f, 1)
                    v.wait_ge(s_f, 4 * pair + 3)
                    nc.vector.tensor_tensor(f4[:], f3[:], f2[:].rearrange("p b c t -> p c b t"), ALU.add).then_inc(s_f, 1)
                    v.wait_ge(s_f, 4 * pair + 4)
                    nc.vector.tensor_tensor(attn_t[:, :, ds(128 * j + 32 * (u - 1), 2 * T)].rearrange("p c (b t) -> p c b t", t=T), f4[:],
                                            sel[:, :, 1], ALU.mult).then_inc(s_fin, 1)

            cross_steps(v, step)
            v.wait_ge(s_pv, B)
            nc.vector.tensor_scalar(bq4[:], bcol[:, QA, :], HD ** -0.5, None, ALU.mult).then_inc(s_b0, 1)

            def block2(k):
                n = k + NB
                def tile_of(t):
                    return xs[:, ds(4 * k + t, 1), :].rearrange("p a d -> p (a d)")
                for t in range(BLK):
                    v.wait_ge(s_wo, 4 * k + t // 2 * 2 + 2)
                    nc.vector.tensor_tensor(tile_of(t), ps[:, 4 + t // 2, t % 2 * D:(t % 2 + 1) * D], tile_of(t), ALU.add).then_inc(s_x1, 1)
                wait_apart(v, s_x1, 4 * k + 4)
                ln_stats(v, tile_of, n)
                ln_apply(v, tile_of, n)
                v.wait_ge(s_tr, 2 * n + 2)
                nc.vector.tensor_copy(xT[:, 1, :], ps[:, 1, :]).then_inc(s_xtd, 1)
                for i in range(2):
                    v.wait_ge(s_v2, 2 * k + i + 1)
                    nc.vector.tensor_copy(v_all[:, ds(4 * k + 2 * i, 2), :].rearrange("p a d -> p (a d)"), ps[:, 4 + i, :]).then_inc(s_v2ev, 1)

            blocks(v, block2)

            def step2(m, u):
                slot, nslot = u, (u + 1) % 2
                n = 2 * m + u
                scores = ps[:, nslot, :].rearrange("p (h k) -> p h k", h=H)

                def rank_pass(i):
                    if not has2(m, u, 1):
                        return
                    if i == 0:
                        wait_apart(v, s_S2, n + 2)
                    else:
                        wait_apart(v, s_top, 64 * (n + 1) + 16 * i)
                    for h in range(H):
                        if i == 0:
                            ins = nc.vector.max(top_a[:, nslot, h, :], scores[:, h, :])
                        elif i == 1:
                            ins = nc.vector.match_replace(left_a[:, h, :], top_a[:, nslot, h, :], scores[:, h, :], TAKEN)
                        elif i == 2:
                            ins = nc.vector.max(top_b[:, h, :], left_a[:, h, :])
                        else:
                            ins = nc.vector.match_replace(left_b[:, h, :], top_b[:, h, :], left_a[:, h, :], TAKEN)
                        ins.then_inc(s_top, 1)

                rank_pass(0)
                if has2(m, u, -1):
                    v.wait_ge(s_rt, n)
                    nc.vector.tensor_tensor(logits[:, ds(n - 1, 1), :].rearrange("p a e -> p (a e)"), ps[:, 6, D:D + E], br[:], ALU.add).then_inc(s_lg, 1)
                if has2(m, u, 0):
                    wait_apart(v, s_e2, n + 1)
                    nc.vector.tensor_reduce(prs[:], pr[:, slot], axis=AX, op=ALU.add).then_inc(s_red, 1)
                    v.wait_ge(s_red, 3 * n + 1)
                    nc.vector.reciprocal(prr[:], prs[:]).then_inc(s_red, 1)
                    v.wait_ge(s_red, 3 * n + 2)
                    nc.vector.tensor_tensor(prn[:], pr[:, slot], prr[:].unsqueeze(2).to_broadcast([P, H, T]), ALU.mult).then_inc(s_red, 1)
                    if has2(m, u, -2):
                        v.wait_ge(s_pv2, n - 1)
                    v.wait_ge(s_red, 3 * n + 3)
                    nc.vector.transpose(prt[:, slot].rearrange("p h k -> p (h k)"), prn[:].rearrange("p h k -> p (h k)")).then_inc(s_prt, 1)
                rank_pass(1)
                if has2(m, u, 0):
                    v.wait_ge(s_pv2, n + 1)
                    if has2(m, u, -2):
                        v.wait_ge(s_wo2, n - 1)
                    for hf in range(C):
                        nc.vector.tensor_scalar(g1[:, hf], ps[:, 2:6, hf * 64:hf * 64 + T], parity[:, 0:1], None, ALU.mult).then_inc(s_g, 1)
                    for hf in range(C):
                        v.wait_ge(s_g, 4 * n + 1 + hf)
                        nc.vector.scalar_tensor_tensor(at2[:, slot, hf].rearrange("p (b t) -> p b t", t=T),
                                                       ps[:, 2:6, hf * 64 + T:hf * 64 + 2 * T], parity[:, 1:2], g1[:, hf],
                                                       ALU.mult, ALU.add).then_inc(s_g, 1)
                rank_pass(2)
                if has2(m, u, 0):
                    row = xs[:, ds(n, 1), :].rearrange("p a d -> p (a d)")
                    v.wait_ge(s_wo2, n + 1)
                    nc.vector.tensor_tensor(row, ps[:, 6, 0:D], row, ALU.add).then_inc(s_x2, 1)
                    wait_apart(v, s_x2, n + 1)
                    nc.vector.bn_stats(stats[:, 0, :], row).then_inc(s_st2, 1)
                    wait_apart(v, s_st2, 2 * n + 1)
                    nc.vector.bn_aggr(st2[:, 0:2], stats[:, 0, :]).then_inc(s_st2, 1)
                rank_pass(3)
                if has2(m, u, 1):
                    if has2(m, u, -1):
                        v.wait_ge(s_sub, n)
                    wait_apart(v, s_top, 64 * (n + 2))
                    nc.vector.scalar_tensor_tensor(kept[:, nslot], left_b[:], 0.1 * TAKEN, scores, ALU.is_lt, ALU.mult).then_inc(s_kept, 1)
                    nc.vector.tensor_scalar(rmax[:, nslot], top_a[:, nslot, :, 0], 0.0, None, ALU.max).then_inc(s_kept, 1)
                if has2(m, u, 0):
                    v.wait_ge(s_rs2, 2 * n + 2)
                    if has2(m, u, -2):
                        v.wait_ge(x2n_in, 16 * (n - 1))
                        v.wait_ge(s_tr2, n - 1)
                    nc.vector.tensor_scalar(xn2[:, slot], row, st2[:, 0:1], rstd[:, 0:1], ALU.subtract, ALU.mult).then_inc(s_xn2, 1)

            self_steps(v, step2)
            v.wait_ge(s_rt, NT)
            nc.vector.tensor_tensor(logits[:, NT - 1, :], ps[:, 6, D:D + E], br[:], ALU.add).then_inc(s_lg, 1)

            v.wait_ge(s_lg, NT)
            for t in range(NT):
                nc.vector.max(rank[:, t, :], logits[:, t, :]).then_inc(s_r0, 1)
            v.wait_ge(s_r0, NT)
            for t in range(NT):
                nc.vector.max_index(rix[:, t, :], rank[:, t, :], logits[:, t, :]).then_inc(s_r0, 1)
            nc.vector.tensor_tensor(rdiff[:], rank[:, :, 1], rank[:, :, 0], ALU.subtract).then_inc(s_r, 1)
            v.wait_ge(s_r0, 2 * NT)
            nc.vector.tensor_copy(rixf[:], rix[:, :, 0:2]).then_inc(s_r, 1)
            v.wait_ge(s_rexp, 1)
            nc.vector.tensor_scalar(rtmp[:], rexp[:], 1.0, None, ALU.add).then_inc(s_r, 1)
            v.wait_ge(s_r, 3)
            nc.vector.reciprocal(rwt[:, :, 0], rtmp[:]).then_inc(s_r, 1)
            v.wait_ge(s_r, 4)
            nc.vector.tensor_tensor(rwt[:, :, 1], rwt[:, :, 0], rexp[:], ALU.mult).then_inc(s_r, 1)
            for i in range(2):
                nc.vector.tensor_tensor(hot[:, i], const("iota").unsqueeze(1).to_broadcast([P, NT, E]),
                                        rixf[:, :, i:i + 1].to_broadcast([P, NT, E]), ALU.is_equal).then_inc(s_r, 1)
            v.wait_ge(s_r, 7)
            for i in range(2):
                nc.vector.tensor_tensor(hot[:, i], hot[:, i], rwt[:, :, i:i + 1].to_broadcast([P, NT, E]), ALU.mult).then_inc(s_r, 1)
            v.wait_ge(s_r, 9)
            nc.vector.tensor_tensor(rw[:], hot[:, 0], hot[:, 1], ALU.add).then_inc(s_r, 1)
            for q in range(NB):
                v.wait_ge(s_rwT, q + 1)
                nc.vector.tensor_copy(rwT[:, 4 * q:4 * q + 4, :].rearrange("e a p -> e (a p)"), ps[0:E, q, :]).then_inc(s_rwTs, 1)
            for q in range(NT // 2):
                v.wait_ge(s_acc0, q + 1)
                nc.vector.tensor_tensor(acc[:, 2 * q:2 * q + 2, :].rearrange("p a d -> p (a d)"), ps[:, 4 + q % 4, :],
                                        x2n[:, 2 * q:2 * q + 2, :].rearrange("p a d -> p (a d)"), ALU.add).then_inc(s_acc1, 1)
            v.wait_ge(s_acc1, NT // 2)
            for e in range(E):
                def chunk(i):
                    for t in range(BLK):
                        n = NT * e + 4 * i + t
                        v.wait_ge(s_o, n + 1)
                        if e:
                            v.wait_ge(s_acc, n + 1 - NT)
                        row = acc[:, ds(4 * i + t, 1), :].rearrange("p a d -> p (a d)")
                        nc.vector.scalar_tensor_tensor(row, ps[:, 4 + t, 0:D],
                                                       rw[:, ds(4 * i + t, 1), e:e + 1].rearrange("p a e -> p (a e)"), row,
                                                       ALU.mult, ALU.add).then_inc(s_acc, 1)
                blocks(v, chunk)
            v.wait_ge(s_acc, E * NT)
            for k in range(NB):
                tile_of = lambda t: acc[:, 4 * k + t, :]
                ln_stats(v, tile_of, 2 * NB + k)
                ln_apply(v, tile_of, 2 * NB + k)
                v.wait_ge(s_xn, 4 * (2 * NB + k) + 4)
                nc.vector.tensor_tensor(xnrm[:], xnrm[:], brow[:, GAMMA, :].unsqueeze(1).to_broadcast([P, BLK, D]), ALU.mult).then_inc(s_yy, 1)
                v.wait_ge(s_yy, 2 * k + 1)
                nc.vector.tensor_tensor(xnrm[:], xnrm[:], brow[:, BETA, :].unsqueeze(1).to_broadcast([P, BLK, D]), ALU.add).then_inc(s_yy, 1)
                v.wait_ge(s_yy, 2 * k + 2)
                if k:
                    v.wait_ge(s_done, 16 * k)
                nc.vector.tensor_tensor(yo[:, 0], xnrm[:], xs[:, 4 * k:4 * k + 4, :], ALU.add).then_inc(s_y, 1)

        @block.tensor
        def _(pe):
            pe.wait_ge(s_load, 16 * NLOAD)
            pe.wait_ge(s_set, 7)
            for i, w in enumerate((wx, wa)):
                for c in range(C):
                    ins = nc.tensor.matmul(ps[:, 4, i * D:(i + 1) * D], bvb[:, i, c, :], w[:, 3, c, :], start=c == 0, stop=c == C - 1)
            ins.then_inc(s_corr_mm, 1)
            for hf in range(C):
                for c in range(C):
                    ins = nc.tensor.matmul(ps[:, 5, hf * B:(hf + 1) * B], wx[:, 2, c, hf * P:(hf + 1) * P], clast[:, c, :],
                                           start=c == 0, stop=c == C - 1)
            ins.then_inc(s_vlast_mm, 1)
            with pe.Fori(0, NB) as k:
                transpose_block(pe, k)
                pe.wait_ge(s_xta, k + 1)
                pe.wait_ge(s_xtd, k + 1)
                for hf in range(C):
                    for c in range(C):
                        ins = nc.tensor.matmul(ps[:, 2 + hf, :], wx[:, 0, c, hf * P:(hf + 1) * P], xT[:, c, :], start=c == 0, stop=c == C - 1)
                    ins.then_inc(s_q, 1)

            pe.wait_ge(s_qb, 2 * NB)
            pe.wait_ge(s_set, 10)

            def split_product(dst, lhs, rhs, chunks):
                terms = [(a, b, c) for c in range(chunks) for a, b in ((0, 0), (0, 1), (1, 0))]
                for i, (a, b, c) in enumerate(terms):
                    ins = nc.tensor.matmul(dst, lhs(a, c), rhs(b, c), start=i == 0, stop=i == len(terms) - 1)
                return ins

            def step(j, u):
                if has(j, u, 0):
                    pe.wait_ge(s_exp, 4 * (4 * j + u + 1))
                    if has(j, u, 2):
                        pe.wait_ge(s_kev, 2 * (4 * j + u + 3))
                    for c in range(2):
                        for g in range(4):
                            ins = nc.tensor.transpose(ps[:, c, g * P:(g + 1) * P], pexp[:, u, g, c * P:(c + 1) * P], ident)
                        ins.then_inc(s_T, 1)
                if has(j, u, 1):
                    m = u + 1
                    pair, slot = (m % 4) // 2, m % 2
                    pe.wait_ge(s_khl, 2 * (4 * j + m + 1))
                    if m % 2 == 0:
                        pe.wait_ge(qbd_in[pair], (j + m // 4 + 1) * 16 * HH)
                    for g in range(4):
                        hf, gl = g // 2, g % 2
                        ins = split_product(ps[:, 3 + g, 0:SP],
                                            lambda a, c: qbd[:, pair, a, hf].rearrange("p h x -> p (h x)")[:, 8 * T * gl + slot:8 * T * (gl + 1):2],
                                            lambda b, c: khl[:, slot, b, hf, :], 1)
                        if gl == 1:
                            ins.then_inc(s_S, 1)
                if has(j, u, 0):
                    b = 4 * j + u
                    pe.wait_ge(s_pt0, b + 1)
                    pe.wait_ge(s_pt1, b + 1)
                    pe.wait_ge(s_vev, b + 1)
                    if u % 2 == 0 and has(j, u, -1):
                        pe.wait_ge(s_fin, 2 * j + u // 2)
                    for hf in range(C):
                        for c in range(2):
                            for i in range(4):
                                col = (u % 2) * 128 + hf * 64
                                ins = nc.tensor.matmul(ps[32 * i:32 * i + 32, 7, col:col + 64],
                                                       vv[:, u, c, hf * P + 32 * i:hf * P + 32 * i + 32],
                                                       pt[:, u % 2, c, hf * 256 + 64 * i:hf * 256 + 64 * i + 64],
                                                       start=c == 0, stop=c == 1)
                    ins.then_inc(s_pv, 1)
                    if u % 2 == 1:
                        pe.wait_ge(s_dg, 2 * (2 * j + u // 2 + 1))
                        for hf in range(C):
                            for gl in range(2):
                                ins = nc.tensor.matmul(ps[:, 7, 256 + 128 * hf:384 + 128 * hf], const(f"pick{gl}"),
                                                       dg[:, u // 2, 2 * hf + gl].rearrange("p w b t -> p (w b t)"),
                                                       start=gl == 0, stop=gl == 1)
                        ins.then_inc(s_L, 1)
                if has(j, u, 3):
                    m, slot = u + 3, (u + 3) % 2
                    if has(j, u, 2) and not has(j, u, 0):
                        pe.wait_ge(s_kev, 2 * (4 * j + m))
                    pe.wait_ge(s_split, 2 * (4 * j + m + 1))
                    for hf in range(C):
                        split_product(ps[:, hf, 0:SP], lambda a, c: wk_hl[:, a, c, hf * P:(hf + 1) * P],
                                      lambda b, c: cx[:, slot, b, c, :], C).then_inc(s_K, 1)
                    if has(j, u, 2):
                        pe.wait_ge(s_vev, 4 * j + m)
                    for sc in range(2):
                        ins = split_product(ps[:, 2, sc * D:(sc + 1) * D], lambda a, c: cx[:, slot, a, c, sc * P:(sc + 1) * P],
                                            lambda b, c: wv_hl[:, b, c, :], C)
                    ins.then_inc(s_V, 1)

            cross_steps(pe, step)
            pe.wait_ge(s_fin, B // 2)

            def block2(k):
                n = k + NB
                if later(k):
                    pe.wait_ge(s_v2ev, 2 * k)
                pe.wait_ge(ast_in, 16 * (k + 1))
                for t in range(BLK):
                    for c in range(C):
                        ins = nc.tensor.matmul(ps[:, 4 + t // 2, t % 2 * D:(t % 2 + 1) * D], ast[:, c, t * P:(t + 1) * P], wx[:, 3, c, :],
                                               start=c == 0, stop=c == C - 1)
                    ins.then_inc(s_wo, 1)
                transpose_block(pe, n)
                pe.wait_ge(s_xta, n + 1)
                pe.wait_ge(s_xtd, n + 1)
                if later(k):
                    pe.wait_ge(s_qkev, 4 * k)
                for i in range(4):
                    w, hf = i // 2, i % 2
                    for c in range(C):
                        ins = nc.tensor.matmul(ps[:, (2, 3, 6, 7)[i], :], wa[:, w, c, hf * P:(hf + 1) * P], xT[:, c, :],
                                               start=c == 0, stop=c == C - 1)
                    ins.then_inc(s_qk, 1)
                for t in range(BLK):
                    for c in range(C):
                        ins = nc.tensor.matmul(ps[:, 4 + t // 2, t % 2 * D:(t % 2 + 1) * D], xT[:, c, t * P:(t + 1) * P], wa[:, 2, c, :],
                                               start=c == 0, stop=c == C - 1)
                    if t % 2:
                        ins.then_inc(s_v2, 1)

            blocks(pe, block2)
            pe.wait_ge(s_v2ev, 2 * NB)
            pe.wait_ge(s_qkev, 4 * NB)

            def step2(m, u):
                n = 2 * m + u
                if has2(m, u, 0):
                    wait_apart(pe, s_prt, n + 1)
                    wait_apart(pe, v_in[u], nth2(m, u, 0, 16))
                    if has2(m, u, -1):
                        wait_apart(pe, s_g, 4 * n)
                    for hf in range(C):
                        for i in range(4):
                            for b in range(4):
                                ins = nc.tensor.matmul(ps[32 * i:32 * i + 32, 2 + b, hf * 64:hf * 64 + 64],
                                                       vst[32 * b:32 * b + 32, u, hf * P + 32 * i:hf * P + 32 * i + 32],
                                                       prt[32 * b:32 * b + 32, u, HH * hf + 2 * i:HH * hf + 2 * i + 2, :],
                                                       start=True, stop=True)
                    ins.then_inc(s_pv2, 1)
                    pe.wait_ge(s_g, 4 * n + 4)
                    if has2(m, u, -1):
                        pe.wait_ge(s_lg, n)
                    for c in range(C):
                        ins = nc.tensor.matmul(ps[:, 6, 0:D], at2[:, u, c, :], wa[:, 3, c, :], start=c == 0, stop=c == C - 1)
                    ins.then_inc(s_wo2, 1)
                if has2(m, u, 2):
                    slot = u
                    pe.wait_ge(kq_in[slot], nth2(m, u, 2, 16 * (HH + 1)))
                    if has2(m, u, 0):
                        pe.wait_ge(s_kept, 2 * n + 2)
                    for b in range(4):
                        for hf in range(C):
                            ins = nc.tensor.matmul(ps[32 * b:32 * b + 32, slot, hf * 256:(hf + 1) * 256], qst[:, slot, hf, 32 * b:32 * b + 32],
                                                   kbd[:, slot, hf, :, 32 * b:32 * b + 32], start=True, stop=True)
                    ins.then_inc(s_S2, 1)
                if has2(m, u, 0):
                    pe.wait_ge(s_xn2, n + 1)
                    if has2(m, u, -1):
                        pe.wait_ge(s_xt2, 2 * n)
                    for c in range(C):
                        ins = nc.tensor.transpose(ps[:, 7, c * P:(c + 1) * P], xn2[:, u, c * P:(c + 1) * P], ident)
                    ins.then_inc(s_tr2, 1)
                    pe.wait_ge(s_x2, n + 1)
                    pe.wait_ge(s_xt2, 2 * n + 1)
                    for c in range(C):
                        ins = nc.tensor.matmul(ps[:, 6, D:D + E], xt2[:, u, c, :], wr[:, c, :], start=c == 0, stop=c == C - 1)
                    ins.then_inc(s_rt, 1)

            self_steps(pe, step2)
            pe.wait_ge(s_lg, NT)
            pe.wait_ge(s_xt2, 2 * NT)
            pe.wait_ge(s_r, 10)
            pe.wait_ge(s_ix, 32)
            for t in range(NT):
                ins = nc.tensor.transpose(ps[0:E, t // 4, t % 4 * P:(t % 4 + 1) * P], rw[:, t, :], ident)
                if t % 4 == 3:
                    ins.then_inc(s_rwT, 1)
            for t in range(NT):
                pe.wait_ge(s_rwTs, t // 4 + 1)
                if t >= 8 and t % 2 == 0:
                    pe.wait_ge(s_acc1, t // 2 - 3)
                ins = nc.tensor.matmul(ps[:, 4 + t // 2 % 4, t % 2 * D:(t % 2 + 1) * D], rwT[:, t, :], b2s[:], start=True, stop=True)
                if t % 2:
                    ins.then_inc(s_acc0, 1)
            pe.wait_ge(s_rwTs, NB)
            pe.wait_ge(s_acc1, NT // 2)
            for e in range(E):
                pe.wait_ge(w_in[e % 2], 32 * (e // 2 + 1))

                def chunk(i):
                    n = NB * e + i
                    for f in range(FC):
                        if f >= 4 or e or later(i):
                            pe.wait_ge(s_relu, FC * n + f - 3)
                        for c in range(C):
                            ins = nc.tensor.matmul(ps[:, f % 4, :], w1s[:, e % 2, c, f * P:(f + 1) * P], x2t[:, c, ds(512 * i, 512)],
                                                   start=c == 0, stop=c == C - 1)
                        ins.then_inc(s_hid, 1)
                    pe.wait_ge(s_relu, FC * n + FC)
                    for t in range(BLK):
                        if e or later(i):
                            pe.wait_ge(s_acc, 4 * n + t - 3)
                        for f in range(FC):
                            ins = nc.tensor.matmul(ps[:, 4 + t, 0:D], hid[:, f, t * P:(t + 1) * P], w2s[:, e % 2, f, :],
                                                   start=f == 0, stop=f == FC - 1)
                        ins.then_inc(s_o, 1)

                blocks(pe, chunk)


def kernel(**inputs):
    import concourse.bacc as bacc
    from concourse.bass_utils import run_bass_kernel_spmd as run

    a = {k: np.asarray(v) for k, v in inputs.items()}

    def chunked(w, n=C):
        return w.reshape(n, P, -1).transpose(1, 0, 2)

    ctx = a["ctx_1024"].transpose(0, 2, 1).reshape(B, C, P, S).transpose(0, 2, 1, 3)
    arrays = {
        "x": a["x"].reshape(TOK, D),
        "ctx_t": np.pad(ctx, ((0, 0), (0, 0), (0, 0), (0, SP - S))),
        "ctx_last": ctx[:, :, :, S - 1].transpose(1, 2, 0),
        "w_x": np.stack([chunked(a[f"L0_xattn_W{n}"].T) for n in "qkvo"], 1),
        "w_a": np.stack([chunked(a[f"L0_attn_W{n}"]) for n in "qkvo"], 1),
        "bias_cols": np.stack([a[f"L0_{m}_b{n}"].reshape(C, P).T for m in ("xattn", "attn") for n in "qkv"], 1),
        "bias_rows": np.stack([np.broadcast_to(r, (P, D)) for r in (a["L0_xattn_bo"], a["L0_attn_bo"], a["L0_ffn_gamma"], a["L0_ffn_beta"])], 1),
        "w_r": chunked(a["L0_ffn_Wr"].T),
        "b_r": np.broadcast_to(a["L0_ffn_br"], (P, E)),
        "w_1": a["L0_ffn_W1"].transpose(0, 2, 1).reshape(E, C, P, F).transpose(0, 2, 1, 3),
        "b_1": a["L0_ffn_b1"].reshape(E, FC, P).transpose(2, 0, 1),
        "w_2": a["L0_ffn_W2"].transpose(0, 2, 1).reshape(E, FC, P, D).transpose(0, 2, 1, 3),
        "b_2": a["L0_ffn_b2"],
        "consts": build_consts(),
    }
    nc = bacc.Bacc("TRN2", target_bir_lowering=False, num_devices=1)
    arrays = {f"{n}_dram": np.ascontiguousarray(v) for n, v in arrays.items()}
    args = [nc.dram_tensor(n, v.shape, F32, kind="ExternalInput").ap() for n, v in arrays.items()]
    args.append(nc.dram_tensor("out_dram", (TOK, D), F32, kind="ExternalOutput").ap())
    perceiver(nc, *args)
    return run(nc, [arrays], core_ids=[0]).results[0]["out_dram"].reshape(B, T, D)
```

```python
from contextlib import ExitStack

import numpy as np

import concourse.bass as bass
from concourse import mybir

P = 128
B, T, D, S = 64, 32, 256, 257
SP = S + 1
H, HD = 16, 16
TOK = B * T
NT = TOK // P
C = D // P
BLK = 4
NB = NT // BLK
HH = H // C
TOPK = 16
E, F = 8, 1024
FC = F // P
LN_EPS = 1e-5
SLOT = 256
NS = (2 * TOK + E * (SLOT - 1)) // SLOT
GF = 2
NG = FC // GF
WROW = FC * 2 * D + FC
LAG = 3
SPLIT = 6
TAKEN = -3.0e38

F32 = mybir.dt.float32
F32R = mybir.dt.float32r
U32 = mybir.dt.uint32
ALU = mybir.AluOpType
ACT = mybir.ActivationFunctionType
AX = mybir.AxisListType.X
ds = bass.ds

CONSTS = {}


def build_consts():
    cols = {}
    p = np.arange(P)
    cols["ident"] = np.eye(P)
    cols["delta"] = (p[:, None] % T == np.arange(T)[None, :])
    chan = np.arange(P)
    for gl in range(2):
        cols[f"pick{gl}"] = (chan[None, :] // 64 == gl) & (chan[None, :] % 64 // HD == p[:, None] // T)
    cols["parity"] = np.stack([p // HD % 2 == 0, p // HD % 2 == 1], 1)
    cols["before"] = p[:, None] < p[None, :]
    cols["ones"] = np.ones((P, P))
    cols["slot_no"] = np.tile(np.arange(NS), (P, 1))
    cols["steps"] = np.tile(SLOT * np.arange(TOK // SLOT), (P, 1))
    cols["part"] = p[:, None]
    cols["iota"] = np.tile(np.arange(E), (P, 1))
    half = HD // 2
    base = ((np.arange(0, HD, 2, dtype=np.float32) + np.float32(0.4 * HD)) / np.float32(1.4 * HD)).astype(np.float32)
    inv_freq = (1.0 / np.float32(10000.0) ** (np.arange(half, dtype=np.float32) / half)).astype(np.float32)
    for name, length, down, factor in (("k", S, True, 1.0), ("q", T, False, HD ** -0.5)):
        pos = np.arange(length, dtype=np.float32)
        scale = base[None, :] ** (pos[:, None] / np.float32(D))
        if down:
            scale = np.float32(1.0) / scale
        angle = pos[:, None] * inv_freq[None, :]
        pair = p % HD // 2
        cos = (np.cos(angle) * scale * factor)[:, pair].T
        sin = (np.sin(angle) * scale * factor)[:, pair].T * np.where(p % 2 == 0, 1.0, -1.0)[:, None]
        if length % 2:
            cos, sin = np.pad(cos, ((0, 0), (0, 1))), np.pad(sin, ((0, 0), (0, 1)))
        cols[name + "cos"], cols[name + "sin"] = cos, sin
    at = 0
    for name, a in cols.items():
        CONSTS[name] = (at, a.shape[1])
        at += a.shape[1]
    return np.ascontiguousarray(np.concatenate([np.asarray(a, np.float32) for a in cols.values()], 1))


build_consts()
NCONST = sum(n for _, n in CONSTS.values())
QX, KX, VX, QA, KA, VA = range(6)
BOX, BOA, GAMMA, BETA = range(4)


def perceiver(nc, x, ctx_t, ctx_last, w_x, w_a, bias_cols, bias_rows, w_r, b_r, w_e, b_2, consts, out):
    with ExitStack() as stack:
        def sb(name, shape, dt=F32):
            return stack.enter_context(nc.sbuf_tensor(name, shape, dt))

        def sem(name):
            return stack.enter_context(nc.semaphore(name))

        x_rows = nc.dram_tensor("x_rows", (NS * SLOT, D), F32, kind="Internal").ap()
        y_rows = nc.dram_tensor("y_rows", (NS * SLOT, D), F32, kind="Internal").ap()

        cst = sb("cst", [P, NCONST])
        wx = sb("wx", [P, 4, C, D])
        wa = sb("wa", [P, 4, C, D])
        bcol = sb("bcol", [P, 6, C])
        brow = sb("brow", [P, 4, D])
        wr = sb("wr", [P, C, E])
        br = sb("br", [P, E])
        xs = sb("xs", [P, NT, D])
        xnrm = sb("xnrm", [P, BLK, D])
        stats = sb("stats", [P, BLK, 6])
        mv = sb("mv", [P, BLK, 2])
        rstd = sb("rstd", [P, BLK])
        vareps = sb("vareps", [P, BLK])
        nhalf = sb("nhalf", [P, BLK])
        bvb = sb("bvb", [P, 2, C, P])
        ocorr = sb("ocorr", [P, 2, D])
        ps = stack.enter_context(nc.psum_tensor("ps", [P, 8, 512], F32))

        def const(name):
            at, n = CONSTS[name]
            return cst[:, at:at + n]

        ident, delta, parity = const("ident"), const("delta"), const("parity")

        s_x0 = sem("s_x0")
        s_first = sem("s_first")
        s_load = sem("s_load")
        s_set = sem("s_set")
        s_pset = sem("s_pset")
        s_corr_mm = sem("s_corr_mm")
        s_vlast_mm = sem("s_vlast_mm")
        s_st = sem("s_st")
        s_rstd = sem("s_rstd")
        s_xn = sem("s_xn")
        s_tr = sem("s_tr")
        s_xta = sem("s_xta")
        s_xtd = sem("s_xtd")
        s_zero = sem("s_zero")
        s_done = sem("s_done")

        NFIRST, NLOAD = 3, 6
        zn, total = 2 * 2 * C * HH * 2 * T, NS * SLOT * D // P
        NZERO = (total + zn - 1) // zn
        NPOS = 32

        def wait_apart(eng, semaphore, value):
            value = value if isinstance(value, int) else eng.to_reg(value)
            eng.wait_ge(s_x0, 16)
            eng.wait_ge(semaphore, value)

        def ln_stats(v, tile_of, n):
            for t in range(BLK):
                nc.vector.bn_stats(stats[:, t, :], tile_of(t)).then_inc(s_st, 1)
            wait_apart(v, s_st, 8 * n + 4)
            for t in range(BLK):
                nc.vector.bn_aggr(mv[:, t, :], stats[:, t, :]).then_inc(s_st, 1)

        def ln_apply(v, tile_of, n):
            v.wait_ge(s_rstd, 2 * n + 2)
            for t in range(BLK):
                nc.vector.tensor_scalar(xnrm[:, t, :], tile_of(t), mv[:, t, 0:1], rstd[:, t:t + 1],
                                        ALU.subtract, ALU.mult).then_inc(s_xn, 1)

        def ln_rstd(g, n):
            wait_apart(g, s_st, 8 * n + 8)
            nc.gpsimd.tensor_scalar(vareps[:], mv[:, :, 1], LN_EPS, None, ALU.add).then_inc(s_rstd, 1)
            g.wait_ge(s_rstd, 2 * n + 1)
            nc.gpsimd.tensor_tensor(rstd[:], vareps[:], nhalf[:], ALU.pow).then_inc(s_rstd, 1)

        def transpose_block(pe, n):
            for t in range(BLK):
                pe.wait_ge(s_xn, 4 * n + t + 1)
                for c in range(C):
                    ins = nc.tensor.transpose(ps[:, c, t * P:(t + 1) * P], xnrm[:, t, c * P:(c + 1) * P], ident)
                    if t == BLK - 1:
                        ins.then_inc(s_tr, 1)

        late = ExitStack()
        xT = late.enter_context(nc.sbuf_tensor("xT", [P, C, BLK * P], F32))

        a_ = ExitStack()

        def asb(name, shape, dt=F32):
            return a_.enter_context(nc.sbuf_tensor(name, shape, dt))

        ast = late.enter_context(nc.sbuf_tensor("ast", [P, C, BLK * P], F32))
        attn_t = late.enter_context(nc.sbuf_tensor("attn_t", [P, C, TOK], F32))
        wk_hl = asb("wk_hl", [P, 2, C, D], F32R)
        wv_hl = asb("wv_hl", [P, 2, C, D], F32R)
        q_hl = asb("q_hl", [P, 2, C, TOK], F32R)
        clast = asb("clast", [P, C, B])
        vlast = asb("vlast", [P, C, B])
        raw = asb("raw", [P, 2, C, SP])
        cx = asb("cx", [P, 2, 2, C, SP], F32R)
        kb = asb("kb", [P, 2, C, SP])
        kc = asb("kc", [P, 2, C, SP])
        ks = asb("ks", [P, 2, C, SP])
        kw = asb("kw", [P, 2, C, SP])
        khl = asb("khl", [P, 2, 2, C, SP], F32R)
        vv = asb("vv", [P, 4, 2, D])
        qbd = asb("qbd", [P, 2, 2, C, HH, 2 * T], F32R)
        room = asb("room", [P, 4 * 4 * SP])
        qb, qc, qs, qw = (room[:, 1024 * i:1024 * (i + 1)].rearrange("p (c t) -> p c t", c=C) for i in range(4))
        pexp = room[:].rearrange("p (s g k) -> p s g k", s=4, g=4)
        negmax = asb("negmax", [P, 4, 4])
        rsum = asb("rsum", [P, 4, 4])
        rrec = asb("rrec", [P, 2, 2, 4])
        pt = asb("pt", [P, 2, 2, 512])
        dg = asb("dg", [P, 2, 4, 2, 2, T])
        f1 = asb("f1", [P, 2, C, T])
        f2 = asb("f2", [P, 2, C, T])
        f3 = asb("f3", [P, C, 2, T])
        f4 = asb("f4", [P, C, 2, T])

        s_q = sem("s_q")
        s_qb = sem("s_qb")
        s_qd = sem("s_qd")
        ctx_in = [sem(f"ctx_in{i}") for i in range(2)]
        s_kw = sem("s_kw")
        qbd_in = [sem(f"qbd_in{i}") for i in range(2)]
        s_split = sem("s_split")
        s_K = sem("s_K")
        s_V = sem("s_V")
        s_kev = sem("s_kev")
        s_vev = sem("s_vev")
        s_kc = sem("s_kc")
        s_ks = sem("s_ks")
        s_kadd = sem("s_kadd")
        s_khl = sem("s_khl")
        s_S = sem("s_S")
        s_max = sem("s_max")
        s_exp = sem("s_exp")
        s_T = sem("s_T")
        s_pt0 = sem("s_pt0")
        s_pt1 = sem("s_pt1")
        s_pv = sem("s_pv")
        s_rec = sem("s_rec")
        s_dg = sem("s_dg")
        s_L = sem("s_L")
        s_f = sem("s_f")
        s_fin = sem("s_fin")

        J0, J1 = 1, 14

        def has(j, u, k):
            return not isinstance(j, int) or 0 <= 4 * j + u + k < B

        def cross_steps(eng, step):
            for b in range(-6, 4 * J0):
                step(b // 4, b % 4)
            with eng.Fori(J0, J1) as j:
                for u in range(4):
                    step(j, u)
            for b in range(4 * J1, B):
                step(b // 4, b % 4)

        def nth(j, m, slots, per):
            return (4 // slots * j + m // slots + 1) * per

        a_.close()

        b_ = ExitStack()

        def bsb(name, shape, dt=F32):
            return b_.enter_context(nc.sbuf_tensor(name, shape, dt))

        x2n = attn_t[:].rearrange("p c t -> p (c t)").rearrange("p (a d) -> p a d", a=NT)
        logits = bsb("logits", [P, NT, E])
        qt_all = bsb("qt_all", [P, C, TOK])
        kt_all = bsb("kt_all", [P, C, TOK])
        v_all = bsb("v_all", [P, NT, D])
        bq4 = bsb("bq4", [P, C])
        kbd = bsb("kbd", [P, 2, C, HH, P])
        qst = bsb("qst", [P, 2, C, P])
        vst = bsb("vst", [P, 2, D])
        top_a = bsb("top_a", [P, 2, H, 8])
        top_b = bsb("top_b", [P, H, 8])
        left_a = bsb("left_a", [P, H, T])
        left_b = bsb("left_b", [P, H, T])
        kept = bsb("kept", [P, 2, H, T])
        rmax = bsb("rmax", [P, 2, H])
        shifted = bsb("shifted", [P, 2, H, T])
        pr = bsb("pr", [P, 2, H, T])
        prs = bsb("prs", [P, H])
        prr = bsb("prr", [P, H])
        prn = bsb("prn", [P, H, T])
        prt = bsb("prt", [P, 2, H, T])
        g1 = bsb("g1", [P, C, 4, T])
        at2 = bsb("at2", [P, 2, C, P])
        st2 = bsb("st2", [P, 8])
        xn2 = bsb("xn2", [P, 2, D])
        xt2 = bsb("xt2", [P, 2, C, P])

        ast_in = sem("ast_in")
        s_wo = sem("s_wo")
        s_x1 = sem("s_x1")
        s_corr2 = sem("s_corr2")
        s_qk = sem("s_qk")
        s_qkev = sem("s_qkev")
        s_v2 = sem("s_v2")
        s_v2ev = sem("s_v2ev")
        s_b0 = sem("s_b0")
        kq_in = [sem(f"kq_in{i}") for i in range(2)]
        v_in = [sem(f"v_in{i}") for i in range(2)]
        s_S2 = sem("s_S2")
        s_top = sem("s_top")
        s_kept = sem("s_kept")
        s_sub = sem("s_sub")
        s_e2 = sem("s_e2")
        s_red = sem("s_red")
        s_prn = sem("s_prn")
        s_prt = sem("s_prt")
        s_pv2 = sem("s_pv2")
        s_g1 = sem("s_g1")
        s_g = sem("s_g")
        s_wo2 = sem("s_wo2")
        s_x2 = sem("s_x2")
        s_st2 = sem("s_st2")
        s_rs2 = sem("s_rs2")
        s_xn2 = sem("s_xn2")
        s_tr2 = sem("s_tr2")
        s_xt2 = sem("s_xt2")
        s_rt = sem("s_rt")
        s_lg = sem("s_lg")
        x2n_in = [sem(f"x2n_in{i}") for i in range(2)]

        M0, M1 = 2, 6

        def has2(m, u, k):
            return not isinstance(m, int) or 0 <= 2 * m + u + k < NT

        def self_steps(eng, step):
            for j in range(-3, 2 * M0):
                step(j // 2, j % 2)
            with eng.Fori(M0, M1) as m:
                for u in range(2):
                    step(m, u)
            for j in range(2 * M1, NT + 2):
                step(j // 2, j % 2)

        def nth2(m, u, k, per):
            return (m + (u + k) // 2 + 1) * per

        def blocks(eng, body):
            body(0)
            with eng.Fori(1, NB) as k:
                body(k)

        def ahead_blocks(eng, body):
            body(0)
            with eng.Fori(1, NB - 1) as k:
                body(k)
            body(NB - 1)

        def later(k):
            return not isinstance(k, int) or k > 0

        b_.close()

        c_ = ExitStack()

        def csb(name, shape, dt=F32):
            return c_.enter_context(nc.sbuf_tensor(name, shape, dt))

        logits_ = csb("logits_c", [P, NT, E])
        h32 = csb("h32", [P, 2, GF, SLOT])
        yst = csb("yst", [P, 2, 2, D])
        xraw = ast[:].rearrange("p c t -> p (c t)").rearrange("p (s a d) -> p s a d", s=2, a=2)
        yo = xT[:].rearrange("p c t -> p (c t)").rearrange("p (a d) -> p a d", a=BLK)
        wraw = csb("wraw", [P, 2, WROW])
        yg = wraw[:].rearrange("p s w -> p (s w)")[:, 0:2 * NT * D].rearrange("p (i t d) -> p i t d", i=2, t=NT)
        whl = csb("whl", [P, 2, 2, FC, 2 * D], F32R)
        xhl = csb("xhl", [P, 2, 2, C, SLOT], F32R)
        hhl = csb("hhl", [P, NG, 2, GF, SLOT], F32R)
        bst = csb("bst", [P, 2, FC])
        ist = csb("ist", [P, 2], U32)
        b2s = csb("b2s", [E, D])
        room_at = [0]

        def small(shape):
            n = int(np.prod(shape[1:]))
            view = wx[:].rearrange("p w c d -> p (w c d)")[:, room_at[0]:room_at[0] + n]
            room_at[0] += n
            assert room_at[0] <= 4 * C * D
            if len(shape) == 3:
                return view.rearrange("p (a b) -> p a b", a=shape[1])
            return view if len(shape) == 2 else view.rearrange("p (a b c) -> p a b c", a=shape[1], b=shape[2])

        rank = small([P, NT, 8])
        rix = csb("rix", [P, NT, 8], U32)
        rixf = small([P, NT, 2])
        rdiff = small([P, NT])
        rexp = small([P, NT])
        rtmp = small([P, NT])
        rwt = small([P, NT, 2])
        hot = small([P, 2, NT, E])
        rw = small([P, NT, E])
        rwT = wa[0:E].rearrange("p w c d -> p (w c d)").rearrange("p (t x) -> p t x", t=NT)
        hw = small([P, 2, NT, E])
        hsum = small([P, NT, E])
        cnt = small([P, 2, NT, E])
        over = small([P, E, TOK // SLOT])
        tl = small([P, E])
        st8 = small([P, 2, E])
        start = small([P, E])
        below = small([P, NS, E - 1])
        eix = small([P, NS])
        eixu = csb("eixu", [P, NS], U32)
        posf = small([P, 2, NT])
        posu = csb("posu", [P, 2, NT], U32)

        w_in = [sem(f"w_in{i}") for i in range(2)]
        s_ix = sem("s_ix")
        s_r = sem("s_r")
        s_rexp = sem("s_rexp")
        s_cnt = sem("s_cnt")
        s_pos = sem("s_pos")
        zero_out = sem("zero_out")
        rows_out = sem("rows_out")
        x_in = [sem(f"x_in{i}") for i in range(2)]
        y_out = [sem(f"y_out{i}") for i in range(2)]
        g_in = [sem(f"g_in{i}") for i in range(NB)]
        b2_in = sem("b2_in")
        s_ist = sem("s_ist")
        s_bst = sem("s_bst")
        s_w1hi = sem("s_w1hi")
        s_w1lo = sem("s_w1lo")
        s_w2hi = sem("s_w2hi")
        s_w2lo = sem("s_w2lo")
        s_xtr = sem("s_xtr")
        s_xhi = sem("s_xhi")
        s_xlo = sem("s_xlo")
        s_w1 = sem("s_w1")
        s_relu = sem("s_relu")
        s_hlo = sem("s_hlo")
        s_w2 = sem("s_w2")
        s_yev = sem("s_yev")
        s_rwT = sem("s_rwT")
        s_rwTs = sem("s_rwTs")
        s_acc0 = sem("s_acc0")
        s_acc1 = sem("s_acc1")
        s_comb = sem("s_comb")
        s_beta = sem("s_beta")
        s_y = sem("s_y")
        s_yy = sem("s_yy")
        s_r0 = sem("s_r0")

        S0, S1 = 1, (NS - 3) // 2

        def has3(m, u, k):
            return not isinstance(m, int) or 0 <= 2 * m + u + k < NS

        def raw_part(slot, gr, w):
            rows = wraw[:, slot, 2 * D * GF * gr:2 * D * GF * (gr + 1)].rearrange("p (f w) -> p f w", f=GF)
            return rows[:, :, w * D:(w + 1) * D]

        def split_part(slot, part, gr, w):
            return whl[:, slot, part, GF * gr:GF * (gr + 1), w * D:(w + 1) * D]

        def expert_steps(eng, step):
            for n in range(-3, 2 * S0):
                step(n // 2, n % 2)
            with eng.Fori(S0, S1) as m:
                for u in range(2):
                    step(m, u)
            for n in range(2 * S1, NS + 1):
                step(n // 2, n % 2)

        c_.close()

        stack.enter_context(late)
        block = stack.enter_context(nc.Block())

        @block.sync
        def _(sp):
            x_v = x.rearrange("(j p) c -> p j c", p=P)
            sp.dma_start(xs[:, 0:BLK], x_v[:, 0:BLK]).then_inc(s_x0, 16)
            sp.dma_start(cst[:], consts).then_inc(s_first, 16)
            sp.dma_start(wx[:], w_x).then_inc(s_first, 16)
            sp.dma_start(bcol[:], bias_cols).then_inc(s_first, 16)
            sp.dma_start(xs[:, BLK:NT], x_v[:, BLK:NT]).then_inc(s_load, 16)
            sp.dma_start(brow[:], bias_rows).then_inc(s_load, 16)
            sp.dma_start(clast[:], ctx_last).then_inc(s_load, 16)
            sp.dma_start(wa[:], w_a).then_inc(s_load, 16)
            sp.dma_start(wr[:], w_r).then_inc(s_load, 16)
            sp.dma_start(br[:], b_r).then_inc(s_load, 16)

            sp.wait_ge(s_zero, 1)
            zeros = qbd[:].rearrange("p a b c h x -> p (a b c h x)").bitcast(F32)
            rows = x_rows.rearrange("(p a) c -> p (a c)", p=P)
            for i in range(NZERO):
                n = min(zn, total - i * zn)
                sp.dma_start(rows[:, i * zn:i * zn + n], zeros[:, 0:n]).then_inc(zero_out, 16)

            def fill_queries(slot, first):
                for h in range(HH):
                    rows = slice(HD * h, HD * (h + 1))
                    sp.dma_start(qbd[rows, slot, :, :, h, :].bitcast(F32), q_hl[rows, :, :, ds(first, 2 * T)].bitcast(F32)).then_inc(qbd_in[slot], 16)

            def step(j, u):
                if has(j, u, 6):
                    m, slot = u + 6, (u + 6) % 2
                    if has(j, u, 4):
                        wait_apart(sp, s_split, 2 * (4 * j + u + 5))
                    sp.dma_start(raw[:, slot], ctx_t[ds(4 * j + m, 1)].rearrange("a p c s -> p (a c) s")).then_inc(ctx_in[slot], 16)
                if u % 2 == 1 and has(j, u, 0) and has(j, u, 4):
                    wait_apart(sp, s_S, 2 * (4 * j + u + 1))
                    fill_queries(u // 2, 128 * j + 32 * (u - 1) + 4 * T)

            for b in range(-6, -2):
                step(b // 4, b % 4)
            sp.wait_ge(s_qd, 6)
            sp.wait_ge(zero_out, 16 * NZERO)
            fill_queries(0, 0)
            fill_queries(1, 2 * T)
            for b in range(-2, 4 * J0):
                step(b // 4, b % 4)
            with sp.Fori(J0, J1) as j:
                for u in range(4):
                    step(j, u)
            for b in range(4 * J1, B):
                step(b // 4, b % 4)
            def stage(k):
                if later(k):
                    sp.wait_ge(s_fin, B // 2)
                    wait_apart(sp, s_wo, 4 * k)
                else:
                    sp.wait_ge(s_fin, B // 2 // NB)
                sp.dma_start(ast[:], attn_t[:, :, ds(512 * k, 512)]).then_inc(ast_in, 16)

            blocks(sp, stage)
            sp.wait_ge(s_v2ev, 2)
            sp.wait_ge(s_qkev, 4)
            sp.wait_ge(s_b0, 2)

            def step2(m, u):
                if has2(m, u, 3):
                    slot = (u + 3) % 2
                    if has2(m, u, 1):
                        wait_apart(sp, s_S2, 2 * m + u + 2)
                    first = 256 * m + 128 * (u + 3)
                    sp.dma_start(qst[:, slot], qt_all[:, :, ds(first, P)]).then_inc(kq_in[slot], 16)
                    for h in range(HH):
                        rows = slice(HD * h, HD * (h + 1))
                        sp.dma_start(kbd[rows, slot, :, h, :], kt_all[rows, :, ds(first, P)]).then_inc(kq_in[slot], 16)
                if has2(m, u, 1):
                    slot = (u + 1) % 2
                    if has2(m, u, -1):
                        wait_apart(sp, s_pv2, 2 * m + u)
                    sp.dma_start(vst[:, slot], v_all[:, ds(2 * m + u + 1, 1), :].rearrange("p a d -> p (a d)")).then_inc(v_in[slot], 16)
                if has2(m, u, -1):
                    slot = (u + 1) % 2
                    wait_apart(sp, s_xn2, 2 * m + u)
                    sp.dma_start(x2n[:, ds(2 * m + u - 1, 1), :].rearrange("p a d -> p (a d)"), xn2[:, slot]).then_inc(x2n_in[slot], 16)

            self_steps(sp, step2)
            sp.wait_ge(s_lg, NT)
            for i in range(2):
                sp.wait_ge(x2n_in[i], 16 * NT // 2)
            sp.dma_start(b2s[:], b_2).then_inc(b2_in, 16)
            sp.wait_ge(rows_out, 16 * 2 * NT)

            def step3(m, u):
                if has3(m, u, 3):
                    slot = (u + 1) % 2
                    if has3(m, u, 1):
                        wait_apart(sp, s_xtr, 2 * m + u + 2)
                    sp.dma_start(xraw[:, slot], x_rows[ds(SLOT * (2 * m + u + 3), SLOT), :].rearrange("(a p) d -> p a d", p=P)).then_inc(x_in[slot], 16)
                if has3(m, u, -1):
                    slot = (u + 1) % 2
                    wait_apart(sp, s_yev, 2 * m + u)
                    sp.dma_start(y_rows[ds(SLOT * (2 * m + u - 1), SLOT), :].rearrange("(a p) d -> p a d", p=P), yst[:, slot]).then_inc(y_out[slot], 16)

            expert_steps(sp, step3)
            out_v = out.rearrange("(j p) c -> p j c", p=P)

            def store(k):
                wait_apart(sp, s_y, k + 1)
                sp.dma_start(out_v[:, ds(4 * k, 4), :], yo).then_inc(s_done, 16)

            blocks(sp, store)
            sp.wait_ge(s_done, 16 * NB)

        @block.gpsimd
        def _(g):
            nc.gpsimd.memset(nhalf[:], -0.5).then_inc(s_pset, 1)
            g.wait_ge(s_pset, 1)
            ln_rstd(g, 0)
            nc.gpsimd.memset(qbd[:].bitcast(F32), 0.0).then_inc(s_zero, 1)
            with g.Fori(1, NB) as k:
                ln_rstd(g, k)

            def step(j, u):
                if has(j, u, 2):
                    m, slot = u + 2, (u + 2) % 2
                    g.wait_ge(s_kev, 2 * (4 * j + m + 1))
                    if has(j, u, 0):
                        g.wait_ge(s_kw, 4 * j + u + 1)
                    nc.gpsimd.tensor_tensor(ks[:, slot], kb[:, slot], const("ksin").unsqueeze(1).to_broadcast([P, C, SP]),
                                            ALU.mult).then_inc(s_ks, 1)
                if u % 2 == 1 and has(j, u, 0):
                    pair, slot = 2 * j + u // 2, u // 2
                    g.wait_ge(s_exp, 4 * (4 * j + u + 1))
                    g.wait_ge(s_rec, pair + 1)
                    if has(j, u, -4):
                        g.wait_ge(s_L, pair - 1)
                    dl = delta.unsqueeze(1).unsqueeze(1).to_broadcast([P, 2, 4, T])
                    nc.gpsimd.tensor_tensor(dg[:, slot, :, 0].rearrange("p g b t -> p b g t"),
                                            pexp[:, u - 1:u + 1, :, S - 1:S].to_broadcast([P, 2, 4, T]), dl, ALU.mult).then_inc(s_dg, 1)
                    nc.gpsimd.tensor_tensor(dg[:, slot, :, 1].rearrange("p g b t -> p b g t"),
                                            rrec[:, slot].unsqueeze(3).to_broadcast([P, 2, 4, T]), dl, ALU.mult).then_inc(s_dg, 1)
                if u == 0 and has(j, u, 0):
                    g.wait_ge(s_set, 8)
                    g.wait_ge(s_xn, NT)
                    nc.gpsimd.tensor_tensor(xs[:, ds(j, 1), :].rearrange("p a d -> p (a d)"), xs[:, ds(j, 1), :].rearrange("p a d -> p (a d)"),
                                            ocorr[:, 0, :], ALU.add).then_inc(s_pset, 1)
                if has(j, u, 4):
                    m, slot = u + 4, (u + 4) % 2
                    wait_apart(g, ctx_in[slot], nth(j, m, 2, 16))
                    if has(j, u, 2):
                        g.wait_ge(s_V, 4 * j + u + 3)
                    nc.gpsimd.tensor_scalar(cx[:, slot, 0], raw[:, slot], 1.0, None, ALU.mult).then_inc(s_split, 1)
                    g.wait_ge(s_split, 2 * (4 * j + m) + 1)
                    nc.gpsimd.tensor_tensor(cx[:, slot, 1], raw[:, slot], cx[:, slot, 0].bitcast(F32), ALU.subtract).then_inc(s_split, 1)

            cross_steps(g, step)
            g.wait_ge(s_fin, B // 2)
            nc.gpsimd.memset(kbd[:], 0.0).then_inc(s_b0, 1)

            def block2(k):
                ln_rstd(g, k + NB)
                wait_apart(g, s_xn, 4 * (k + NB) + 4)
                rows = xs[:, ds(4 * k, 4), :]
                nc.gpsimd.tensor_tensor(rows, rows, ocorr[:, 1, :].unsqueeze(1).to_broadcast([P, BLK, D]), ALU.add).then_inc(s_corr2, 1)

            blocks(g, block2)

            def step2(m, u):
                if has2(m, u, 0):
                    n = 2 * m + u
                    g.wait_ge(s_red, 2 * n + 2)
                    if has2(m, u, -1):
                        g.wait_ge(s_prt, n)
                    nc.gpsimd.tensor_tensor(prn[:], pr[:, u], prr[:].unsqueeze(2).to_broadcast([P, H, T]), ALU.mult).then_inc(s_prn, 1)
                if has2(m, u, -1):
                    n = 2 * m + u - 1
                    wait_apart(g, s_st2, 2 * n + 2)
                    nc.gpsimd.tensor_scalar(st2[:, 2:3], st2[:, 1:2], LN_EPS, None, ALU.add).then_inc(s_rs2, 1)
                    g.wait_ge(s_rs2, 2 * n + 1)
                    nc.gpsimd.tensor_tensor(rstd[:, 0:1], st2[:, 2:3], nhalf[:, 0:1], ALU.pow).then_inc(s_rs2, 1)
                if has2(m, u, 1):
                    n, slot = 2 * m + u + 1, (u + 1) % 2
                    g.wait_ge(s_kept, 2 * n + 2)
                    if has2(m, u, -1):
                        g.wait_ge(s_e2, n - 1)
                    nc.gpsimd.tensor_tensor(shifted[:, slot], kept[:, slot], rmax[:, slot].unsqueeze(2).to_broadcast([P, H, T]),
                                            ALU.subtract).then_inc(s_sub, 1)

            self_steps(g, step2)
            g.wait_ge(s_pos, NPOS)
            g.wait_ge(zero_out, 16 * NZERO)
            for i in range(2):
                g.wait_ge(x2n_in[i], 16 * NT // 2)

            def scatter(n):
                if n < -1:
                    for t in range((n + 3) * NT // 2, (n + 4) * NT // 2):
                        for i in range(2):
                            nc.gpsimd.indirect_dma_start(x_rows, bass.IndirectOffsetOnAxis(posu[:, i, t:t + 1], 0), x2n[:, t, :], None).then_inc(rows_out, 16)

            def step3(m, u):
                n = 2 * m + u
                for q in range(NG):
                    if q == 2 and has3(m, u, 3):
                        slot = (u + 1) % 2
                        if has3(m, u, 1):
                            wait_apart(g, s_w1lo, NG * (n + 2))
                            g.wait_ge(s_w2lo, NG * (n + 2))
                        wait_apart(g, s_ist, n + 4)
                        nc.gpsimd.indirect_dma_start(wraw[:, slot], None, w_e, bass.IndirectOffsetOnAxis(ist[:, slot:slot + 1], 0)).then_inc(w_in[slot], 16)
                        if isinstance(m, int):
                            scatter(n)
                    k, gr = (q + SPLIT) // NG, (q + SPLIT) % NG
                    if has3(m, u, k):
                        slot = (u + k) % 2
                        g.wait_ge(s_w1hi, NG * (n + k) + gr + 1)
                        nc.gpsimd.tensor_tensor(split_part(slot, 1, gr, 0), raw_part(slot, gr, 0), split_part(slot, 0, gr, 0).bitcast(F32),
                                                ALU.subtract).then_inc(s_w1lo, 1)

            expert_steps(g, step3)
            g.wait_ge(y_out[0], 16 * ((NS + 1) // 2))
            g.wait_ge(y_out[1], 16 * (NS // 2))
            for k in range(NB + 1):
                if k < NB:
                    for t in range(BLK * k, BLK * (k + 1)):
                        for i in range(2):
                            nc.gpsimd.indirect_dma_start(yg[:, i, t, :], None, y_rows, bass.IndirectOffsetOnAxis(posu[:, i, t:t + 1], 0)).then_inc(g_in[k], 16)
                if k:
                    ln_rstd(g, 2 * NB + k - 1)

        @block.scalar
        def _(act):
            act.wait_ge(s_first, 16 * NFIRST)

            def query_block(k):
                for c, done in enumerate((s_xta, s_xtd)):
                    act.wait_ge(s_tr, 2 * k + c + 1)
                    nc.scalar.copy(xT[:, c, :], ps[:, c, :]).then_inc(done, 1)
                for hf in range(C):
                    act.wait_ge(s_q, 2 * k + hf + 1)
                    if later(k):
                        act.wait_ge(s_qd, 6 * k)
                    nc.scalar.activation(qb[:, hf, :], ps[:, 2 + hf, :], ACT.Identity, bias=bcol[:, QX, hf:hf + 1]).then_inc(s_qb, 1)

            blocks(act, query_block)

            def step(j, u):
                if has(j, u, 0):
                    act.wait_ge(s_T, 2 * (4 * j + u) + 1)
                    if has(j, u, -2):
                        act.wait_ge(s_pv, 4 * j + u - 1)
                    nc.scalar.copy(pt[:, u % 2, 0], ps[:, 0, :]).then_inc(s_pt0, 1)
                if has(j, u, 1):
                    m, slot = u + 1, (u + 1) % 4
                    if has(j, u, -3):
                        act.wait_ge(s_T, 2 * (4 * j + u - 2))
                        act.wait_ge(s_dg, 2 * (2 * j + (u - 3) // 2 + 1))
                    for g in range(4):
                        if g % 2 == 0:
                            act.wait_ge(s_max, 2 * (4 * j + m) + g // 2 + 1)
                        nc.scalar.activation(pexp[:, slot, g, 0:S], ps[:, 3 + g, 0:S], ACT.Exp, bias=negmax[:, slot, g:g + 1],
                                             accum_out=rsum[:, slot, g:g + 1]).then_inc(s_exp, 1)
                if has(j, u, 3):
                    m, slot = u + 3, (u + 3) % 2
                    if has(j, u, 1):
                        act.wait_ge(s_kc, 4 * j + u + 2)
                        act.wait_ge(s_ks, 4 * j + u + 2)
                    for hf in range(C):
                        act.wait_ge(s_K, 2 * (4 * j + m) + hf + 1)
                        nc.scalar.activation(kb[:, slot, hf, :], ps[:, hf, 0:SP], ACT.Identity, bias=bcol[:, KX, hf:hf + 1]).then_inc(s_kev, 1)
                    act.wait_ge(s_V, 4 * j + m + 1)
                    if has(j, u, -1):
                        act.wait_ge(s_pv, 4 * j + u)
                    nc.scalar.copy(vv[:, m % 4].rearrange("p c d -> p (c d)"), ps[:, 2, :]).then_inc(s_vev, 1)

            cross_steps(act, step)
            act.wait_ge(s_b0, 2)

            def block2(k):
                n = k + NB
                act.wait_ge(s_tr, 2 * n + 1)
                nc.scalar.copy(xT[:, 0, :], ps[:, 0, :]).then_inc(s_xta, 1)
                for i, (dst, bias, scale, hf) in enumerate(((qt_all, bq4, HD ** -0.5, 0), (qt_all, bq4, HD ** -0.5, 1),
                                                            (kt_all, bcol[:, KA], 1.0, 0), (kt_all, bcol[:, KA], 1.0, 1))):
                    act.wait_ge(s_qk, 4 * k + i + 1)
                    nc.scalar.activation(dst[:, hf, ds(512 * k, 512)], ps[:, (2, 3, 6, 7)[i], :], ACT.Identity, bias=bias[:, hf:hf + 1],
                                         scale=scale).then_inc(s_qkev, 1)

            blocks(act, block2)

            def step2(m, u):
                if has2(m, u, -1):
                    n = 2 * m + u - 1
                    act.wait_ge(s_pv2, n + 1)
                    if has2(m, u, -2):
                        act.wait_ge(s_g, 2 * n)
                    for hf in range(C):
                        nc.scalar.activation(g1[:, hf], ps[:, 2:6, hf * 64:hf * 64 + T], ACT.Copy, scale=parity[:, 0:1]).then_inc(s_g1, 1)
                    act.wait_ge(s_tr2, n + 1)
                    if has2(m, u, -3):
                        act.wait_ge(s_rt, n - 1)
                    src = ps[:, 7, 0:D].rearrange("p (c t) -> p c t", c=C)
                    nc.scalar.copy(xt2[:, (u + 1) % 2], src).then_inc(s_xt2, 1)
                if has2(m, u, 1):
                    n, slot = 2 * m + u + 1, (u + 1) % 2
                    act.wait_ge(s_sub, n + 1)
                    if has2(m, u, -1):
                        act.wait_ge(s_prn, n - 1)
                    nc.scalar.activation(pr[:, slot], shifted[:, slot], ACT.Exp).then_inc(s_e2, 1)

            self_steps(act, step2)
            act.wait_ge(s_r, 1)
            nc.scalar.activation(rexp, rdiff, ACT.Exp).then_inc(s_rexp, 1)

            def step3(m, u):
                n = 2 * m + u
                for q in range(NG):
                    k, gr = (q + SPLIT) // NG, (q + SPLIT) % NG
                    if has3(m, u, k):
                        slot = (u + k) % 2
                        if gr == 0:
                            act.wait_ge(w_in[slot], nth2(m, u, k, 16))
                        if has3(m, u, k - 2):
                            act.wait_ge(s_w1, NG * (n + k - 2) + gr + 1)
                        nc.scalar.copy(split_part(slot, 0, gr, 0), raw_part(slot, gr, 0)).then_inc(s_w1hi, 1)
                    k, gr = (q + LAG) // NG, (q + LAG) % NG
                    if has3(m, u, k):
                        slot, at = (u + k) % 2, NG * (n + k) + gr
                        act.wait_ge(s_w1, at + 1)
                        if gr == 0:
                            act.wait_ge(s_bst, n + k + 1)
                        if gr >= 2 or has3(m, u, k - 1):
                            act.wait_ge(s_hlo, at - 1)
                        if has3(m, u, k - 1):
                            act.wait_ge(s_w2, at - 3)
                        for f in range(GF):
                            src, bias = ps[:, gr % 2, f * SLOT:(f + 1) * SLOT], bst[:, slot, GF * gr + f:GF * gr + f + 1]
                            nc.scalar.activation(hhl[:, gr, 0, f], src, ACT.Relu, bias=bias)
                            nc.scalar.activation(h32[:, gr % 2, f], src, ACT.Relu, bias=bias).then_inc(s_relu, 1)
                    if q == 1 and has3(m, u, -1):
                        slot = (u + 1) % 2
                        act.wait_ge(s_w2, NG * n)
                        if has3(m, u, -3):
                            act.wait_ge(y_out[slot], nth2(m, u, -3, 16))
                        nc.scalar.copy(yst[:, slot], ps[:, 4 + 2 * slot:6 + 2 * slot, 0:D]).then_inc(s_yev, 1)
                    if q == 2 and has3(m, u, 2):
                        act.wait_ge(s_xtr, n + 3)
                        if has3(m, u, 0):
                            act.wait_ge(s_w1, NG * (n + 1))
                        nc.scalar.copy(xhl[:, u, 0].rearrange("p c t -> p (c t)"), ps[:, 2, :]).then_inc(s_xhi, 1)

            expert_steps(act, step3)

        @block.vector
        def _(v):
            def tile_at(k):
                return lambda t: xs[:, ds(4 * k + t, 1), :].rearrange("p a d -> p (a d)")

            v.wait_ge(s_x0, 16)
            ln_stats(v, tile_at(0), 0)
            ln_apply(v, tile_at(0), 0)

            def query_block(k):
                v.wait_ge(s_tr, 2 * k + 2)
                if isinstance(k, int) and k == 0:
                    v.wait_ge(s_first, 16 * NFIRST)
                    for w, src in ((wk_hl, wx[:, 1]), (wv_hl, wx[:, 2])):
                        nc.vector.tensor_copy(w[:, 0], src).then_inc(s_set, 1)
                    v.wait_ge(s_set, 2)
                    for w, src in ((wk_hl, wx[:, 1]), (wv_hl, wx[:, 2])):
                        nc.vector.tensor_tensor(w[:, 1], src, w[:, 0].bitcast(F32), ALU.subtract).then_inc(s_set, 1)
                    for i, col in enumerate((VX, VA)):
                        nc.vector.tensor_copy(bvb[:, i], bcol[:, col, :].unsqueeze(2).to_broadcast([P, C, P])).then_inc(s_set, 1)
                    v.wait_ge(s_load, 16 * NLOAD)
                if not isinstance(k, int) or k < NB - 1:
                    ln_stats(v, tile_at(k + 1), k + 1)
                    ln_apply(v, tile_at(k + 1), k + 1)
                v.wait_ge(s_qb, 2 * k + 2)
                by_pos = lambda a: a.rearrange("p c (b t) -> p (c b) t", t=T)
                by_pair = lambda a: a.rearrange("p c (i b t) -> p (c i) b t", b=2, t=T)
                by_latent = lambda a: a.rearrange("p c (i t b) -> p (c i) b t", b=2, t=T)
                for dst, tab in ((qc, "qcos"), (qs, "qsin")):
                    nc.vector.tensor_tensor(by_pos(dst), by_pos(qb), const(tab).unsqueeze(1).to_broadcast([P, C * BLK * 4, T]),
                                            ALU.mult).then_inc(s_qd, 1)
                wait_apart(v, s_qd, 6 * k + 2)
                nc.vector.stream_shuffle(qw, qs, [i ^ 1 for i in range(32)]).then_inc(s_qd, 1)
                v.wait_ge(s_qd, 6 * k + 3)
                nc.vector.tensor_tensor(by_latent(qb), by_pair(qc), by_pair(qw), ALU.add).then_inc(s_qd, 1)
                v.wait_ge(s_qd, 6 * k + 4)
                nc.vector.tensor_copy(q_hl[:, 0, :, ds(512 * k, 512)], qb).then_inc(s_qd, 1)
                v.wait_ge(s_qd, 6 * k + 5)
                nc.vector.tensor_tensor(q_hl[:, 1, :, ds(512 * k, 512)], qb, q_hl[:, 0, :, ds(512 * k, 512)].bitcast(F32),
                                        ALU.subtract).then_inc(s_qd, 1)

            ahead_blocks(v, query_block)
            v.wait_ge(s_corr_mm, 1)
            for i, row in enumerate((BOX, BOA)):
                nc.vector.tensor_tensor(ocorr[:, i, :], ps[:, 4, i * D:(i + 1) * D], brow[:, row, :], ALU.add).then_inc(s_set, 1)
            v.wait_ge(s_vlast_mm, 1)
            nc.vector.tensor_copy(vlast[:], ps[:, 5, 0:C * B].rearrange("p (c b) -> p c b", c=C)).then_inc(s_set, 1)

            def step(j, u):
                if u % 2 == 1 and has(j, u, 0):
                    pair, slot = 2 * j + u // 2, u // 2
                    v.wait_ge(s_exp, 4 * (4 * j + u + 1))
                    if has(j, u, -4):
                        v.wait_ge(s_dg, 2 * (pair - 1))
                    nc.vector.reciprocal(rrec[:, slot], rsum[:, u - 1:u + 1]).then_inc(s_rec, 1)
                if has(j, u, 0):
                    v.wait_ge(s_T, 2 * (4 * j + u) + 2)
                    if has(j, u, -2):
                        v.wait_ge(s_pv, 4 * j + u - 1)
                    nc.vector.tensor_copy(pt[:, u % 2, 1], ps[:, 1, :]).then_inc(s_pt1, 1)
                if has(j, u, 1):
                    m, slot = u + 1, (u + 1) % 4
                    if has(j, u, -3):
                        v.wait_ge(s_exp, 4 * (4 * j + u - 2))
                    for hf in range(C):
                        v.wait_ge(s_S, 2 * (4 * j + m) + hf + 1)
                        nc.vector.tensor_reduce(negmax[:, slot, 2 * hf:2 * hf + 2], ps[:, 3 + 2 * hf:5 + 2 * hf, 0:S], axis=AX,
                                                op=ALU.max, negate=True).then_inc(s_max, 1)
                if has(j, u, 2):
                    m, slot = u + 2, (u + 2) % 2
                    n = 4 * j + m
                    v.wait_ge(s_kev, 2 * (n + 1))
                    nc.vector.tensor_tensor(kc[:, slot], kb[:, slot], const("kcos").unsqueeze(1).to_broadcast([P, C, SP]),
                                            ALU.mult).then_inc(s_kc, 1)
                    if has(j, u, 0):
                        wait_apart(v, s_khl, 2 * (4 * j + u + 1))
                    wait_apart(v, s_ks, n + 1)
                    nc.vector.stream_shuffle(kw[:, slot], ks[:, slot], [i ^ 1 for i in range(32)]).then_inc(s_kw, 1)
                    v.wait_ge(s_kw, n + 1)
                    v.wait_ge(s_kc, n + 1)
                    nc.vector.tensor_tensor(kw[:, slot], kc[:, slot], kw[:, slot], ALU.add).then_inc(s_kadd, 1)
                    v.wait_ge(s_kadd, n + 1)
                    if has(j, u, 0):
                        v.wait_ge(s_S, 2 * (4 * j + u + 1))
                    nc.vector.tensor_copy(khl[:, slot, 0], kw[:, slot]).then_inc(s_khl, 1)
                    v.wait_ge(s_khl, 2 * n + 1)
                    nc.vector.tensor_tensor(khl[:, slot, 1], kw[:, slot], khl[:, slot, 0].bitcast(F32), ALU.subtract).then_inc(s_khl, 1)
                if u % 2 == 1 and has(j, u, 0):
                    pair = 2 * j + u // 2
                    both = ps[:, 7, 0:256].rearrange("p (b c r t) -> p b c r t", b=2, c=C, r=2)
                    sel = ps[:, 7, 256:512].rearrange("p (c w b t) -> p c w b t", c=C, w=2, b=2)
                    v.wait_ge(s_L, pair + 1)
                    nc.vector.tensor_scalar(f1[:].rearrange("p b c t -> p (b c) t"), both[:, :, :, 0, :].rearrange("p b c t -> p (b c) t"),
                                            parity[:, 0:1], None, ALU.mult).then_inc(s_f, 1)
                    nc.vector.tensor_tensor(f3[:], sel[:, :, 0], vlast[:, :, ds(4 * j + u - 1, 2)].unsqueeze(3).to_broadcast([P, C, 2, T]),
                                            ALU.mult).then_inc(s_f, 1)
                    v.wait_ge(s_f, 4 * pair + 1)
                    nc.vector.scalar_tensor_tensor(f2[:].rearrange("p b c t -> p (b c) t"), both[:, :, :, 1, :].rearrange("p b c t -> p (b c) t"),
                                                   parity[:, 1:2], f1[:].rearrange("p b c t -> p (b c) t"), ALU.mult, ALU.add).then_inc(s_f, 1)
                    v.wait_ge(s_f, 4 * pair + 3)
                    nc.vector.tensor_tensor(f4[:], f3[:], f2[:].rearrange("p b c t -> p c b t"), ALU.add).then_inc(s_f, 1)
                    v.wait_ge(s_f, 4 * pair + 4)
                    nc.vector.tensor_tensor(attn_t[:, :, ds(128 * j + 32 * (u - 1), 2 * T)].rearrange("p c (b t) -> p c b t", t=T), f4[:],
                                            sel[:, :, 1], ALU.mult).then_inc(s_fin, 1)

            cross_steps(v, step)
            v.wait_ge(s_pv, B)
            nc.vector.tensor_scalar(bq4[:], bcol[:, QA, :], HD ** -0.5, None, ALU.mult).then_inc(s_b0, 1)

            v.wait_ge(s_pset, 1 + NT)

            def add_and_norm(k):
                for t in range(BLK):
                    v.wait_ge(s_wo, 4 * k + t // 2 * 2 + 2)
                    nc.vector.tensor_tensor(tile_at(k)(t), ps[:, 4 + t // 2, t % 2 * D:(t % 2 + 1) * D], tile_at(k)(t), ALU.add).then_inc(s_x1, 1)
                wait_apart(v, s_x1, 4 * k + 4)
                ln_stats(v, tile_at(k), k + NB)
                ln_apply(v, tile_at(k), k + NB)

            add_and_norm(0)

            def block2(k):
                v.wait_ge(s_tr, 2 * (k + NB) + 2)
                nc.vector.tensor_copy(xT[:, 1, :], ps[:, 1, :]).then_inc(s_xtd, 1)
                if not isinstance(k, int) or k < NB - 1:
                    add_and_norm(k + 1)
                for i in range(2):
                    v.wait_ge(s_v2, 2 * k + i + 1)
                    nc.vector.tensor_copy(v_all[:, ds(4 * k + 2 * i, 2), :].rearrange("p a d -> p (a d)"), ps[:, 4 + i, :]).then_inc(s_v2ev, 1)

            ahead_blocks(v, block2)

            def step2(m, u):
                slot, nslot = u, (u + 1) % 2
                n = 2 * m + u
                scores = ps[:, nslot, :].rearrange("p (h k) -> p h k", h=H)

                def rank_pass(i):
                    if not has2(m, u, 1):
                        return
                    if i == 0:
                        wait_apart(v, s_S2, n + 2)
                    else:
                        wait_apart(v, s_top, 64 * (n + 1) + 16 * i)
                    for h in range(H):
                        if i == 0:
                            ins = nc.vector.max(top_a[:, nslot, h, :], scores[:, h, :])
                        elif i == 1:
                            ins = nc.vector.match_replace(left_a[:, h, :], top_a[:, nslot, h, :], scores[:, h, :], TAKEN)
                        elif i == 2:
                            ins = nc.vector.max(top_b[:, h, :], left_a[:, h, :])
                        else:
                            ins = nc.vector.match_replace(left_b[:, h, :], top_b[:, h, :], left_a[:, h, :], TAKEN)
                        ins.then_inc(s_top, 1)

                rank_pass(0)
                if has2(m, u, -2):
                    v.wait_ge(s_rt, n - 1)
                    nc.vector.tensor_tensor(logits[:, ds(n - 2, 1), :].rearrange("p a e -> p (a e)"), ps[:, 6, D:D + E], br[:], ALU.add).then_inc(s_lg, 1)
                if has2(m, u, -1):
                    if has2(m, u, -3):
                        v.wait_ge(s_wo2, n - 2)
                    v.wait_ge(s_g1, 2 * n)
                    for hf in range(C):
                        nc.vector.scalar_tensor_tensor(at2[:, nslot, hf].rearrange("p (b t) -> p b t", t=T),
                                                       ps[:, 2:6, hf * 64 + T:hf * 64 + 2 * T], parity[:, 1:2], g1[:, hf],
                                                       ALU.mult, ALU.add).then_inc(s_g, 1)
                if has2(m, u, 0):
                    wait_apart(v, s_e2, n + 1)
                    nc.vector.tensor_reduce(prs[:], pr[:, slot], axis=AX, op=ALU.add).then_inc(s_red, 1)
                    v.wait_ge(s_red, 2 * n + 1)
                    nc.vector.reciprocal(prr[:], prs[:]).then_inc(s_red, 1)
                rank_pass(1)
                if has2(m, u, 0):
                    if has2(m, u, -2):
                        v.wait_ge(s_pv2, n - 1)
                    v.wait_ge(s_prn, n + 1)
                    nc.vector.transpose(prt[:, slot].rearrange("p h k -> p (h k)"), prn[:].rearrange("p h k -> p (h k)")).then_inc(s_prt, 1)
                if has2(m, u, -1):
                    row = xs[:, ds(n - 1, 1), :].rearrange("p a d -> p (a d)")
                    v.wait_ge(s_wo2, n)
                    nc.vector.tensor_tensor(row, ps[:, 6, 0:D], row, ALU.add).then_inc(s_x2, 1)
                    wait_apart(v, s_x2, n)
                    nc.vector.bn_stats(stats[:, 0, :], row).then_inc(s_st2, 1)
                    wait_apart(v, s_st2, 2 * n - 1)
                    nc.vector.bn_aggr(st2[:, 0:2], stats[:, 0, :]).then_inc(s_st2, 1)
                rank_pass(2)
                if has2(m, u, -1):
                    v.wait_ge(s_rs2, 2 * n)
                    if has2(m, u, -3):
                        v.wait_ge(x2n_in[nslot], nth2(m, u, -3, 16))
                        v.wait_ge(s_tr2, n - 2)
                    nc.vector.tensor_scalar(xn2[:, nslot], row, st2[:, 0:1], rstd[:, 0:1], ALU.subtract, ALU.mult).then_inc(s_xn2, 1)
                rank_pass(3)
                if has2(m, u, 1):
                    if has2(m, u, -1):
                        v.wait_ge(s_sub, n)
                    wait_apart(v, s_top, 64 * (n + 2))
                    nc.vector.scalar_tensor_tensor(kept[:, nslot], left_b[:], 0.1 * TAKEN, scores, ALU.is_lt, ALU.mult).then_inc(s_kept, 1)
                    nc.vector.tensor_scalar(rmax[:, nslot], top_a[:, nslot, :, 0], 0.0, None, ALU.max).then_inc(s_kept, 1)

            self_steps(v, step2)

            v.wait_ge(s_lg, NT)
            for t in range(NT):
                nc.vector.max(rank[:, t, :], logits[:, t, :]).then_inc(s_r0, 1)
            v.wait_ge(s_r0, NT)
            for t in range(NT):
                nc.vector.max_index(rix[:, t, :], rank[:, t, :], logits[:, t, :]).then_inc(s_r0, 1)
            nc.vector.tensor_tensor(rdiff, rank[:, :, 1], rank[:, :, 0], ALU.subtract).then_inc(s_r, 1)
            v.wait_ge(s_r0, 2 * NT)
            nc.vector.tensor_copy(rixf, rix[:, :, 0:2]).then_inc(s_r, 1)
            v.wait_ge(s_rexp, 1)
            nc.vector.tensor_scalar(rtmp, rexp, 1.0, None, ALU.add).then_inc(s_r, 1)
            v.wait_ge(s_r, 3)
            nc.vector.reciprocal(rwt[:, :, 0], rtmp).then_inc(s_r, 1)
            v.wait_ge(s_r, 4)
            nc.vector.tensor_tensor(rwt[:, :, 1], rwt[:, :, 0], rexp, ALU.mult).then_inc(s_r, 1)
            for i in range(2):
                nc.vector.tensor_tensor(hot[:, i], const("iota").unsqueeze(1).to_broadcast([P, NT, E]),
                                        rixf[:, :, i:i + 1].to_broadcast([P, NT, E]), ALU.is_equal).then_inc(s_r, 1)
            v.wait_ge(s_r, 7)
            for i in range(2):
                nc.vector.tensor_tensor(hw[:, i], hot[:, i], rwt[:, :, i:i + 1].to_broadcast([P, NT, E]), ALU.mult).then_inc(s_r, 1)
            nc.vector.tensor_tensor(hsum, hot[:, 0], hot[:, 1], ALU.add).then_inc(s_r, 1)
            v.wait_ge(s_r, 9)
            nc.vector.tensor_tensor(rw, hw[:, 0], hw[:, 1], ALU.add).then_inc(s_r, 1)

            done = [0]

            def pos(ins):
                ins.then_inc(s_pos, 1)
                done[0] += 1
                v.wait_ge(s_pos, done[0])

            within = ps[:, 3, 0:NT * E].rearrange("p (t e) -> p t e", e=E)
            totals = ps[:, 3, NT * E:2 * NT * E].rearrange("p (t e) -> p t e", e=E)
            v.wait_ge(s_cnt, 1)
            pos(nc.vector.tensor_copy(cnt[:, 0], totals))
            for i in range(4):
                d, a, b = 1 << i, i % 2, (i + 1) % 2
                pos(nc.vector.tensor_copy(cnt[:, b, 0:d], cnt[:, a, 0:d]))
                pos(nc.vector.tensor_tensor(cnt[:, b, d:NT], cnt[:, a, d:NT], cnt[:, a, 0:NT - d], ALU.add))
            pos(nc.vector.tensor_tensor(over, cnt[:, 0, NT - 1:NT, :].rearrange("p a e -> p e a").to_broadcast([P, E, TOK // SLOT]),
                                        const("steps").unsqueeze(1).to_broadcast([P, E, TOK // SLOT]), ALU.is_gt))
            pos(nc.vector.tensor_reduce(tl, over, axis=AX, op=ALU.add))
            pos(nc.vector.tensor_copy(st8[:, 0], tl))
            for i in range(3):
                d, a, b = 1 << i, i % 2, (i + 1) % 2
                pos(nc.vector.tensor_copy(st8[:, b, 0:d], st8[:, a, 0:d]))
                pos(nc.vector.tensor_tensor(st8[:, b, d:E], st8[:, a, d:E], st8[:, a, 0:E - d], ALU.add))
            pos(nc.vector.tensor_tensor(start, st8[:, 1], tl, ALU.subtract))
            pos(nc.vector.tensor_tensor(below, start[:, 1:E].unsqueeze(1).to_broadcast([P, NS, E - 1]),
                                        const("slot_no").unsqueeze(2).to_broadcast([P, NS, E - 1]), ALU.is_le))
            pos(nc.vector.tensor_reduce(eix, below, axis=AX, op=ALU.add))
            pos(nc.vector.tensor_scalar(eix, eix, float(P), const("part"), ALU.mult, ALU.add))
            pos(nc.vector.tensor_copy(eixu[:], eix))
            pos(nc.vector.tensor_tensor(cnt[:, 1], cnt[:, 0], totals, ALU.subtract))
            pos(nc.vector.tensor_tensor(cnt[:, 0], cnt[:, 1], within, ALU.add))
            pos(nc.vector.tensor_scalar(st8[:, 0], start, float(SLOT), None, ALU.mult))
            pos(nc.vector.tensor_tensor(cnt[:, 1], cnt[:, 0], st8[:, 0:1].to_broadcast([P, NT, E]), ALU.add))
            for i in range(2):
                pos(nc.vector.tensor_tensor(hot[:, i], hot[:, i], cnt[:, 1], ALU.mult))
                pos(nc.vector.tensor_reduce(posf[:, i], hot[:, i], axis=AX, op=ALU.add))
            pos(nc.vector.tensor_copy(posu[:], posf))
            assert done[0] == NPOS

            def step3(m, u):
                n = 2 * m + u
                for q in range(NG):
                    if q == 2 and has3(m, u, 3):
                        slot = (u + 1) % 2
                        if has3(m, u, 1):
                            v.wait_ge(w_in[slot], nth2(m, u, 1, 16))
                        nc.vector.tensor_copy(ist[:, slot:slot + 1], eixu[:, ds(n + 3, 1)]).then_inc(s_ist, 1)
                    k, gr = (q + SPLIT) // NG, (q + SPLIT) % NG
                    if has3(m, u, k):
                        slot, at = (u + k) % 2, NG * (n + k) + gr
                        if gr == 0:
                            v.wait_ge(w_in[slot], nth2(m, u, k, 16))
                            if has3(m, u, k - 2):
                                v.wait_ge(s_relu, FC * (n + k - 1))
                            nc.vector.tensor_copy(bst[:, slot], wraw[:, slot, 2 * D * FC:]).then_inc(s_bst, 1)
                        if has3(m, u, k - 2):
                            v.wait_ge(s_w2, at - 2 * NG + 1)
                        nc.vector.tensor_copy(split_part(slot, 0, gr, 1), raw_part(slot, gr, 1)).then_inc(s_w2hi, 1)
                        v.wait_ge(s_w2hi, at + 1)
                        nc.vector.tensor_tensor(split_part(slot, 1, gr, 1), raw_part(slot, gr, 1), split_part(slot, 0, gr, 1).bitcast(F32),
                                                ALU.subtract).then_inc(s_w2lo, 1)
                    k, gr = (q + LAG) // NG, (q + LAG) % NG
                    if has3(m, u, k):
                        v.wait_ge(s_relu, FC * (n + k) + GF * (gr + 1))
                        nc.vector.tensor_tensor(hhl[:, gr, 1], h32[:, gr % 2], hhl[:, gr, 0].bitcast(F32), ALU.subtract).then_inc(s_hlo, 1)
                    if q == 2 and has3(m, u, 2):
                        v.wait_ge(s_xhi, n + 3)
                        nc.vector.tensor_tensor(xhl[:, u, 1].rearrange("p c t -> p (c t)"), ps[:, 2, :],
                                                xhl[:, u, 0].rearrange("p c t -> p (c t)").bitcast(F32), ALU.subtract).then_inc(s_xlo, 1)

            expert_steps(v, step3)
            for q in range(NB):
                v.wait_ge(s_rwT, q + 1)
                nc.vector.tensor_copy(rwT[:, 4 * q:4 * q + 4, :].rearrange("e a p -> e (a p)"), ps[0:E, q, :]).then_inc(s_rwTs, 1)
            v.wait_ge(rows_out, 32 * NT)
            for q in range(NT // 2):
                v.wait_ge(s_acc0, q + 1)
                pair = x2n[:, 2 * q:2 * q + 2, :].rearrange("p a d -> p (a d)")
                nc.vector.tensor_tensor(pair, ps[:, 4 + q % 4, :], pair, ALU.add).then_inc(s_acc1, 1)
            nc.vector.tensor_tensor(xs[:], xs[:], brow[:, BETA, :].unsqueeze(1).to_broadcast([P, NT, D]), ALU.add).then_inc(s_beta, 1)
            v.wait_ge(s_beta, 1)
            for k in range(NB):
                tile_of = lambda t: x2n[:, 4 * k + t, :]
                v.wait_ge(s_acc1, 2 * k + 2)
                v.wait_ge(g_in[k], 16 * 2 * BLK)
                for i in range(2):
                    for t in range(BLK):
                        if i:
                            v.wait_ge(s_comb, 2 * BLK * k + t + 1)
                        nc.vector.scalar_tensor_tensor(tile_of(t), yg[:, i, 4 * k + t, :], rwt[:, 4 * k + t, i:i + 1], tile_of(t),
                                                       ALU.mult, ALU.add).then_inc(s_comb, 1)
                v.wait_ge(s_comb, 2 * BLK * (k + 1))
                ln_stats(v, tile_of, 2 * NB + k)
                ln_apply(v, tile_of, 2 * NB + k)
                v.wait_ge(s_xn, 4 * (2 * NB + k) + 4)
                nc.vector.tensor_tensor(xnrm[:], xnrm[:], brow[:, GAMMA, :].unsqueeze(1).to_broadcast([P, BLK, D]), ALU.mult).then_inc(s_yy, 1)
                v.wait_ge(s_yy, k + 1)
                if k:
                    v.wait_ge(s_done, 16 * k)
                nc.vector.tensor_tensor(yo, xnrm[:], xs[:, 4 * k:4 * k + 4, :], ALU.add).then_inc(s_y, 1)

        @block.tensor
        def _(pe):
            pe.wait_ge(s_first, 16 * NFIRST)

            def query_block(k):
                transpose_block(pe, k)
                pe.wait_ge(s_xta, k + 1)
                pe.wait_ge(s_xtd, k + 1)
                if later(k):
                    pe.wait_ge(s_qb, 2 * k)
                for hf in range(C):
                    for c in range(C):
                        ins = nc.tensor.matmul(ps[:, 2 + hf, :], wx[:, 0, c, hf * P:(hf + 1) * P], xT[:, c, :], start=c == 0, stop=c == C - 1)
                    ins.then_inc(s_q, 1)

            blocks(pe, query_block)

            pe.wait_ge(s_load, 16 * NLOAD)
            pe.wait_ge(s_set, 6)
            for i, w in enumerate((wx, wa)):
                for c in range(C):
                    ins = nc.tensor.matmul(ps[:, 4, i * D:(i + 1) * D], bvb[:, i, c, :], w[:, 3, c, :], start=c == 0, stop=c == C - 1)
            ins.then_inc(s_corr_mm, 1)
            for hf in range(C):
                for c in range(C):
                    ins = nc.tensor.matmul(ps[:, 5, hf * B:(hf + 1) * B], wx[:, 2, c, hf * P:(hf + 1) * P], clast[:, c, :],
                                           start=c == 0, stop=c == C - 1)
            ins.then_inc(s_vlast_mm, 1)
            pe.wait_ge(s_qb, 2 * NB)
            pe.wait_ge(s_set, 9)

            def split_product(dst, lhs, rhs, chunks):
                terms = [(a, b, c) for c in range(chunks) for a, b in ((0, 0), (0, 1), (1, 0))]
                for i, (a, b, c) in enumerate(terms):
                    ins = nc.tensor.matmul(dst, lhs(a, c), rhs(b, c), start=i == 0, stop=i == len(terms) - 1)
                return ins

            def step(j, u):
                if has(j, u, 0):
                    pe.wait_ge(s_exp, 4 * (4 * j + u + 1))
                    if has(j, u, 2):
                        pe.wait_ge(s_kev, 2 * (4 * j + u + 3))
                    for c in range(2):
                        for g in range(4):
                            ins = nc.tensor.transpose(ps[:, c, g * P:(g + 1) * P], pexp[:, u, g, c * P:(c + 1) * P], ident)
                        ins.then_inc(s_T, 1)
                if has(j, u, 1):
                    m = u + 1
                    pair, slot = (m % 4) // 2, m % 2
                    pe.wait_ge(s_khl, 2 * (4 * j + m + 1))
                    if m % 2 == 0:
                        pe.wait_ge(qbd_in[pair], (j + m // 4 + 1) * 16 * HH)
                    for g in range(4):
                        hf, gl = g // 2, g % 2
                        ins = split_product(ps[:, 3 + g, 0:SP],
                                            lambda a, c: qbd[:, pair, a, hf].rearrange("p h x -> p (h x)")[:, 8 * T * gl + slot:8 * T * (gl + 1):2],
                                            lambda b, c: khl[:, slot, b, hf, :], 1)
                        if gl == 1:
                            ins.then_inc(s_S, 1)
                if has(j, u, 0):
                    b = 4 * j + u
                    pe.wait_ge(s_pt0, b + 1)
                    pe.wait_ge(s_pt1, b + 1)
                    pe.wait_ge(s_vev, b + 1)
                    if u % 2 == 0 and has(j, u, -1):
                        pe.wait_ge(s_fin, 2 * j + u // 2)
                    for hf in range(C):
                        for c in range(2):
                            for i in range(4):
                                col = (u % 2) * 128 + hf * 64
                                ins = nc.tensor.matmul(ps[32 * i:32 * i + 32, 7, col:col + 64],
                                                       vv[:, u, c, hf * P + 32 * i:hf * P + 32 * i + 32],
                                                       pt[:, u % 2, c, hf * 256 + 64 * i:hf * 256 + 64 * i + 64],
                                                       start=c == 0, stop=c == 1)
                    ins.then_inc(s_pv, 1)
                    if u % 2 == 1:
                        pe.wait_ge(s_dg, 2 * (2 * j + u // 2 + 1))
                        for hf in range(C):
                            for gl in range(2):
                                ins = nc.tensor.matmul(ps[:, 7, 256 + 128 * hf:384 + 128 * hf], const(f"pick{gl}"),
                                                       dg[:, u // 2, 2 * hf + gl].rearrange("p w b t -> p (w b t)"),
                                                       start=gl == 0, stop=gl == 1)
                        ins.then_inc(s_L, 1)
                if has(j, u, 3):
                    m, slot = u + 3, (u + 3) % 2
                    if has(j, u, 2) and not has(j, u, 0):
                        pe.wait_ge(s_kev, 2 * (4 * j + m))
                    pe.wait_ge(s_split, 2 * (4 * j + m + 1))
                    for hf in range(C):
                        split_product(ps[:, hf, 0:SP], lambda a, c: wk_hl[:, a, c, hf * P:(hf + 1) * P],
                                      lambda b, c: cx[:, slot, b, c, :], C).then_inc(s_K, 1)
                    if has(j, u, 2):
                        pe.wait_ge(s_vev, 4 * j + m)
                    for sc in range(2):
                        ins = split_product(ps[:, 2, sc * D:(sc + 1) * D], lambda a, c: cx[:, slot, a, c, sc * P:(sc + 1) * P],
                                            lambda b, c: wv_hl[:, b, c, :], C)
                    ins.then_inc(s_V, 1)

            cross_steps(pe, step)
            pe.wait_ge(s_fin, B // 2)

            def project_out(k, values_read=None):
                if values_read is not None:
                    pe.wait_ge(s_v2ev, values_read)
                pe.wait_ge(ast_in, 16 * (k + 1))
                for t in range(BLK):
                    for c in range(C):
                        ins = nc.tensor.matmul(ps[:, 4 + t // 2, t % 2 * D:(t % 2 + 1) * D], ast[:, c, t * P:(t + 1) * P], wx[:, 3, c, :],
                                               start=c == 0, stop=c == C - 1)
                    ins.then_inc(s_wo, 1)

            project_out(0)

            def block2(k):
                n = k + NB
                transpose_block(pe, n)
                if not isinstance(k, int) or k < NB - 1:
                    project_out(k + 1, 2 * k if later(k) else None)
                pe.wait_ge(s_xta, n + 1)
                pe.wait_ge(s_xtd, n + 1)
                if later(k):
                    pe.wait_ge(s_qkev, 4 * k)
                for i in range(4):
                    w, hf = i // 2, i % 2
                    for c in range(C):
                        ins = nc.tensor.matmul(ps[:, (2, 3, 6, 7)[i], :], wa[:, w, c, hf * P:(hf + 1) * P], xT[:, c, :],
                                               start=c == 0, stop=c == C - 1)
                    ins.then_inc(s_qk, 1)
                if not isinstance(k, int) or k < NB - 1:
                    pe.wait_ge(s_x1, 4 * k + 8)
                for t in range(BLK):
                    for c in range(C):
                        ins = nc.tensor.matmul(ps[:, 4 + t // 2, t % 2 * D:(t % 2 + 1) * D], xT[:, c, t * P:(t + 1) * P], wa[:, 2, c, :],
                                               start=c == 0, stop=c == C - 1)
                    if t % 2:
                        ins.then_inc(s_v2, 1)

            ahead_blocks(pe, block2)
            pe.wait_ge(s_v2ev, 2 * NB)
            pe.wait_ge(s_qkev, 4 * NB)

            def step2(m, u):
                n = 2 * m + u
                nslot = (u + 1) % 2
                if has2(m, u, -1):
                    pe.wait_ge(s_g, 2 * n)
                    if has2(m, u, -2):
                        pe.wait_ge(s_lg, n - 1)
                    for c in range(C):
                        ins = nc.tensor.matmul(ps[:, 6, 0:D], at2[:, nslot, c, :], wa[:, 3, c, :], start=c == 0, stop=c == C - 1)
                    ins.then_inc(s_wo2, 1)
                if has2(m, u, 2):
                    slot = u
                    pe.wait_ge(kq_in[slot], nth2(m, u, 2, 16 * (HH + 1)))
                    if has2(m, u, 0):
                        pe.wait_ge(s_kept, 2 * n + 2)
                    for b in range(4):
                        for hf in range(C):
                            ins = nc.tensor.matmul(ps[32 * b:32 * b + 32, slot, hf * 256:(hf + 1) * 256], qst[:, slot, hf, 32 * b:32 * b + 32],
                                                   kbd[:, slot, hf, :, 32 * b:32 * b + 32], start=True, stop=True)
                    ins.then_inc(s_S2, 1)
                if has2(m, u, 0):
                    wait_apart(pe, s_prt, n + 1)
                    wait_apart(pe, v_in[u], nth2(m, u, 0, 16))
                    if has2(m, u, -1):
                        wait_apart(pe, s_g, 2 * n)
                    for hf in range(C):
                        for i in range(4):
                            for b in range(4):
                                ins = nc.tensor.matmul(ps[32 * i:32 * i + 32, 2 + b, hf * 64:hf * 64 + 64],
                                                       vst[32 * b:32 * b + 32, u, hf * P + 32 * i:hf * P + 32 * i + 32],
                                                       prt[32 * b:32 * b + 32, u, HH * hf + 2 * i:HH * hf + 2 * i + 2, :],
                                                       start=True, stop=True)
                    ins.then_inc(s_pv2, 1)
                if has2(m, u, -1):
                    pe.wait_ge(s_xn2, n)
                    if has2(m, u, -2):
                        pe.wait_ge(s_xt2, n - 1)
                    for c in range(C):
                        ins = nc.tensor.transpose(ps[:, 7, c * P:(c + 1) * P], xn2[:, nslot, c * P:(c + 1) * P], ident)
                    ins.then_inc(s_tr2, 1)
                    pe.wait_ge(s_x2, n)
                    pe.wait_ge(s_xt2, n)
                    for c in range(C):
                        ins = nc.tensor.matmul(ps[:, 6, D:D + E], xt2[:, nslot, c, :], wr[:, c, :], start=c == 0, stop=c == C - 1)
                    ins.then_inc(s_rt, 1)

            self_steps(pe, step2)
            pe.wait_ge(s_lg, NT)
            pe.wait_ge(s_xt2, NT)
            pe.wait_ge(s_r, 10)
            hs = hsum.rearrange("p t e -> p (t e)")
            nc.tensor.matmul(ps[:, 3, 0:NT * E], const("before"), hs, start=True, stop=True)
            nc.tensor.matmul(ps[:, 3, NT * E:2 * NT * E], const("ones"), hs, start=True, stop=True).then_inc(s_cnt, 1)
            pe.wait_ge(s_pos, NPOS)

            def step3(m, u):
                n = 2 * m + u
                for q in range(NG):
                    k, gr = (q + LAG) // NG, (q + LAG) % NG
                    if has3(m, u, k):
                        slot, at = (u + k) % 2, NG * (n + k) + gr
                        pe.wait_ge(s_w1lo, at + 1)
                        if gr == 0:
                            pe.wait_ge(s_xlo, n + k + 1)
                        if gr >= 2 or has3(m, u, k - 1):
                            pe.wait_ge(s_relu, GF * (at - 1))
                        for f in range(GF):
                            ins = split_product(ps[:, gr % 2, f * SLOT:(f + 1) * SLOT],
                                                lambda a, c: whl[:, slot, a, GF * gr + f, c * P:(c + 1) * P],
                                                lambda b, c: xhl[:, slot, b, c, :], C)
                        ins.then_inc(s_w1, 1)
                    if q == 2 and has3(m, u, 2):
                        pe.wait_ge(x_in[u], nth2(m, u, 2, 16))
                        if has3(m, u, 1):
                            pe.wait_ge(s_xlo, n + 2)
                        for c in range(C):
                            for t in range(2):
                                ins = nc.tensor.transpose(ps[:, 2, c * SLOT + t * P:c * SLOT + (t + 1) * P], xraw[:, u, t, c * P:(c + 1) * P], ident)
                        ins.then_inc(s_xtr, 1)
                    if has3(m, u, 0):
                        pe.wait_ge(s_w2lo, NG * n + q + 1)
                        pe.wait_ge(s_hlo, NG * n + q + 1)
                        if q == 0 and has3(m, u, -2):
                            pe.wait_ge(s_yev, n - 1)
                        for t in range(2):
                            terms = [(a, b, f) for f in range(GF) for a, b in ((0, 0), (0, 1), (1, 0))]
                            for i, (a, b, f) in enumerate(terms):
                                ins = nc.tensor.matmul(ps[:, 4 + 2 * u + t, 0:D], hhl[:, q, a, f, t * P:(t + 1) * P], whl[:, u, b, GF * q + f, D:2 * D],
                                                       start=q == 0 and i == 0, stop=q == NG - 1 and i == len(terms) - 1)
                        ins.then_inc(s_w2, 1)

            expert_steps(pe, step3)
            pe.wait_ge(s_yev, NS)
            pe.wait_ge(b2_in, 16)
            for t in range(NT):
                ins = nc.tensor.transpose(ps[0:E, t // 4, t % 4 * P:(t % 4 + 1) * P], rw[:, t, :], ident)
                if t % 4 == 3:
                    ins.then_inc(s_rwT, 1)
            for t in range(NT):
                pe.wait_ge(s_rwTs, t // 4 + 1)
                if t >= 8 and t % 2 == 0:
                    pe.wait_ge(s_acc1, t // 2 - 3)
                ins = nc.tensor.matmul(ps[:, 4 + t // 2 % 4, t % 2 * D:(t % 2 + 1) * D], rwT[:, t, :], b2s[:], start=True, stop=True)
                if t % 2:
                    ins.then_inc(s_acc0, 1)


def kernel(**inputs):
    import concourse.bacc as bacc
    from concourse.bass_utils import run_bass_kernel_spmd as run

    a = {k: np.asarray(v) for k, v in inputs.items()}

    def chunked(w, n=C):
        return w.reshape(n, P, -1).transpose(1, 0, 2)

    ctx = a["ctx_1024"].transpose(0, 2, 1).reshape(B, C, P, S).transpose(0, 2, 1, 3)
    arrays = {
        "x": a["x"].reshape(TOK, D),
        "ctx_t": np.pad(ctx, ((0, 0), (0, 0), (0, 0), (0, SP - S))),
        "ctx_last": ctx[:, :, :, S - 1].transpose(1, 2, 0),
        "w_x": np.stack([chunked(a[f"L0_xattn_W{n}"].T) for n in "qkvo"], 1),
        "w_a": np.stack([chunked(a[f"L0_attn_W{n}"]) for n in "qkvo"], 1),
        "bias_cols": np.stack([a[f"L0_{m}_b{n}"].reshape(C, P).T for m in ("xattn", "attn") for n in "qkv"], 1),
        "bias_rows": np.stack([np.broadcast_to(r, (P, D)) for r in (a["L0_xattn_bo"], a["L0_attn_bo"], a["L0_ffn_gamma"], a["L0_ffn_beta"])], 1),
        "w_r": chunked(a["L0_ffn_Wr"].T),
        "b_r": np.broadcast_to(a["L0_ffn_br"], (P, E)),
        "w_e": np.concatenate([np.concatenate([a["L0_ffn_W1"].reshape(E, FC, P, C, P).transpose(0, 4, 1, 3, 2).reshape(E, P, FC, D),
                                               a["L0_ffn_W2"].transpose(0, 2, 1).reshape(E, FC, P, D).transpose(0, 2, 1, 3)], 3)
                               .reshape(E, P, 2 * FC * D),
                               a["L0_ffn_b1"].reshape(E, FC, P).transpose(0, 2, 1)], 2).reshape(E * P, WROW),
        "b_2": a["L0_ffn_b2"],
        "consts": build_consts(),
    }
    nc = bacc.Bacc("TRN2", target_bir_lowering=False, num_devices=1)
    arrays = {f"{n}_dram": np.ascontiguousarray(v) for n, v in arrays.items()}
    args = [nc.dram_tensor(n, v.shape, F32, kind="ExternalInput").ap() for n, v in arrays.items()]
    args.append(nc.dram_tensor("out_dram", (TOK, D), F32, kind="ExternalOutput").ap())
    perceiver(nc, *args)
    return run(nc, [arrays], core_ids=[0]).results[0]["out_dram"].reshape(B, T, D)
```

```python
from contextlib import ExitStack

import numpy as np

import concourse.bass as bass
from concourse import mybir

P = 128
B, T, D, S = 64, 32, 256, 257
SP = S + 1
H, HD = 16, 16
TOK = B * T
NT = TOK // P
C = D // P
BLK = 4
NB = NT // BLK
HH = H // C
TOPK = 16
E, F = 8, 1024
FC = F // P
LN_EPS = 1e-5
SLOT = 256
NS = (2 * TOK + E * (SLOT - 1)) // SLOT
GF = 2
NG = FC // GF
WROW = FC * 2 * D + FC
LAG = 3
SPLIT = 6
TAKEN = -3.0e38

F32 = mybir.dt.float32
F32R = mybir.dt.float32r
U32 = mybir.dt.uint32
ALU = mybir.AluOpType
ACT = mybir.ActivationFunctionType
AX = mybir.AxisListType.X
ds = bass.ds

CONSTS = {}


def build_consts():
    cols = {}
    p = np.arange(P)
    cols["ident"] = np.eye(P)
    cols["delta"] = (p[:, None] % T == np.arange(T)[None, :])
    chan = np.arange(P)
    for gl in range(2):
        cols[f"pick{gl}"] = (chan[None, :] // 64 == gl) & (chan[None, :] % 64 // HD == p[:, None] // T)
    cols["parity"] = np.stack([p // HD % 2 == 0, p // HD % 2 == 1], 1)
    cols["before"] = p[:, None] < p[None, :]
    cols["ones"] = np.ones((P, P))
    cols["slot_no"] = np.tile(np.arange(NS), (P, 1))
    cols["steps"] = np.tile(SLOT * np.arange(TOK // SLOT), (P, 1))
    cols["part"] = p[:, None]
    cols["row_no"] = np.tile(np.arange(P), (P, 1))
    cols["col_no"] = np.tile(np.arange(NS * SLOT // P), (P, 1))
    cols["result"] = 1 + np.arange(2 * NT)[None, :] * P + p[:, None]
    cols["spare"] = 1 + 2 * TOK + np.arange(NS * SLOT // P)[None, :] * P + p[:, None]
    cols["iota"] = np.tile(np.arange(E), (P, 1))
    half = HD // 2
    base = ((np.arange(0, HD, 2, dtype=np.float32) + np.float32(0.4 * HD)) / np.float32(1.4 * HD)).astype(np.float32)
    inv_freq = (1.0 / np.float32(10000.0) ** (np.arange(half, dtype=np.float32) / half)).astype(np.float32)
    for name, length, down, factor in (("k", S, True, 1.0), ("q", T, False, HD ** -0.5)):
        pos = np.arange(length, dtype=np.float32)
        scale = base[None, :] ** (pos[:, None] / np.float32(D))
        if down:
            scale = np.float32(1.0) / scale
        angle = pos[:, None] * inv_freq[None, :]
        pair = p % HD // 2
        cos = (np.cos(angle) * scale * factor)[:, pair].T
        sin = (np.sin(angle) * scale * factor)[:, pair].T * np.where(p % 2 == 0, 1.0, -1.0)[:, None]
        if length % 2:
            cos, sin = np.pad(cos, ((0, 0), (0, 1))), np.pad(sin, ((0, 0), (0, 1)))
        cols[name + "cos"], cols[name + "sin"] = cos, sin
    at = 0
    for name, a in cols.items():
        CONSTS[name] = (at, a.shape[1])
        at += a.shape[1]
    return np.ascontiguousarray(np.concatenate([np.asarray(a, np.float32) for a in cols.values()], 1))


build_consts()
NCONST = sum(n for _, n in CONSTS.values())
QX, KX, VX, QA, KA, VA = range(6)
BOX, BOA, GAMMA, BETA = range(4)


def perceiver(nc, x, ctx_t, ctx_last, w_x, w_a, bias_cols, bias_rows, w_r, b_r, w_e, b_2, consts, out):
    with ExitStack() as stack:
        def sb(name, shape, dt=F32):
            return stack.enter_context(nc.sbuf_tensor(name, shape, dt))

        def sem(name):
            return stack.enter_context(nc.semaphore(name))

        x_rows = nc.dram_tensor("x_rows", (TOK, D), F32, kind="Internal").ap()
        y_rows = nc.dram_tensor("y_rows", (1 + 2 * TOK + NS * SLOT, D), F32, kind="Internal").ap()

        cst = sb("cst", [P, NCONST])
        wx = sb("wx", [P, 4, C, D])
        wa = sb("wa", [P, 4, C, D])
        bcol = sb("bcol", [P, 6, C])
        brow = sb("brow", [P, 4, D])
        wr = sb("wr", [P, C, E])
        br = sb("br", [P, E])
        xs = sb("xs", [P, NT, D])
        xnrm = sb("xnrm", [P, BLK, D])
        stats = sb("stats", [P, BLK, 6])
        mv = sb("mv", [P, BLK, 2])
        rstd = sb("rstd", [P, BLK])
        vareps = sb("vareps", [P, BLK])
        nhalf = sb("nhalf", [P, BLK])
        bvb = sb("bvb", [P, 2, C, P])
        ocorr = sb("ocorr", [P, 2, D])
        ps = stack.enter_context(nc.psum_tensor("ps", [P, 8, 512], F32))

        def const(name):
            at, n = CONSTS[name]
            return cst[:, at:at + n]

        ident, delta, parity = const("ident"), const("delta"), const("parity")

        x_first_in = sem("x_first_in")
        x_rest_in = sem("x_rest_in")
        first_in = sem("first_in")
        rest_in = sem("rest_in")
        setup_step = sem("setup_step")
        xs_biased = sem("xs_biased")
        bias_projected = sem("bias_projected")
        last_projected = sem("last_projected")
        stats_done = sem("stats_done")
        rstd_done = sem("rstd_done")
        tile_normed = sem("tile_normed")
        chunk_transposed = sem("chunk_transposed")
        xT0_out = sem("xT0_out")
        xT1_out = sem("xT1_out")
        qbd_zeroed = sem("qbd_zeroed")
        stored = [sem(f"stored{i}") for i in range(2)]

        NFIRST, NLOAD = 3, 5
        NPOS = 32

        def wait_apart(eng, semaphore, value):
            value = value if isinstance(value, int) else eng.to_reg(value)
            eng.wait_ge(x_first_in, 16)
            eng.wait_ge(semaphore, value)

        def ln_stats(v, tile_of, n, mv=mv):
            for t in range(BLK):
                nc.vector.bn_stats(stats[:, t, :], tile_of(t)).then_inc(stats_done, 1)
            wait_apart(v, stats_done, 8 * n + 4)
            for t in range(BLK):
                nc.vector.bn_aggr(mv[:, t, :], stats[:, t, :]).then_inc(stats_done, 1)

        def ln_apply(v, tile_of, n):
            v.wait_ge(rstd_done, 2 * n + 2)
            for t in range(BLK):
                nc.vector.tensor_scalar(xnrm[:, t, :], tile_of(t), mv[:, t, 0:1], rstd[:, t:t + 1],
                                        ALU.subtract, ALU.mult).then_inc(tile_normed, 1)

        def ln_rstd(g, n, mv=mv, rstd=rstd):
            wait_apart(g, stats_done, 8 * n + 8)
            nc.gpsimd.tensor_scalar(vareps[:], mv[:, :, 1], LN_EPS, None, ALU.add).then_inc(rstd_done, 1)
            g.wait_ge(rstd_done, 2 * n + 1)
            nc.gpsimd.tensor_tensor(rstd[:, 0:BLK], vareps[:], nhalf[:], ALU.pow).then_inc(rstd_done, 1)

        def transpose_block(pe, n):
            for t in range(BLK):
                pe.wait_ge(tile_normed, 4 * n + t + 1)
                for c in range(C):
                    ins = nc.tensor.transpose(ps[:, c, t * P:(t + 1) * P], xnrm[:, t, c * P:(c + 1) * P], ident)
                    if t == BLK - 1:
                        ins.then_inc(chunk_transposed, 1)

        late = ExitStack()
        xT = late.enter_context(nc.sbuf_tensor("xT", [P, C, BLK * P], F32))

        a_ = ExitStack()

        def asb(name, shape, dt=F32):
            return a_.enter_context(nc.sbuf_tensor(name, shape, dt))

        ast = late.enter_context(nc.sbuf_tensor("ast", [P, C, BLK * P], F32))
        attn_t = late.enter_context(nc.sbuf_tensor("attn_t", [P, C, TOK], F32))
        wk_hl = asb("wk_hl", [P, 2, C, D], F32R)
        wv_hl = asb("wv_hl", [P, 2, C, D], F32R)
        q_hl = asb("q_hl", [P, 2, C, TOK], F32R)
        clast = asb("clast", [P, C, B])
        vlast = asb("vlast", [P, C, B])
        raw = asb("raw", [P, 2, C, SP])
        cx = asb("cx", [P, 2, 2, C, SP], F32R)
        kb = asb("kb", [P, 2, C, SP])
        kc = asb("kc", [P, 2, C, SP])
        ks = asb("ks", [P, 2, C, SP])
        kw = asb("kw", [P, 2, C, SP])
        khl = asb("khl", [P, 2, 2, C, SP], F32R)
        vv = asb("vv", [P, 4, 2, D])
        qbd = asb("qbd", [P, 2, 2, C, HH, 2 * T], F32R)
        room = asb("room", [P, 4 * 4 * SP])
        qb, qc, qs, qw = (room[:, 1024 * i:1024 * (i + 1)].rearrange("p (c t) -> p c t", c=C) for i in range(4))
        pexp = room[:].rearrange("p (s g k) -> p s g k", s=4, g=4)
        negmax = asb("negmax", [P, 4, 4])
        rsum = asb("rsum", [P, 4, 4])
        rrec = asb("rrec", [P, 2, 2, 4])
        pt = asb("pt", [P, 2, 2, 512])
        dg = asb("dg", [P, 2, 4, 2, 2, T])
        f1 = asb("f1", [P, 2, C, T])
        f2 = asb("f2", [P, 2, C, T])
        f3 = asb("f3", [P, C, 2, T])
        f4 = asb("f4", [P, C, 2, T])

        q_projected = sem("q_projected")
        q_biased = sem("q_biased")
        q_cos_done = sem("q_cos_done")
        q_step_done = sem("q_step_done")
        ctx_in = [sem(f"ctx_in{i}") for i in range(2)]
        k_swapped = sem("k_swapped")
        qbd_in = [sem(f"qbd_in{i}") for i in range(2)]
        ctx_split = sem("ctx_split")
        keys_projected = sem("keys_projected")
        values_projected = sem("values_projected")
        keys_biased = sem("keys_biased")
        values_out = sem("values_out")
        k_cos_done = sem("k_cos_done")
        k_sin_done = sem("k_sin_done")
        k_rotated = sem("k_rotated")
        k_split = sem("k_split")
        scores_ready = sem("scores_ready")
        max_ready = sem("max_ready")
        exp_ready = sem("exp_ready")
        exp_transposed = sem("exp_transposed")
        chunk0_out = sem("chunk0_out")
        chunk1_out = sem("chunk1_out")
        pv_ready = sem("pv_ready")
        sums_inverted = sem("sums_inverted")
        diagonals_ready = sem("diagonals_ready")
        spread_ready = sem("spread_ready")
        finish_step = sem("finish_step")
        pair_done = sem("pair_done")

        J0, J1 = 1, 14

        def has(j, u, k):
            return not isinstance(j, int) or 0 <= 4 * j + u + k < B

        def cross_steps(eng, step):
            for b in range(-6, 4 * J0):
                step(b // 4, b % 4)
            with eng.Fori(J0, J1) as j:
                for u in range(4):
                    step(j, u)
            for b in range(4 * J1, B):
                step(b // 4, b % 4)

        def nth(j, m, slots, per):
            return (4 // slots * j + m // slots + 1) * per

        a_.close()

        b_ = ExitStack()

        def bsb(name, shape, dt=F32):
            return b_.enter_context(nc.sbuf_tensor(name, shape, dt))

        x2n = attn_t[:].rearrange("p c t -> p (c t)").rearrange("p (a d) -> p a d", a=NT)
        logits = bsb("logits", [P, NT, E])
        qt_all = bsb("qt_all", [P, C, TOK])
        kt_all = bsb("kt_all", [P, C, TOK])
        v_all = bsb("v_all", [P, NT, D])
        wa_hl = bsb("wa_hl", [P, 2, 3, C, D], F32R)
        x_hl = bsb("x_hl", [P, 2, C, BLK * P], F32R)
        bq4 = bsb("bq4", [P, C])
        kbd = bsb("kbd", [P, 2, C, HH, P])
        qst = bsb("qst", [P, 2, C, P])
        vst = bsb("vst", [P, 2, D])
        top_a = bsb("top_a", [P, 2, H, 8])
        top_b = bsb("top_b", [P, H, 8])
        left_a = bsb("left_a", [P, H, T])
        left_b = bsb("left_b", [P, H, T])
        kept = bsb("kept", [P, 2, H, T])
        rmax = bsb("rmax", [P, 2, H])
        shifted = bsb("shifted", [P, 2, H, T])
        pr = bsb("pr", [P, 2, H, T])
        prs = bsb("prs", [P, H])
        prr = bsb("prr", [P, H])
        prn = bsb("prn", [P, H, T])
        prt = bsb("prt", [P, 2, H, T])
        g1 = bsb("g1", [P, C, 4, T])
        at2 = bsb("at2", [P, 2, C, P])
        st2 = bsb("st2", [P, 8])
        xn2 = bsb("xn2", [P, 2, D])
        xt2 = bsb("xt2", [P, 2, C, P])

        ast_in = sem("ast_in")
        out_projected = sem("out_projected")
        tile_added = sem("tile_added")
        block_biased = sem("block_biased")
        wa_split = sem("wa_split")
        block_hi = sem("block_hi")
        block_lo = sem("block_lo")
        qk_projected = sem("qk_projected")
        qk_out = sem("qk_out")
        v_projected = sem("v_projected")
        v_out = sem("v_out")
        phase_ready = sem("phase_ready")
        kq_in = [sem(f"kq_in{i}") for i in range(2)]
        v_in = [sem(f"v_in{i}") for i in range(2)]
        self_scores = sem("self_scores")
        rank_step = sem("rank_step")
        kept_ready = sem("kept_ready")
        shifted_ready = sem("shifted_ready")
        self_exp = sem("self_exp")
        self_sums = sem("self_sums")
        probs_ready = sem("probs_ready")
        probs_transposed = sem("probs_transposed")
        self_pv = sem("self_pv")
        even_picked = sem("even_picked")
        odd_added = sem("odd_added")
        self_projected = sem("self_projected")
        self_added = sem("self_added")
        self_stats = sem("self_stats")
        self_rstd = sem("self_rstd")
        self_normed = sem("self_normed")
        self_transposed = sem("self_transposed")
        xt2_out = sem("xt2_out")
        router_ready = sem("router_ready")
        logits_ready = sem("logits_ready")
        x2n_in = [sem(f"x2n_in{i}") for i in range(2)]

        M0, M1 = 2, 6

        def has2(m, u, k):
            return not isinstance(m, int) or 0 <= 2 * m + u + k < NT

        def self_steps(eng, step):
            for j in range(-3, 2 * M0):
                step(j // 2, j % 2)
            with eng.Fori(M0, M1) as m:
                for u in range(2):
                    step(m, u)
            for j in range(2 * M1, NT + 2):
                step(j // 2, j % 2)

        def nth2(m, u, k, per):
            return (m + (u + k) // 2 + 1) * per

        def blocks(eng, body):
            body(0)
            with eng.Fori(1, NB) as k:
                body(k)

        def ahead_blocks(eng, body):
            body(0)
            with eng.Fori(1, NB - 1) as k:
                body(k)
            body(NB - 1)

        def later(k):
            return not isinstance(k, int) or k > 0

        b_.close()

        NCOL = NS * SLOT // P
        NJ = 2 * NT
        PIECE = 8
        c_ = ExitStack()

        def csb(name, shape, dt=F32):
            return c_.enter_context(nc.sbuf_tensor(name, shape, dt))

        logits_ = csb("logits_c", [P, NT, E])
        h32 = csb("h32", [P, 2, GF, SLOT])
        yst = csb("yst", [P, 2, 2, D])
        xraw = ast[:].rearrange("p c t -> p (c t)").rearrange("p (s a d) -> p s a d", s=2, a=2)
        yo = [a[:].rearrange("p c t -> p (c t)").rearrange("p (a d) -> p a d", a=BLK) for a in (xT, ast)]
        wraw = csb("wraw", [P, 2, WROW])
        yg = wraw[:].rearrange("p s w -> p (s w)")[:, 0:2 * NT * D].rearrange("p (i t d) -> p i t d", i=2, t=NT)
        whl = csb("whl", [P, 2, 2, FC, 2 * D], F32R)
        xhl = csb("xhl", [P, 2, 2, C, SLOT], F32R)
        hhl = csb("hhl", [P, NG, 2, GF, SLOT], F32R)
        flat = hhl[:].rearrange("p g a f t -> p (g a f t)")
        rowhot = [flat[:, i * PIECE * P:(i + 1) * PIECE * P].rearrange("p (j r) -> p j r", j=PIECE) for i in range(2)]
        colhot = [flat[:, (2 + i) * PIECE * P:(2 + i) * PIECE * P + PIECE * NCOL].rearrange("p (j c) -> p j c", j=PIECE) for i in range(2)]
        bst = csb("bst", [P, 2, FC])
        ist = csb("ist", [P, 2], U32)
        xist = csb("xist", [P, 2, 2], U32)
        yist = csb("yist", [P, 2, 2], U32)
        b2s = csb("b2s", [E, D])
        room_at = [0]

        def small(shape):
            n = int(np.prod(shape[1:]))
            view = wx[:].rearrange("p w c d -> p (w c d)")[:, room_at[0]:room_at[0] + n]
            room_at[0] += n
            assert room_at[0] <= 4 * C * D
            if len(shape) == 3:
                return view.rearrange("p (a b) -> p a b", a=shape[1])
            return view if len(shape) == 2 else view.rearrange("p (a b c) -> p a b c", a=shape[1], b=shape[2])

        rank = small([P, NT, 8])
        rix = csb("rix", [P, NT, 8], U32)
        rixf = small([P, NT, 2])
        rdiff = small([P, NT])
        mvf = [small([P, BLK, 2]) for _ in range(2)]
        rstdf = [small([P, BLK]) for _ in range(2)]
        nmr = [small([P, BLK]) for _ in range(2)]
        rexp = small([P, NT])
        rtmp = small([P, NT])
        rwt = small([P, NT, 2])
        hot = small([P, 2, NT, E])
        rw = small([P, NT, E])
        rwT = wa[0:E].rearrange("p w c d -> p (w c d)").rearrange("p (t x) -> p t x", t=NT)
        hw = small([P, 2, NT, E])
        hsum = small([P, NT, E])
        cnt = small([P, 2, NT, E])
        over = small([P, E, TOK // SLOT])
        tl = small([P, E])
        st8 = small([P, 2, E])
        start = small([P, E])
        below = small([P, NS, E - 1])
        eix = small([P, NS])
        eixu = csb("eixu", [P, NS], U32)
        posf = small([P, 2, NT])
        bitf = small([P, 2, NJ])
        resf = small([P, 3, NCOL])
        posu = csb("posu", [P, 2, NT], U32)
        bitu = csb("bitu", [P, 2, NJ], U32)
        tok_of = csb("tok_of", [P, NCOL], U32)
        res_of = csb("res_of", [P, NCOL], U32)

        w_in = [sem(f"w_in{i}") for i in range(2)]
        route_step = sem("route_step")
        route_exp = sem("route_exp")
        counts_ready = sem("counts_ready")
        position_step = sem("position_step")
        bits_step = sem("bits_step")
        rowhot_ready = sem("rowhot_ready")
        coleq_ready = sem("coleq_ready")
        colhot_ready = sem("colhot_ready")
        table_piece = sem("table_piece")
        table_step = sem("table_step")
        result_rows_staged = sem("result_rows_staged")
        tokens_staged = sem("tokens_staged")
        x_in = [sem(f"x_in{i}") for i in range(2)]
        y_out = [sem(f"y_out{i}") for i in range(2)]
        g_in = [sem(f"g_in{i}") for i in range(NB)]
        b2_in = sem("b2_in")
        weight_rows_staged = sem("weight_rows_staged")
        b1_staged = sem("b1_staged")
        w1_hi = sem("w1_hi")
        w1_lo = sem("w1_lo")
        w2_hi = sem("w2_hi")
        w2_lo = sem("w2_lo")
        slot_transposed = sem("slot_transposed")
        slot_hi = sem("slot_hi")
        slot_lo = sem("slot_lo")
        hidden_ready = sem("hidden_ready")
        relu_ready = sem("relu_ready")
        hidden_lo = sem("hidden_lo")
        second_done = sem("second_done")
        result_out = sem("result_out")
        router_w_transposed = sem("router_w_transposed")
        router_w_out = sem("router_w_out")
        b2_product = sem("b2_product")
        b2_added = sem("b2_added")
        combined = sem("combined")
        shift_step = sem("shift_step")
        beta_added = sem("beta_added")
        block_ready = sem("block_ready")
        half_ready = sem("half_ready")
        gamma_done = sem("gamma_done")
        ranks_ready = sem("ranks_ready")

        S0, S1 = 2, (NS - 3) // 2

        def has3(m, u, k):
            return not isinstance(m, int) or 0 <= 2 * m + u + k < NS

        def input_step(m, u, q):
            n = 2 * m + u
            if isinstance(n, int) and n < 0:
                return 1 if (n, q) == (-1, 0) else 2 if (n, q) == (-1, 2) else None
            return 2 if q == 2 and has3(m, u, 2) else None

        def raw_part(slot, gr, w):
            rows = wraw[:, slot, 2 * D * GF * gr:2 * D * GF * (gr + 1)].rearrange("p (f w) -> p f w", f=GF)
            return rows[:, :, w * D:(w + 1) * D]

        def split_part(slot, part, gr, w):
            return whl[:, slot, part, GF * gr:GF * (gr + 1), w * D:(w + 1) * D]

        def expert_steps(eng, step):
            for n in range(-3, 2 * S0):
                step(n // 2, n % 2)
            with eng.Fori(S0, S1) as m:
                for u in range(2):
                    step(m, u)
            for n in range(2 * S1, NS + 1):
                step(n // 2, n % 2)

        c_.close()

        stack.enter_context(late)
        block = stack.enter_context(nc.Block())

        @block.sync
        def _(sp):
            x_v = x.rearrange("(j p) c -> p j c", p=P)
            sp.dma_start(xs[:, 0:BLK], x_v[:, 0:BLK]).then_inc(x_first_in, 16)
            sp.dma_start(cst[:], consts).then_inc(first_in, 16)
            sp.dma_start(wx[:], w_x).then_inc(first_in, 16)
            sp.dma_start(bcol[:], bias_cols).then_inc(first_in, 16)
            sp.dma_start(xs[:, BLK:NT], x_v[:, BLK:NT]).then_inc(x_rest_in, 16)
            sp.dma_start(brow[:], bias_rows).then_inc(rest_in, 16)
            sp.dma_start(clast[:], ctx_last).then_inc(rest_in, 16)
            sp.dma_start(wa[:], w_a).then_inc(rest_in, 16)
            sp.dma_start(wr[:], w_r).then_inc(rest_in, 16)
            sp.dma_start(br[:], b_r).then_inc(rest_in, 16)

            def fill_queries(slot, first):
                for h in range(HH):
                    rows = slice(HD * h, HD * (h + 1))
                    sp.dma_start(qbd[rows, slot, :, :, h, :].bitcast(F32), q_hl[rows, :, :, ds(first, 2 * T)].bitcast(F32)).then_inc(qbd_in[slot], 16)

            def step(j, u):
                if has(j, u, 6):
                    m, slot = u + 6, (u + 6) % 2
                    if has(j, u, 4):
                        wait_apart(sp, ctx_split, 2 * (4 * j + u + 5))
                    sp.dma_start(raw[:, slot], ctx_t[ds(4 * j + m, 1)].rearrange("a p c s -> p (a c) s")).then_inc(ctx_in[slot], 16)
                if u % 2 == 1 and has(j, u, 0) and has(j, u, 4):
                    wait_apart(sp, scores_ready, 2 * (4 * j + u + 1))
                    fill_queries(u // 2, 128 * j + 32 * (u - 1) + 4 * T)

            for b in range(-6, -2):
                step(b // 4, b % 4)
            sp.wait_ge(q_step_done, 5)
            sp.wait_ge(qbd_zeroed, 1)
            fill_queries(0, 0)
            fill_queries(1, 2 * T)
            for b in range(-2, 4 * J0):
                step(b // 4, b % 4)
            with sp.Fori(J0, J1) as j:
                for u in range(4):
                    step(j, u)
            for b in range(4 * J1, B):
                step(b // 4, b % 4)

            def stage(k):
                if later(k):
                    sp.wait_ge(pair_done, B // 2)
                    wait_apart(sp, out_projected, 4 * k)
                else:
                    sp.wait_ge(pair_done, B // 2 // NB)
                sp.dma_start(ast[:], attn_t[:, :, ds(512 * k, 512)]).then_inc(ast_in, 16)

            blocks(sp, stage)
            sp.wait_ge(v_out, 2)
            sp.wait_ge(qk_out, 4)
            sp.wait_ge(phase_ready, 2)

            def step2(m, u):
                if has2(m, u, 3):
                    slot = (u + 3) % 2
                    if has2(m, u, 1):
                        wait_apart(sp, self_scores, 2 * m + u + 2)
                    first = 256 * m + 128 * (u + 3)
                    sp.dma_start(qst[:, slot], qt_all[:, :, ds(first, P)]).then_inc(kq_in[slot], 16)
                    for h in range(HH):
                        rows = slice(HD * h, HD * (h + 1))
                        sp.dma_start(kbd[rows, slot, :, h, :], kt_all[rows, :, ds(first, P)]).then_inc(kq_in[slot], 16)
                if has2(m, u, 1):
                    slot = (u + 1) % 2
                    if has2(m, u, -1):
                        wait_apart(sp, self_pv, 2 * m + u)
                    sp.dma_start(vst[:, slot], v_all[:, ds(2 * m + u + 1, 1), :].rearrange("p a d -> p (a d)")).then_inc(v_in[slot], 16)
                if has2(m, u, -1):
                    slot = (u + 1) % 2
                    wait_apart(sp, self_normed, 2 * m + u)
                    sp.dma_start(x2n[:, ds(2 * m + u - 1, 1), :].rearrange("p a d -> p (a d)"), xn2[:, slot]).then_inc(x2n_in[slot], 16)
                    sp.dma_start(x_rows[ds(P * (2 * m + u - 1), P), :], xn2[:, slot]).then_inc(x2n_in[slot], 16)

            self_steps(sp, step2)
            sp.wait_ge(logits_ready, NT)
            for i in range(2):
                sp.wait_ge(x2n_in[i], 32 * NT // 2)
            sp.dma_start(b2s[:], b_2).then_inc(b2_in, 16)
            sp.wait_ge(y_out[0], 32 * ((NS + 1) // 2))
            sp.wait_ge(y_out[1], 32 * (NS // 2))
            for k in range(NB):
                for i in range(2):
                    first = 1 + i * TOK + BLK * k * P
                    sp.dma_start(yg[:, i, BLK * k:BLK * (k + 1), :], y_rows[first:first + BLK * P, :].rearrange("(t p) d -> p t d", p=P)).then_inc(g_in[k], 16)
            out_v = out.rearrange("(j p) c -> p j c", p=P)

            for k in range(NB - 1):
                sp.wait_ge(block_ready, k + 1)
                sp.dma_start(out_v[:, BLK * k:BLK * (k + 1), :], yo[k % 2]).then_inc(stored[k % 2], 16)
            for hf in range(2):
                sp.wait_ge(half_ready, hf + 1)
                first = BLK * (NB - 1) + BLK // 2 * hf
                sp.dma_start(out_v[:, first:first + BLK // 2, :], yo[(NB - 1) % 2][:, BLK // 2 * hf:BLK // 2 * (hf + 1)]).then_inc(stored[(NB - 1) % 2], 16)
            for i in range(2):
                sp.wait_ge(stored[i], 16 * (NB // 2 + i))

        @block.gpsimd
        def _(g):
            nc.gpsimd.memset(nhalf[:], -0.5).then_inc(xs_biased, 1)
            g.wait_ge(xs_biased, 1)
            ln_rstd(g, 0)
            nc.gpsimd.memset(qbd[:].bitcast(F32), 0.0).then_inc(qbd_zeroed, 1)
            for k in range(NB):
                if k + 1 < NB:
                    ln_rstd(g, k + 1)
                g.wait_ge(q_biased, 2 * k + 2)
                if k:
                    g.wait_ge(q_step_done, 5 * k)
                by_pos = lambda a: a.rearrange("p c (b t) -> p (c b) t", t=T)
                nc.gpsimd.tensor_tensor(by_pos(qc), by_pos(qb), const("qcos").unsqueeze(1).to_broadcast([P, C * BLK * 4, T]),
                                        ALU.mult).then_inc(q_cos_done, 1)

            def step(j, u):
                if has(j, u, 2):
                    m, slot = u + 2, (u + 2) % 2
                    g.wait_ge(keys_biased, 2 * (4 * j + m + 1))
                    if has(j, u, 0):
                        g.wait_ge(k_swapped, 4 * j + u + 1)
                    nc.gpsimd.tensor_tensor(ks[:, slot], kb[:, slot], const("ksin").unsqueeze(1).to_broadcast([P, C, SP]),
                                            ALU.mult).then_inc(k_sin_done, 1)
                if u % 2 == 1 and has(j, u, 0):
                    pair, slot = 2 * j + u // 2, u // 2
                    g.wait_ge(exp_ready, 4 * (4 * j + u + 1))
                    g.wait_ge(sums_inverted, pair + 1)
                    if has(j, u, -4):
                        g.wait_ge(spread_ready, pair - 1)
                    dl = delta.unsqueeze(1).unsqueeze(1).to_broadcast([P, 2, 4, T])
                    nc.gpsimd.tensor_tensor(dg[:, slot, :, 0].rearrange("p g b t -> p b g t"),
                                            pexp[:, u - 1:u + 1, :, S - 1:S].to_broadcast([P, 2, 4, T]), dl, ALU.mult).then_inc(diagonals_ready, 1)
                    nc.gpsimd.tensor_tensor(dg[:, slot, :, 1].rearrange("p g b t -> p b g t"),
                                            rrec[:, slot].unsqueeze(3).to_broadcast([P, 2, 4, T]), dl, ALU.mult).then_inc(diagonals_ready, 1)
                if u == 0 and has(j, u, 0):
                    g.wait_ge(setup_step, 8)
                    g.wait_ge(tile_normed, NT)
                    nc.gpsimd.tensor_tensor(xs[:, ds(j, 1), :].rearrange("p a d -> p (a d)"), xs[:, ds(j, 1), :].rearrange("p a d -> p (a d)"),
                                            ocorr[:, 0, :], ALU.add).then_inc(xs_biased, 1)
                if has(j, u, 4):
                    m, slot = u + 4, (u + 4) % 2
                    wait_apart(g, ctx_in[slot], nth(j, m, 2, 16))
                    if has(j, u, 2):
                        g.wait_ge(values_projected, 4 * j + u + 3)
                    nc.gpsimd.tensor_scalar(cx[:, slot, 0], raw[:, slot], 1.0, None, ALU.mult).then_inc(ctx_split, 1)
                    g.wait_ge(ctx_split, 2 * (4 * j + m) + 1)
                    nc.gpsimd.tensor_tensor(cx[:, slot, 1], raw[:, slot], cx[:, slot, 0].bitcast(F32), ALU.subtract).then_inc(ctx_split, 1)

            cross_steps(g, step)
            g.wait_ge(pair_done, B // 2)
            nc.gpsimd.memset(kbd[:], 0.0).then_inc(phase_ready, 1)

            def block2(k):
                ln_rstd(g, k + NB)
                wait_apart(g, tile_normed, 4 * (k + NB) + 4)
                rows = xs[:, ds(4 * k, 4), :]
                nc.gpsimd.tensor_tensor(rows, rows, ocorr[:, 1, :].unsqueeze(1).to_broadcast([P, BLK, D]), ALU.add).then_inc(block_biased, 1)

            blocks(g, block2)

            def step2(m, u):
                if has2(m, u, 0):
                    n = 2 * m + u
                    g.wait_ge(self_sums, 2 * n + 2)
                    if has2(m, u, -1):
                        g.wait_ge(probs_transposed, n)
                    nc.gpsimd.tensor_tensor(prn[:], pr[:, u], prr[:].unsqueeze(2).to_broadcast([P, H, T]), ALU.mult).then_inc(probs_ready, 1)
                if has2(m, u, -1):
                    n = 2 * m + u - 1
                    wait_apart(g, self_stats, 2 * n + 2)
                    nc.gpsimd.tensor_scalar(st2[:, 2:3], st2[:, 1:2], LN_EPS, None, ALU.add).then_inc(self_rstd, 1)
                    g.wait_ge(self_rstd, 2 * n + 1)
                    nc.gpsimd.tensor_tensor(rstd[:, 0:1], st2[:, 2:3], nhalf[:, 0:1], ALU.pow).then_inc(self_rstd, 1)
                if has2(m, u, 1):
                    n, slot = 2 * m + u + 1, (u + 1) % 2
                    g.wait_ge(kept_ready, 2 * n + 2)
                    if has2(m, u, -1):
                        g.wait_ge(self_exp, n - 1)
                    nc.gpsimd.tensor_tensor(shifted[:, slot], kept[:, slot], rmax[:, slot].unsqueeze(2).to_broadcast([P, H, T]),
                                            ALU.subtract).then_inc(shifted_ready, 1)

            self_steps(g, step2)

            def load_weights(slot):
                nc.gpsimd.indirect_dma_start(wraw[:, slot], None, w_e, bass.IndirectOffsetOnAxis(ist[:, slot:slot + 1], 0)).then_inc(w_in[slot], 16)

            g.wait_ge(weight_rows_staged, 2)
            load_weights(0)
            load_weights(1)
            for c in range(NJ // PIECE):
                js = slice(PIECE * c, PIECE * (c + 1))
                g.wait_ge(coleq_ready, c + 1)
                nc.gpsimd.tensor_tensor(colhot[c % 2], colhot[c % 2].bitcast(F32), const("result")[:, js].unsqueeze(2).to_broadcast([P, PIECE, NCOL]),
                                        ALU.mult).then_inc(colhot_ready, 1)
            for i in range(2):
                g.wait_ge(x2n_in[i], 32 * NT // 2)

            def step3(m, u):
                n = 2 * m + u
                for q in range(NG):
                    if q == 2 and has3(m, u, 3) and has3(m, u, 1):
                        slot = (u + 1) % 2
                        wait_apart(g, w1_lo, NG * (n + 2))
                        g.wait_ge(w2_lo, NG * (n + 2))
                        wait_apart(g, weight_rows_staged, n + 4)
                        load_weights(slot)
                    if q == 2 and has3(m, u, 3):
                        slot = (u + 1) % 2
                        if has3(m, u, 1):
                            wait_apart(g, slot_transposed, n + 2)
                        wait_apart(g, tokens_staged, n + 4)
                        for a in range(2):
                            nc.gpsimd.indirect_dma_start(xraw[:, slot, a, :], None, x_rows, bass.IndirectOffsetOnAxis(xist[:, slot, a:a + 1], 0)).then_inc(x_in[slot], 16)
                    if q == 3 and has3(m, u, -1):
                        slot = (u + 1) % 2
                        wait_apart(g, result_rows_staged, n)
                        wait_apart(g, result_out, n)
                        for a in range(2):
                            nc.gpsimd.indirect_dma_start(y_rows, bass.IndirectOffsetOnAxis(yist[:, slot, a:a + 1], 0), yst[:, slot, a, :], None).then_inc(y_out[slot], 16)
                    k, gr = (q + SPLIT) // NG, (q + SPLIT) % NG
                    if has3(m, u, k):
                        slot = (u + k) % 2
                        g.wait_ge(w1_hi, NG * (n + k) + gr + 1)
                        nc.gpsimd.tensor_tensor(split_part(slot, 1, gr, 0), raw_part(slot, gr, 0), split_part(slot, 0, gr, 0).bitcast(F32),
                                                ALU.subtract).then_inc(w1_lo, 1)

            expert_steps(g, step3)

            def add_residual(k):
                g.wait_ge(gamma_done, k + 1)
                g.wait_ge(beta_added, NB)
                nc.gpsimd.tensor_tensor(yo[k % 2], yo[k % 2], xs[:, BLK * k:BLK * (k + 1), :], ALU.add).then_inc(block_ready, 1)

            for k in range(NB):
                if k >= 2:
                    g.wait_ge(tile_normed, 4 * (2 * NB + k - 1))
                ln_rstd(g, 2 * NB + k, mvf[k % 2], rstdf[k % 2])
                g.wait_ge(rstd_done, 2 * (2 * NB + k) + 2)
                nc.gpsimd.tensor_tensor(nmr[k % 2], mvf[k % 2][:, :, 0], rstdf[k % 2], ALU.mult).then_inc(shift_step, 1)
                g.wait_ge(shift_step, 2 * k + 1)
                nc.gpsimd.tensor_scalar(nmr[k % 2], nmr[k % 2], -1.0, None, ALU.mult).then_inc(shift_step, 1)
                if k:
                    add_residual(k - 1)

        @block.scalar
        def _(act):
            act.wait_ge(first_in, 16 * NFIRST)

            def query_block(k):
                for c, done in enumerate((xT0_out, xT1_out)):
                    act.wait_ge(chunk_transposed, 2 * k + c + 1)
                    nc.scalar.copy(xT[:, c, :], ps[:, c, :]).then_inc(done, 1)
                for hf in range(C):
                    act.wait_ge(q_projected, 2 * k + hf + 1)
                    if later(k):
                        act.wait_ge(q_step_done, 5 * k)
                    nc.scalar.activation(qb[:, hf, :], ps[:, 2 + hf, :], ACT.Identity, bias=bcol[:, QX, hf:hf + 1]).then_inc(q_biased, 1)

            blocks(act, query_block)

            def step(j, u):
                if has(j, u, 0):
                    act.wait_ge(exp_transposed, 2 * (4 * j + u) + 1)
                    if has(j, u, -2):
                        act.wait_ge(pv_ready, 4 * j + u - 1)
                    nc.scalar.copy(pt[:, u % 2, 0], ps[:, 0, :]).then_inc(chunk0_out, 1)
                if has(j, u, 1):
                    m, slot = u + 1, (u + 1) % 4
                    if has(j, u, -3):
                        act.wait_ge(exp_transposed, 2 * (4 * j + u - 2))
                        act.wait_ge(diagonals_ready, 2 * (2 * j + (u - 3) // 2 + 1))
                    for g in range(4):
                        if g % 2 == 0:
                            act.wait_ge(max_ready, 2 * (4 * j + m) + g // 2 + 1)
                        nc.scalar.activation(pexp[:, slot, g, 0:S], ps[:, 3 + g, 0:S], ACT.Exp, bias=negmax[:, slot, g:g + 1],
                                             accum_out=rsum[:, slot, g:g + 1]).then_inc(exp_ready, 1)
                if has(j, u, 3):
                    m, slot = u + 3, (u + 3) % 2
                    if has(j, u, 1):
                        act.wait_ge(k_cos_done, 4 * j + u + 2)
                        act.wait_ge(k_sin_done, 4 * j + u + 2)
                    for hf in range(C):
                        act.wait_ge(keys_projected, 2 * (4 * j + m) + hf + 1)
                        nc.scalar.activation(kb[:, slot, hf, :], ps[:, hf, 0:SP], ACT.Identity, bias=bcol[:, KX, hf:hf + 1]).then_inc(keys_biased, 1)
                    act.wait_ge(values_projected, 4 * j + m + 1)
                    if has(j, u, -1):
                        act.wait_ge(pv_ready, 4 * j + u)
                    nc.scalar.copy(vv[:, m % 4].rearrange("p c d -> p (c d)"), ps[:, 2, :]).then_inc(values_out, 1)

            cross_steps(act, step)
            act.wait_ge(phase_ready, 2)

            def block2(k):
                for c in range(C):
                    act.wait_ge(chunk_transposed, 2 * (k + NB) + c + 1)
                    nc.scalar.copy(x_hl[:, 0, c], ps[:, c, :]).then_inc(block_hi, 1)
                for i, (dst, bias, scale, hf) in enumerate(((qt_all, bq4, HD ** -0.5, 0), (qt_all, bq4, HD ** -0.5, 1),
                                                            (kt_all, bcol[:, KA], 1.0, 0), (kt_all, bcol[:, KA], 1.0, 1))):
                    act.wait_ge(qk_projected, 4 * k + i + 1)
                    nc.scalar.activation(dst[:, hf, ds(512 * k, 512)], ps[:, (2, 3, 6, 7)[i], :], ACT.Identity, bias=bias[:, hf:hf + 1],
                                         scale=scale).then_inc(qk_out, 1)

            blocks(act, block2)

            def step2(m, u):
                if has2(m, u, -1):
                    n = 2 * m + u - 1
                    act.wait_ge(self_pv, n + 1)
                    if has2(m, u, -2):
                        act.wait_ge(odd_added, 2 * n)
                    for hf in range(C):
                        nc.scalar.activation(g1[:, hf], ps[:, 2:6, hf * 64:hf * 64 + T], ACT.Copy, scale=parity[:, 0:1]).then_inc(even_picked, 1)
                    act.wait_ge(self_transposed, n + 1)
                    if has2(m, u, -3):
                        act.wait_ge(router_ready, n - 1)
                    src = ps[:, 7, 0:D].rearrange("p (c t) -> p c t", c=C)
                    nc.scalar.copy(xt2[:, (u + 1) % 2], src).then_inc(xt2_out, 1)
                if has2(m, u, 1):
                    n, slot = 2 * m + u + 1, (u + 1) % 2
                    act.wait_ge(shifted_ready, n + 1)
                    if has2(m, u, -1):
                        act.wait_ge(probs_ready, n - 1)
                    nc.scalar.activation(pr[:, slot], shifted[:, slot], ACT.Exp).then_inc(self_exp, 1)

            self_steps(act, step2)
            act.wait_ge(route_step, 1)
            nc.scalar.activation(rexp, rdiff, ACT.Exp).then_inc(route_exp, 1)

            def step3(m, u):
                n = 2 * m + u
                for q in range(NG):
                    k, gr = (q + SPLIT) // NG, (q + SPLIT) % NG
                    if has3(m, u, k):
                        slot = (u + k) % 2
                        if gr == 0:
                            act.wait_ge(w_in[slot], nth2(m, u, k, 16))
                        if has3(m, u, k - 2):
                            act.wait_ge(hidden_ready, NG * (n + k - 2) + gr + 1)
                        nc.scalar.copy(split_part(slot, 0, gr, 0), raw_part(slot, gr, 0)).then_inc(w1_hi, 1)
                    k, gr = (q + LAG) // NG, (q + LAG) % NG
                    if has3(m, u, k):
                        slot, at = (u + k) % 2, NG * (n + k) + gr
                        act.wait_ge(hidden_ready, at + 1)
                        if gr == 0:
                            act.wait_ge(b1_staged, n + k + 1)
                        if gr >= 2 or has3(m, u, k - 1):
                            act.wait_ge(hidden_lo, at - 1)
                        if has3(m, u, k - 1):
                            act.wait_ge(second_done, at - 3)
                        for f in range(GF):
                            src, bias = ps[:, gr % 2, f * SLOT:(f + 1) * SLOT], bst[:, slot, GF * gr + f:GF * gr + f + 1]
                            nc.scalar.activation(hhl[:, gr, 0, f], src, ACT.Relu, bias=bias)
                            nc.scalar.activation(h32[:, gr % 2, f], src, ACT.Relu, bias=bias).then_inc(relu_ready, 1)
                    if q == 1 and has3(m, u, -1):
                        slot = (u + 1) % 2
                        act.wait_ge(second_done, NG * n)
                        if has3(m, u, -3):
                            act.wait_ge(y_out[slot], nth2(m, u, -3, 32))
                        nc.scalar.copy(yst[:, slot], ps[:, 4 + 2 * slot:6 + 2 * slot, 0:D]).then_inc(result_out, 1)
                    k = input_step(m, u, q)
                    if k is not None:
                        slot = (u + k) % 2
                        act.wait_ge(slot_transposed, n + k + 1)
                        if has3(m, u, k - 2):
                            act.wait_ge(hidden_ready, NG * (n + k - 1))
                        nc.scalar.copy(xhl[:, slot, 0].rearrange("p c t -> p (c t)"), ps[:, 2, :]).then_inc(slot_hi, 1)

            expert_steps(act, step3)
            for k in range(NB):
                act.wait_ge(shift_step, 2 * k + 2)
                if k:
                    act.wait_ge(gamma_done, k)
                for t in range(BLK):
                    nc.scalar.activation(xnrm[:, t, :], x2n[:, BLK * k + t, :], ACT.Identity, bias=nmr[k % 2][:, t:t + 1],
                                         scale=rstdf[k % 2][:, t:t + 1]).then_inc(tile_normed, 1)

        @block.vector
        def _(v):
            def tile_at(k):
                return lambda t: xs[:, ds(4 * k + t, 1), :].rearrange("p a d -> p (a d)")

            v.wait_ge(x_first_in, 16)
            ln_stats(v, tile_at(0), 0)
            ln_apply(v, tile_at(0), 0)
            v.wait_ge(x_rest_in, 16)
            ln_stats(v, tile_at(1), 1)
            v.wait_ge(first_in, 16 * NFIRST)
            for w, src in ((wk_hl, wx[:, 1]), (wv_hl, wx[:, 2])):
                nc.vector.tensor_copy(w[:, 0], src).then_inc(setup_step, 1)
            v.wait_ge(setup_step, 2)
            for w, src in ((wk_hl, wx[:, 1]), (wv_hl, wx[:, 2])):
                nc.vector.tensor_tensor(w[:, 1], src, w[:, 0].bitcast(F32), ALU.subtract).then_inc(setup_step, 1)
            for i, col in enumerate((VX, VA)):
                nc.vector.tensor_copy(bvb[:, i], bcol[:, col, :].unsqueeze(2).to_broadcast([P, C, P])).then_inc(setup_step, 1)
            by_pos = lambda a: a.rearrange("p c (b t) -> p (c b) t", t=T)
            by_pair = lambda a: a.rearrange("p c (i b t) -> p (c i) b t", b=2, t=T)
            by_latent = lambda a: a.rearrange("p c (i t b) -> p (c i) b t", b=2, t=T)
            for k in range(NB):
                if k + 1 < NB:
                    v.wait_ge(chunk_transposed, 2 * k + 2)
                    ln_apply(v, tile_at(k + 1), k + 1)
                if k + 2 < NB:
                    ln_stats(v, tile_at(k + 2), k + 2)
                block = slice(512 * k, 512 * (k + 1))
                v.wait_ge(q_biased, 2 * k + 2)
                nc.vector.tensor_tensor(by_pos(qs), by_pos(qb), const("qsin").unsqueeze(1).to_broadcast([P, C * BLK * 4, T]),
                                        ALU.mult).then_inc(q_step_done, 1)
                wait_apart(v, q_step_done, 5 * k + 1)
                nc.vector.stream_shuffle(qw, qs, [i ^ 1 for i in range(32)]).then_inc(q_step_done, 1)
                v.wait_ge(q_step_done, 5 * k + 2)
                v.wait_ge(q_cos_done, k + 1)
                nc.vector.tensor_tensor(by_latent(qb), by_pair(qc), by_pair(qw), ALU.add).then_inc(q_step_done, 1)
                v.wait_ge(q_step_done, 5 * k + 3)
                nc.vector.tensor_copy(q_hl[:, 0, :, block], qb).then_inc(q_step_done, 1)
                v.wait_ge(q_step_done, 5 * k + 4)
                nc.vector.tensor_tensor(q_hl[:, 1, :, block], qb, q_hl[:, 0, :, block].bitcast(F32), ALU.subtract).then_inc(q_step_done, 1)

            v.wait_ge(rest_in, 16 * NLOAD)
            v.wait_ge(bias_projected, 1)
            for i, row in enumerate((BOX, BOA)):
                nc.vector.tensor_tensor(ocorr[:, i, :], ps[:, 4, i * D:(i + 1) * D], brow[:, row, :], ALU.add).then_inc(setup_step, 1)
            v.wait_ge(last_projected, 1)
            nc.vector.tensor_copy(vlast[:], ps[:, 5, 0:C * B].rearrange("p (c b) -> p c b", c=C)).then_inc(setup_step, 1)

            def step(j, u):
                if u % 2 == 1 and has(j, u, 0):
                    pair, slot = 2 * j + u // 2, u // 2
                    v.wait_ge(exp_ready, 4 * (4 * j + u + 1))
                    if has(j, u, -4):
                        v.wait_ge(diagonals_ready, 2 * (pair - 1))
                    nc.vector.reciprocal(rrec[:, slot], rsum[:, u - 1:u + 1]).then_inc(sums_inverted, 1)
                if has(j, u, 0):
                    v.wait_ge(exp_transposed, 2 * (4 * j + u) + 2)
                    if has(j, u, -2):
                        v.wait_ge(pv_ready, 4 * j + u - 1)
                    nc.vector.tensor_copy(pt[:, u % 2, 1], ps[:, 1, :]).then_inc(chunk1_out, 1)
                if has(j, u, 1):
                    m, slot = u + 1, (u + 1) % 4
                    if has(j, u, -3):
                        v.wait_ge(exp_ready, 4 * (4 * j + u - 2))
                    for hf in range(C):
                        v.wait_ge(scores_ready, 2 * (4 * j + m) + hf + 1)
                        nc.vector.tensor_reduce(negmax[:, slot, 2 * hf:2 * hf + 2], ps[:, 3 + 2 * hf:5 + 2 * hf, 0:S], axis=AX,
                                                op=ALU.max, negate=True).then_inc(max_ready, 1)
                if has(j, u, 2):
                    m, slot = u + 2, (u + 2) % 2
                    n = 4 * j + m
                    v.wait_ge(keys_biased, 2 * (n + 1))
                    nc.vector.tensor_tensor(kc[:, slot], kb[:, slot], const("kcos").unsqueeze(1).to_broadcast([P, C, SP]),
                                            ALU.mult).then_inc(k_cos_done, 1)
                    if has(j, u, 0):
                        wait_apart(v, k_split, 2 * (4 * j + u + 1))
                    wait_apart(v, k_sin_done, n + 1)
                    nc.vector.stream_shuffle(kw[:, slot], ks[:, slot], [i ^ 1 for i in range(32)]).then_inc(k_swapped, 1)
                    v.wait_ge(k_swapped, n + 1)
                    v.wait_ge(k_cos_done, n + 1)
                    nc.vector.tensor_tensor(kw[:, slot], kc[:, slot], kw[:, slot], ALU.add).then_inc(k_rotated, 1)
                    v.wait_ge(k_rotated, n + 1)
                    if has(j, u, 0):
                        v.wait_ge(scores_ready, 2 * (4 * j + u + 1))
                    nc.vector.tensor_copy(khl[:, slot, 0], kw[:, slot]).then_inc(k_split, 1)
                    v.wait_ge(k_split, 2 * n + 1)
                    nc.vector.tensor_tensor(khl[:, slot, 1], kw[:, slot], khl[:, slot, 0].bitcast(F32), ALU.subtract).then_inc(k_split, 1)
                if u % 2 == 1 and has(j, u, 0):
                    pair = 2 * j + u // 2
                    both = ps[:, 7, 0:256].rearrange("p (b c r t) -> p b c r t", b=2, c=C, r=2)
                    sel = ps[:, 7, 256:512].rearrange("p (c w b t) -> p c w b t", c=C, w=2, b=2)
                    v.wait_ge(spread_ready, pair + 1)
                    nc.vector.tensor_scalar(f1[:].rearrange("p b c t -> p (b c) t"), both[:, :, :, 0, :].rearrange("p b c t -> p (b c) t"),
                                            parity[:, 0:1], None, ALU.mult).then_inc(finish_step, 1)
                    nc.vector.tensor_tensor(f3[:], sel[:, :, 0], vlast[:, :, ds(4 * j + u - 1, 2)].unsqueeze(3).to_broadcast([P, C, 2, T]),
                                            ALU.mult).then_inc(finish_step, 1)
                    v.wait_ge(finish_step, 4 * pair + 1)
                    nc.vector.scalar_tensor_tensor(f2[:].rearrange("p b c t -> p (b c) t"), both[:, :, :, 1, :].rearrange("p b c t -> p (b c) t"),
                                                   parity[:, 1:2], f1[:].rearrange("p b c t -> p (b c) t"), ALU.mult, ALU.add).then_inc(finish_step, 1)
                    v.wait_ge(finish_step, 4 * pair + 3)
                    nc.vector.tensor_tensor(f4[:], f3[:], f2[:].rearrange("p b c t -> p c b t"), ALU.add).then_inc(finish_step, 1)
                    v.wait_ge(finish_step, 4 * pair + 4)
                    nc.vector.tensor_tensor(attn_t[:, :, ds(128 * j + 32 * (u - 1), 2 * T)].rearrange("p c (b t) -> p c b t", t=T), f4[:],
                                            sel[:, :, 1], ALU.mult).then_inc(pair_done, 1)

            cross_steps(v, step)
            v.wait_ge(pv_ready, B)
            nc.vector.tensor_scalar(bq4[:], bcol[:, QA, :], HD ** -0.5, None, ALU.mult).then_inc(phase_ready, 1)

            v.wait_ge(xs_biased, 1 + NT)

            def add_and_norm(k):
                for t in range(BLK):
                    v.wait_ge(out_projected, 4 * k + t // 2 * 2 + 2)
                    nc.vector.tensor_tensor(tile_at(k)(t), ps[:, 4 + t // 2, t % 2 * D:(t % 2 + 1) * D], tile_at(k)(t), ALU.add).then_inc(tile_added, 1)
                wait_apart(v, tile_added, 4 * k + 4)
                ln_stats(v, tile_at(k), k + NB)
                ln_apply(v, tile_at(k), k + NB)

            nc.vector.tensor_copy(wa_hl[:, 0], wa[:, 0:3]).then_inc(wa_split, 1)
            v.wait_ge(wa_split, 1)
            nc.vector.tensor_tensor(wa_hl[:, 1], wa[:, 0:3], wa_hl[:, 0].bitcast(F32), ALU.subtract).then_inc(wa_split, 1)
            add_and_norm(0)

            def block2(k):
                for c in range(C):
                    v.wait_ge(block_hi, 2 * k + c + 1)
                    nc.vector.tensor_tensor(x_hl[:, 1, c], ps[:, c, :], x_hl[:, 0, c].bitcast(F32), ALU.subtract).then_inc(block_lo, 1)
                if not isinstance(k, int) or k < NB - 1:
                    add_and_norm(k + 1)
                for i in range(2):
                    v.wait_ge(v_projected, 2 * k + i + 1)
                    nc.vector.tensor_copy(v_all[:, ds(4 * k + 2 * i, 2), :].rearrange("p a d -> p (a d)"), ps[:, 4 + i, :]).then_inc(v_out, 1)

            ahead_blocks(v, block2)

            def step2(m, u):
                slot, nslot = u, (u + 1) % 2
                n = 2 * m + u
                scores = ps[:, nslot, :].rearrange("p (h k) -> p h k", h=H)

                def rank_pass(i):
                    if not has2(m, u, 1):
                        return
                    if i == 0:
                        wait_apart(v, self_scores, n + 2)
                    else:
                        wait_apart(v, rank_step, 64 * (n + 1) + 16 * i)
                    for h in range(H):
                        if i == 0:
                            ins = nc.vector.max(top_a[:, nslot, h, :], scores[:, h, :])
                        elif i == 1:
                            ins = nc.vector.match_replace(left_a[:, h, :], top_a[:, nslot, h, :], scores[:, h, :], TAKEN)
                        elif i == 2:
                            ins = nc.vector.max(top_b[:, h, :], left_a[:, h, :])
                        else:
                            ins = nc.vector.match_replace(left_b[:, h, :], top_b[:, h, :], left_a[:, h, :], TAKEN)
                        ins.then_inc(rank_step, 1)

                rank_pass(0)
                if has2(m, u, -2):
                    v.wait_ge(router_ready, n - 1)
                    nc.vector.tensor_tensor(logits[:, ds(n - 2, 1), :].rearrange("p a e -> p (a e)"), ps[:, 6, D:D + E], br[:], ALU.add).then_inc(logits_ready, 1)
                if has2(m, u, -1):
                    if has2(m, u, -3):
                        v.wait_ge(self_projected, n - 2)
                    v.wait_ge(even_picked, 2 * n)
                    for hf in range(C):
                        nc.vector.scalar_tensor_tensor(at2[:, nslot, hf].rearrange("p (b t) -> p b t", t=T),
                                                       ps[:, 2:6, hf * 64 + T:hf * 64 + 2 * T], parity[:, 1:2], g1[:, hf],
                                                       ALU.mult, ALU.add).then_inc(odd_added, 1)
                if has2(m, u, 0):
                    wait_apart(v, self_exp, n + 1)
                    nc.vector.tensor_reduce(prs[:], pr[:, slot], axis=AX, op=ALU.add).then_inc(self_sums, 1)
                    v.wait_ge(self_sums, 2 * n + 1)
                    nc.vector.reciprocal(prr[:], prs[:]).then_inc(self_sums, 1)
                rank_pass(1)
                if has2(m, u, 0):
                    if has2(m, u, -2):
                        v.wait_ge(self_pv, n - 1)
                    v.wait_ge(probs_ready, n + 1)
                    nc.vector.transpose(prt[:, slot].rearrange("p h k -> p (h k)"), prn[:].rearrange("p h k -> p (h k)")).then_inc(probs_transposed, 1)
                if has2(m, u, -1):
                    row = xs[:, ds(n - 1, 1), :].rearrange("p a d -> p (a d)")
                    v.wait_ge(self_projected, n)
                    nc.vector.tensor_tensor(row, ps[:, 6, 0:D], row, ALU.add).then_inc(self_added, 1)
                    wait_apart(v, self_added, n)
                    nc.vector.bn_stats(stats[:, 0, :], row).then_inc(self_stats, 1)
                    wait_apart(v, self_stats, 2 * n - 1)
                    nc.vector.bn_aggr(st2[:, 0:2], stats[:, 0, :]).then_inc(self_stats, 1)
                rank_pass(2)
                if has2(m, u, -1):
                    v.wait_ge(self_rstd, 2 * n)
                    if has2(m, u, -3):
                        v.wait_ge(x2n_in[nslot], nth2(m, u, -3, 32))
                        v.wait_ge(self_transposed, n - 2)
                    nc.vector.tensor_scalar(xn2[:, nslot], row, st2[:, 0:1], rstd[:, 0:1], ALU.subtract, ALU.mult).then_inc(self_normed, 1)
                rank_pass(3)
                if has2(m, u, 1):
                    if has2(m, u, -1):
                        v.wait_ge(shifted_ready, n)
                    wait_apart(v, rank_step, 64 * (n + 2))
                    nc.vector.scalar_tensor_tensor(kept[:, nslot], left_b[:], 0.1 * TAKEN, scores, ALU.is_lt, ALU.mult).then_inc(kept_ready, 1)
                    nc.vector.tensor_scalar(rmax[:, nslot], top_a[:, nslot, :, 0], 0.0, None, ALU.max).then_inc(kept_ready, 1)

            self_steps(v, step2)

            v.wait_ge(logits_ready, NT)
            for t in range(NT):
                nc.vector.max(rank[:, t, :], logits[:, t, :]).then_inc(ranks_ready, 1)
            v.wait_ge(ranks_ready, NT)
            for t in range(NT):
                nc.vector.max_index(rix[:, t, :], rank[:, t, :], logits[:, t, :]).then_inc(ranks_ready, 1)
            nc.vector.tensor_tensor(rdiff, rank[:, :, 1], rank[:, :, 0], ALU.subtract).then_inc(route_step, 1)
            v.wait_ge(ranks_ready, 2 * NT)
            nc.vector.tensor_copy(rixf, rix[:, :, 0:2]).then_inc(route_step, 1)
            v.wait_ge(route_exp, 1)
            nc.vector.tensor_scalar(rtmp, rexp, 1.0, None, ALU.add).then_inc(route_step, 1)
            v.wait_ge(route_step, 3)
            nc.vector.reciprocal(rwt[:, :, 0], rtmp).then_inc(route_step, 1)
            v.wait_ge(route_step, 4)
            nc.vector.tensor_tensor(rwt[:, :, 1], rwt[:, :, 0], rexp, ALU.mult).then_inc(route_step, 1)
            for i in range(2):
                nc.vector.tensor_tensor(hot[:, i], const("iota").unsqueeze(1).to_broadcast([P, NT, E]),
                                        rixf[:, :, i:i + 1].to_broadcast([P, NT, E]), ALU.is_equal).then_inc(route_step, 1)
            v.wait_ge(route_step, 7)
            for i in range(2):
                nc.vector.tensor_tensor(hw[:, i], hot[:, i], rwt[:, :, i:i + 1].to_broadcast([P, NT, E]), ALU.mult).then_inc(route_step, 1)
            nc.vector.tensor_tensor(hsum, hot[:, 0], hot[:, 1], ALU.add).then_inc(route_step, 1)
            v.wait_ge(route_step, 9)
            nc.vector.tensor_tensor(rw, hw[:, 0], hw[:, 1], ALU.add).then_inc(route_step, 1)

            done = [0]

            def pos(ins):
                ins.then_inc(position_step, 1)
                done[0] += 1
                v.wait_ge(position_step, done[0])

            within = ps[:, 3, 0:NT * E].rearrange("p (t e) -> p t e", e=E)
            totals = ps[:, 3, NT * E:2 * NT * E].rearrange("p (t e) -> p t e", e=E)
            v.wait_ge(counts_ready, 1)
            pos(nc.vector.tensor_copy(cnt[:, 0], totals))
            for i in range(4):
                d, a, b = 1 << i, i % 2, (i + 1) % 2
                pos(nc.vector.tensor_copy(cnt[:, b, 0:d], cnt[:, a, 0:d]))
                pos(nc.vector.tensor_tensor(cnt[:, b, d:NT], cnt[:, a, d:NT], cnt[:, a, 0:NT - d], ALU.add))
            pos(nc.vector.tensor_tensor(over, cnt[:, 0, NT - 1:NT, :].rearrange("p a e -> p e a").to_broadcast([P, E, TOK // SLOT]),
                                        const("steps").unsqueeze(1).to_broadcast([P, E, TOK // SLOT]), ALU.is_gt))
            pos(nc.vector.tensor_reduce(tl, over, axis=AX, op=ALU.add))
            pos(nc.vector.tensor_copy(st8[:, 0], tl))
            for i in range(3):
                d, a, b = 1 << i, i % 2, (i + 1) % 2
                pos(nc.vector.tensor_copy(st8[:, b, 0:d], st8[:, a, 0:d]))
                pos(nc.vector.tensor_tensor(st8[:, b, d:E], st8[:, a, d:E], st8[:, a, 0:E - d], ALU.add))
            pos(nc.vector.tensor_tensor(start, st8[:, 1], tl, ALU.subtract))
            pos(nc.vector.tensor_tensor(below, start[:, 1:E].unsqueeze(1).to_broadcast([P, NS, E - 1]),
                                        const("slot_no").unsqueeze(2).to_broadcast([P, NS, E - 1]), ALU.is_le))
            pos(nc.vector.tensor_reduce(eix, below, axis=AX, op=ALU.add))
            pos(nc.vector.tensor_scalar(eix, eix, float(P), const("part"), ALU.mult, ALU.add))
            pos(nc.vector.tensor_copy(eixu[:], eix))
            nc.vector.tensor_copy(ist[:], eixu[:, 0:2]).then_inc(weight_rows_staged, 2)
            pos(nc.vector.tensor_tensor(cnt[:, 1], cnt[:, 0], totals, ALU.subtract))
            pos(nc.vector.tensor_tensor(cnt[:, 0], cnt[:, 1], within, ALU.add))
            pos(nc.vector.tensor_scalar(st8[:, 0], start, float(SLOT), None, ALU.mult))
            pos(nc.vector.tensor_tensor(cnt[:, 1], cnt[:, 0], st8[:, 0:1].to_broadcast([P, NT, E]), ALU.add))
            for i in range(2):
                pos(nc.vector.tensor_tensor(hot[:, i], hot[:, i], cnt[:, 1], ALU.mult))
                pos(nc.vector.tensor_reduce(posf[:, i], hot[:, i], axis=AX, op=ALU.add))
            pos(nc.vector.tensor_copy(posu[:], posf))
            assert done[0] == NPOS
            flat_pos = posu[:].rearrange("p i t -> p (i t)")
            nc.vector.tensor_scalar(bitu[:, 0], flat_pos, P - 1, None, ALU.bitwise_and).then_inc(bits_step, 1)
            nc.vector.tensor_scalar(bitu[:, 1], flat_pos, P.bit_length() - 1, None, ALU.logical_shift_right).then_inc(bits_step, 1)
            for i in range(2):
                v.wait_ge(bits_step, i + 1)
                nc.vector.tensor_copy(bitf[:, i], bitu[:, i]).then_inc(bits_step, 1)
            for i in range(2):
                v.wait_ge(x2n_in[i], 32 * NT // 2)
            for c in range(NJ // PIECE):
                if c == 0:
                    v.wait_ge(bits_step, 4)
                if c >= 2:
                    v.wait_ge(table_piece, c - 1)
                nc.vector.tensor_tensor(colhot[c % 2], bitf[:, 1, PIECE * c:PIECE * (c + 1)].unsqueeze(2).to_broadcast([P, PIECE, NCOL]),
                                        const("col_no").unsqueeze(1).to_broadcast([P, PIECE, NCOL]), ALU.is_equal).then_inc(coleq_ready, 1)
                nc.vector.tensor_tensor(rowhot[c % 2], bitf[:, 0, PIECE * c:PIECE * (c + 1)].unsqueeze(2).to_broadcast([P, PIECE, P]),
                                        const("row_no").unsqueeze(1).to_broadcast([P, PIECE, P]), ALU.is_equal).then_inc(rowhot_ready, 1)
            v.wait_ge(table_piece, NJ // PIECE)
            nc.vector.tensor_copy(resf[:, 0], ps[:, 4, 0:NCOL]).then_inc(table_step, 1)
            v.wait_ge(table_step, 1)
            nc.vector.tensor_scalar(resf[:, 1], resf[:, 0], float(TOK - 1), None, ALU.add).then_inc(table_step, 1)
            nc.vector.scalar_tensor_tensor(resf[:, 2], resf[:, 0], 0.0, const("spare"), ALU.is_equal, ALU.mult).then_inc(table_step, 1)
            v.wait_ge(table_step, 2)
            nc.vector.tensor_copy(tok_of[:], resf[:, 1]).then_inc(table_step, 1)
            v.wait_ge(table_step, 3)
            nc.vector.tensor_tensor(resf[:, 0], resf[:, 0], resf[:, 2], ALU.add).then_inc(table_step, 1)
            v.wait_ge(table_step, 4)
            nc.vector.tensor_scalar(tok_of[:], tok_of[:], TOK - 1, None, ALU.bitwise_and).then_inc(table_step, 1)
            v.wait_ge(table_step, 5)
            nc.vector.tensor_copy(res_of[:], resf[:, 0]).then_inc(table_step, 1)
            v.wait_ge(table_step, 7)

            def step3(m, u):
                n = 2 * m + u
                for q in range(NG):
                    if q == 0 and has3(m, u, -1):
                        slot = (u + 1) % 2
                        if has3(m, u, -3):
                            v.wait_ge(y_out[slot], nth2(m, u, -3, 32))
                        nc.vector.tensor_copy(yist[:, slot], res_of[:, ds(2 * n - 2, 2)]).then_inc(result_rows_staged, 1)
                    if q == 2 and has3(m, u, 3):
                        slot = (u + 1) % 2
                        if has3(m, u, 1):
                            v.wait_ge(w_in[slot], nth2(m, u, 1, 16))
                            nc.vector.tensor_copy(ist[:, slot:slot + 1], eixu[:, ds(n + 3, 1)]).then_inc(weight_rows_staged, 1)
                            v.wait_ge(x_in[slot], nth2(m, u, 1, 32))
                        nc.vector.tensor_copy(xist[:, slot], tok_of[:, ds(2 * n + 6, 2)]).then_inc(tokens_staged, 1)
                    k, gr = (q + SPLIT) // NG, (q + SPLIT) % NG
                    if has3(m, u, k):
                        slot, at = (u + k) % 2, NG * (n + k) + gr
                        if gr == 0:
                            v.wait_ge(w_in[slot], nth2(m, u, k, 16))
                            if has3(m, u, k - 2):
                                v.wait_ge(relu_ready, FC * (n + k - 1))
                            nc.vector.tensor_copy(bst[:, slot], wraw[:, slot, 2 * D * FC:]).then_inc(b1_staged, 1)
                        if has3(m, u, k - 2):
                            v.wait_ge(second_done, at - 2 * NG + 1)
                        nc.vector.tensor_copy(split_part(slot, 0, gr, 1), raw_part(slot, gr, 1)).then_inc(w2_hi, 1)
                        v.wait_ge(w2_hi, at + 1)
                        nc.vector.tensor_tensor(split_part(slot, 1, gr, 1), raw_part(slot, gr, 1), split_part(slot, 0, gr, 1).bitcast(F32),
                                                ALU.subtract).then_inc(w2_lo, 1)
                    k, gr = (q + LAG) // NG, (q + LAG) % NG
                    if has3(m, u, k):
                        v.wait_ge(relu_ready, FC * (n + k) + GF * (gr + 1))
                        nc.vector.tensor_tensor(hhl[:, gr, 1], h32[:, gr % 2], hhl[:, gr, 0].bitcast(F32), ALU.subtract).then_inc(hidden_lo, 1)
                    if isinstance(m, int) and q == 3 and 0 <= n - 2 * S1 < NB:
                        rows = xs[:, BLK * (n - 2 * S1):BLK * (n - 2 * S1 + 1), :]
                        nc.vector.tensor_tensor(rows, rows, brow[:, BETA, :].unsqueeze(1).to_broadcast([P, BLK, D]), ALU.add).then_inc(beta_added, 1)
                    k = input_step(m, u, q)
                    if k is not None:
                        slot = (u + k) % 2
                        v.wait_ge(slot_hi, n + k + 1)
                        nc.vector.tensor_tensor(xhl[:, slot, 1].rearrange("p c t -> p (c t)"), ps[:, 2, :],
                                                xhl[:, slot, 0].rearrange("p c t -> p (c t)").bitcast(F32), ALU.subtract).then_inc(slot_lo, 1)

            expert_steps(v, step3)
            for q in range(NB):
                v.wait_ge(router_w_transposed, q + 1)
                nc.vector.tensor_copy(rwT[:, 4 * q:4 * q + 4, :].rearrange("e a p -> e (a p)"), ps[0:E, q, :]).then_inc(router_w_out, 1)

            def add_b2(q):
                v.wait_ge(b2_product, q + 1)
                pair = x2n[:, 2 * q:2 * q + 2, :].rearrange("p a d -> p (a d)")
                nc.vector.tensor_tensor(pair, ps[:, 4 + q % 4, :], pair, ALU.add).then_inc(b2_added, 1)

            def combine(k):
                v.wait_ge(b2_added, 2 * k + 2)
                v.wait_ge(g_in[k], 32)
                for i in range(2):
                    for t in range(BLK * k, BLK * (k + 1)):
                        if i:
                            v.wait_ge(combined, BLK * k + t + 1)
                        nc.vector.scalar_tensor_tensor(x2n[:, t, :], yg[:, i, t, :], rwt[:, t, i:i + 1], x2n[:, t, :],
                                                       ALU.mult, ALU.add).then_inc(combined, 1)

            def stats_of(k):
                v.wait_ge(combined, 2 * BLK * (k + 1))
                if k >= 2:
                    v.wait_ge(shift_step, 2 * k - 2)
                ln_stats(v, lambda t: x2n[:, BLK * k + t, :], 2 * NB + k, mvf[k % 2])

            for q in range(NT // 2):
                add_b2(q)
                if q == BLK - 1:
                    combine(0)
                if q == 5:
                    stats_of(0)
            for k in range(NB - 1):
                combine(k + 1)
                stats_of(k + 1)
                v.wait_ge(tile_normed, 4 * (2 * NB + k) + 4)
                if k >= 2:
                    v.wait_ge(stored[k % 2], 16)
                nc.vector.tensor_tensor(yo[k % 2], xnrm[:], brow[:, GAMMA, :].unsqueeze(1).to_broadcast([P, BLK, D]), ALU.mult).then_inc(gamma_done, 1)
            v.wait_ge(stored[(NB - 1) % 2], 16 * ((NB - 1) // 2))
            for hf in range(2):
                half = slice(BLK // 2 * hf, BLK // 2 * (hf + 1))
                v.wait_ge(tile_normed, 4 * (3 * NB - 1) + BLK // 2 * (hf + 1))
                nc.vector.tensor_tensor(yo[(NB - 1) % 2][:, half], xnrm[:, half], brow[:, GAMMA, :].unsqueeze(1).to_broadcast([P, BLK // 2, D]),
                                        ALU.mult).then_inc(gamma_done, 1)
                v.wait_ge(gamma_done, NB + hf)
                v.wait_ge(beta_added, NB)
                nc.vector.tensor_tensor(yo[(NB - 1) % 2][:, half], yo[(NB - 1) % 2][:, half], xs[:, BLK * (NB - 1) + half.start:BLK * (NB - 1) + half.stop, :],
                                        ALU.add).then_inc(half_ready, 1)

        @block.tensor
        def _(pe):
            pe.wait_ge(first_in, 16 * NFIRST)

            def query_block(k):
                transpose_block(pe, k)
                pe.wait_ge(xT0_out, k + 1)
                pe.wait_ge(xT1_out, k + 1)
                if later(k):
                    pe.wait_ge(q_biased, 2 * k)
                for hf in range(C):
                    for c in range(C):
                        ins = nc.tensor.matmul(ps[:, 2 + hf, :], wx[:, 0, c, hf * P:(hf + 1) * P], xT[:, c, :], start=c == 0, stop=c == C - 1)
                    ins.then_inc(q_projected, 1)

            blocks(pe, query_block)

            pe.wait_ge(rest_in, 16 * NLOAD)
            pe.wait_ge(setup_step, 6)
            for i, w in enumerate((wx, wa)):
                for c in range(C):
                    ins = nc.tensor.matmul(ps[:, 4, i * D:(i + 1) * D], bvb[:, i, c, :], w[:, 3, c, :], start=c == 0, stop=c == C - 1)
            ins.then_inc(bias_projected, 1)
            for hf in range(C):
                for c in range(C):
                    ins = nc.tensor.matmul(ps[:, 5, hf * B:(hf + 1) * B], wx[:, 2, c, hf * P:(hf + 1) * P], clast[:, c, :],
                                           start=c == 0, stop=c == C - 1)
            ins.then_inc(last_projected, 1)
            pe.wait_ge(q_biased, 2 * NB)
            pe.wait_ge(setup_step, 9)

            def split_product(dst, lhs, rhs, chunks):
                terms = [(a, b, c) for c in range(chunks) for a, b in ((0, 0), (0, 1), (1, 0))]
                for i, (a, b, c) in enumerate(terms):
                    ins = nc.tensor.matmul(dst, lhs(a, c), rhs(b, c), start=i == 0, stop=i == len(terms) - 1)
                return ins

            def step(j, u):
                if has(j, u, 0):
                    pe.wait_ge(exp_ready, 4 * (4 * j + u + 1))
                    if has(j, u, 2):
                        pe.wait_ge(keys_biased, 2 * (4 * j + u + 3))
                    for c in range(2):
                        for g in range(4):
                            ins = nc.tensor.transpose(ps[:, c, g * P:(g + 1) * P], pexp[:, u, g, c * P:(c + 1) * P], ident)
                        ins.then_inc(exp_transposed, 1)
                if has(j, u, 1):
                    m = u + 1
                    pair, slot = (m % 4) // 2, m % 2
                    pe.wait_ge(k_split, 2 * (4 * j + m + 1))
                    if m % 2 == 0:
                        pe.wait_ge(qbd_in[pair], (j + m // 4 + 1) * 16 * HH)
                    for g in range(4):
                        hf, gl = g // 2, g % 2
                        ins = split_product(ps[:, 3 + g, 0:SP],
                                            lambda a, c: qbd[:, pair, a, hf].rearrange("p h x -> p (h x)")[:, 8 * T * gl + slot:8 * T * (gl + 1):2],
                                            lambda b, c: khl[:, slot, b, hf, :], 1)
                        if gl == 1:
                            ins.then_inc(scores_ready, 1)
                if has(j, u, 0):
                    b = 4 * j + u
                    pe.wait_ge(chunk0_out, b + 1)
                    pe.wait_ge(chunk1_out, b + 1)
                    pe.wait_ge(values_out, b + 1)
                    if u % 2 == 0 and has(j, u, -1):
                        pe.wait_ge(pair_done, 2 * j + u // 2)
                    for hf in range(C):
                        for c in range(2):
                            for i in range(4):
                                col = (u % 2) * 128 + hf * 64
                                ins = nc.tensor.matmul(ps[32 * i:32 * i + 32, 7, col:col + 64],
                                                       vv[:, u, c, hf * P + 32 * i:hf * P + 32 * i + 32],
                                                       pt[:, u % 2, c, hf * 256 + 64 * i:hf * 256 + 64 * i + 64],
                                                       start=c == 0, stop=c == 1)
                    ins.then_inc(pv_ready, 1)
                    if u % 2 == 1:
                        pe.wait_ge(diagonals_ready, 2 * (2 * j + u // 2 + 1))
                        for hf in range(C):
                            for gl in range(2):
                                ins = nc.tensor.matmul(ps[:, 7, 256 + 128 * hf:384 + 128 * hf], const(f"pick{gl}"),
                                                       dg[:, u // 2, 2 * hf + gl].rearrange("p w b t -> p (w b t)"),
                                                       start=gl == 0, stop=gl == 1)
                        ins.then_inc(spread_ready, 1)
                if has(j, u, 3):
                    m, slot = u + 3, (u + 3) % 2
                    if has(j, u, 2) and not has(j, u, 0):
                        pe.wait_ge(keys_biased, 2 * (4 * j + m))
                    pe.wait_ge(ctx_split, 2 * (4 * j + m + 1))
                    for hf in range(C):
                        split_product(ps[:, hf, 0:SP], lambda a, c: wk_hl[:, a, c, hf * P:(hf + 1) * P],
                                      lambda b, c: cx[:, slot, b, c, :], C).then_inc(keys_projected, 1)
                    if has(j, u, 2):
                        pe.wait_ge(values_out, 4 * j + m)
                    for sc in range(2):
                        ins = split_product(ps[:, 2, sc * D:(sc + 1) * D], lambda a, c: cx[:, slot, a, c, sc * P:(sc + 1) * P],
                                            lambda b, c: wv_hl[:, b, c, :], C)
                    ins.then_inc(values_projected, 1)

            cross_steps(pe, step)
            pe.wait_ge(pair_done, B // 2)

            def project_out(k, values_read=None):
                if values_read is not None:
                    pe.wait_ge(v_out, values_read)
                pe.wait_ge(ast_in, 16 * (k + 1))
                for t in range(BLK):
                    for c in range(C):
                        ins = nc.tensor.matmul(ps[:, 4 + t // 2, t % 2 * D:(t % 2 + 1) * D], ast[:, c, t * P:(t + 1) * P], wx[:, 3, c, :],
                                               start=c == 0, stop=c == C - 1)
                    ins.then_inc(out_projected, 1)

            project_out(0)

            def block2(k):
                n = k + NB
                transpose_block(pe, n)
                if not isinstance(k, int) or k < NB - 1:
                    project_out(k + 1, 2 * k if later(k) else None)
                pe.wait_ge(wa_split, 2)
                pe.wait_ge(block_lo, 2 * k + 2)
                if later(k):
                    pe.wait_ge(qk_out, 4 * k)
                for i in range(4):
                    w, hf = i // 2, i % 2
                    split_product(ps[:, (2, 3, 6, 7)[i], :], lambda a, c: wa_hl[:, a, w, c, hf * P:(hf + 1) * P],
                                  lambda b, c: x_hl[:, b, c, :], C).then_inc(qk_projected, 1)
                if not isinstance(k, int) or k < NB - 1:
                    pe.wait_ge(tile_added, 4 * k + 8)
                for t in range(BLK):
                    ins = split_product(ps[:, 4 + t // 2, t % 2 * D:(t % 2 + 1) * D], lambda a, c: x_hl[:, a, c, t * P:(t + 1) * P],
                                        lambda b, c: wa_hl[:, b, 2, c, :], C)
                    if t % 2:
                        ins.then_inc(v_projected, 1)

            ahead_blocks(pe, block2)
            pe.wait_ge(v_out, 2 * NB)
            pe.wait_ge(qk_out, 4 * NB)

            def step2(m, u):
                n = 2 * m + u
                nslot = (u + 1) % 2
                if has2(m, u, -1):
                    pe.wait_ge(odd_added, 2 * n)
                    if has2(m, u, -2):
                        pe.wait_ge(logits_ready, n - 1)
                    for c in range(C):
                        ins = nc.tensor.matmul(ps[:, 6, 0:D], at2[:, nslot, c, :], wa[:, 3, c, :], start=c == 0, stop=c == C - 1)
                    ins.then_inc(self_projected, 1)
                if has2(m, u, 2):
                    slot = u
                    pe.wait_ge(kq_in[slot], nth2(m, u, 2, 16 * (HH + 1)))
                    if has2(m, u, 0):
                        pe.wait_ge(kept_ready, 2 * n + 2)
                    for b in range(4):
                        for hf in range(C):
                            ins = nc.tensor.matmul(ps[32 * b:32 * b + 32, slot, hf * 256:(hf + 1) * 256], qst[:, slot, hf, 32 * b:32 * b + 32],
                                                   kbd[:, slot, hf, :, 32 * b:32 * b + 32], start=True, stop=True)
                    ins.then_inc(self_scores, 1)
                if has2(m, u, 0):
                    wait_apart(pe, probs_transposed, n + 1)
                    wait_apart(pe, v_in[u], nth2(m, u, 0, 16))
                    if has2(m, u, -1):
                        wait_apart(pe, odd_added, 2 * n)
                    for hf in range(C):
                        for i in range(4):
                            for b in range(4):
                                ins = nc.tensor.matmul(ps[32 * i:32 * i + 32, 2 + b, hf * 64:hf * 64 + 64],
                                                       vst[32 * b:32 * b + 32, u, hf * P + 32 * i:hf * P + 32 * i + 32],
                                                       prt[32 * b:32 * b + 32, u, HH * hf + 2 * i:HH * hf + 2 * i + 2, :],
                                                       start=True, stop=True)
                    ins.then_inc(self_pv, 1)
                if has2(m, u, -1):
                    pe.wait_ge(self_normed, n)
                    if has2(m, u, -2):
                        pe.wait_ge(xt2_out, n - 1)
                    for c in range(C):
                        ins = nc.tensor.transpose(ps[:, 7, c * P:(c + 1) * P], xn2[:, nslot, c * P:(c + 1) * P], ident)
                    ins.then_inc(self_transposed, 1)
                    pe.wait_ge(self_added, n)
                    pe.wait_ge(xt2_out, n)
                    for c in range(C):
                        ins = nc.tensor.matmul(ps[:, 6, D:D + E], xt2[:, nslot, c, :], wr[:, c, :], start=c == 0, stop=c == C - 1)
                    ins.then_inc(router_ready, 1)

            self_steps(pe, step2)
            pe.wait_ge(logits_ready, NT)
            pe.wait_ge(xt2_out, NT)
            pe.wait_ge(route_step, 10)
            hs = hsum.rearrange("p t e -> p (t e)")
            nc.tensor.matmul(ps[:, 3, 0:NT * E], const("before"), hs, start=True, stop=True)
            nc.tensor.matmul(ps[:, 3, NT * E:2 * NT * E], const("ones"), hs, start=True, stop=True).then_inc(counts_ready, 1)
            for j in range(NJ):
                if j % PIECE == 0:
                    pe.wait_ge(rowhot_ready, j // PIECE + 1)
                    pe.wait_ge(colhot_ready, j // PIECE + 1)
                ins = nc.tensor.matmul(ps[:, 4, 0:NCOL], rowhot[j // PIECE % 2][:, j % PIECE, :], colhot[j // PIECE % 2][:, j % PIECE, :],
                                       start=j == 0, stop=j == NJ - 1)
                if j % PIECE == PIECE - 1:
                    ins.then_inc(table_piece, 1)

            def step3(m, u):
                n = 2 * m + u
                for q in range(NG):
                    k, gr = (q + LAG) // NG, (q + LAG) % NG
                    if has3(m, u, k):
                        slot, at = (u + k) % 2, NG * (n + k) + gr
                        pe.wait_ge(w1_lo, at + 1)
                        if gr == 0:
                            pe.wait_ge(slot_lo, n + k + 1)
                        if gr >= 2 or has3(m, u, k - 1):
                            pe.wait_ge(relu_ready, GF * (at - 1))
                        for f in range(GF):
                            ins = split_product(ps[:, gr % 2, f * SLOT:(f + 1) * SLOT],
                                                lambda a, c: whl[:, slot, a, GF * gr + f, c * P:(c + 1) * P],
                                                lambda b, c: xhl[:, slot, b, c, :], C)
                        ins.then_inc(hidden_ready, 1)
                    k = input_step(m, u, q)
                    if k is not None:
                        slot = (u + k) % 2
                        pe.wait_ge(x_in[slot], nth2(m, u, k, 32))
                        if has3(m, u, k - 1):
                            pe.wait_ge(slot_lo, n + k)
                        for c in range(C):
                            for t in range(2):
                                ins = nc.tensor.transpose(ps[:, 2, c * SLOT + t * P:c * SLOT + (t + 1) * P], xraw[:, slot, t, c * P:(c + 1) * P], ident)
                        ins.then_inc(slot_transposed, 1)
                    if has3(m, u, 0):
                        pe.wait_ge(w2_lo, NG * n + q + 1)
                        pe.wait_ge(hidden_lo, NG * n + q + 1)
                        if q == 0 and has3(m, u, -2):
                            pe.wait_ge(result_out, n - 1)
                        for t in range(2):
                            terms = [(a, b, f) for f in range(GF) for a, b in ((0, 0), (0, 1), (1, 0))]
                            for i, (a, b, f) in enumerate(terms):
                                ins = nc.tensor.matmul(ps[:, 4 + 2 * u + t, 0:D], hhl[:, q, a, f, t * P:(t + 1) * P], whl[:, u, b, GF * q + f, D:2 * D],
                                                       start=q == 0 and i == 0, stop=q == NG - 1 and i == len(terms) - 1)
                        ins.then_inc(second_done, 1)

            expert_steps(pe, step3)
            pe.wait_ge(result_out, NS)
            pe.wait_ge(b2_in, 16)
            for t in range(NT):
                ins = nc.tensor.transpose(ps[0:E, t // 4, t % 4 * P:(t % 4 + 1) * P], rw[:, t, :], ident)
                if t % 4 == 3:
                    ins.then_inc(router_w_transposed, 1)
            for t in range(NT):
                pe.wait_ge(router_w_out, t // 4 + 1)
                if t >= 8 and t % 2 == 0:
                    pe.wait_ge(b2_added, t // 2 - 3)
                ins = nc.tensor.matmul(ps[:, 4 + t // 2 % 4, t % 2 * D:(t % 2 + 1) * D], rwT[:, t, :], b2s[:], start=True, stop=True)
                if t % 2:
                    ins.then_inc(b2_product, 1)


def kernel(**inputs):
    import concourse.bacc as bacc
    from concourse.bass_utils import run_bass_kernel_spmd as run

    a = {k: np.asarray(v) for k, v in inputs.items()}

    def chunked(w, n=C):
        return w.reshape(n, P, -1).transpose(1, 0, 2)

    ctx = a["ctx_1024"].transpose(0, 2, 1).reshape(B, C, P, S).transpose(0, 2, 1, 3)
    arrays = {
        "x": a["x"].reshape(TOK, D),
        "ctx_t": np.pad(ctx, ((0, 0), (0, 0), (0, 0), (0, SP - S))),
        "ctx_last": ctx[:, :, :, S - 1].transpose(1, 2, 0),
        "w_x": np.stack([chunked(a[f"L0_xattn_W{n}"].T) for n in "qkvo"], 1),
        "w_a": np.stack([chunked(a[f"L0_attn_W{n}"]) for n in "qkvo"], 1),
        "bias_cols": np.stack([a[f"L0_{m}_b{n}"].reshape(C, P).T for m in ("xattn", "attn") for n in "qkv"], 1),
        "bias_rows": np.stack([np.broadcast_to(r, (P, D)) for r in (a["L0_xattn_bo"], a["L0_attn_bo"], a["L0_ffn_gamma"], a["L0_ffn_beta"])], 1),
        "w_r": chunked(a["L0_ffn_Wr"].T),
        "b_r": np.broadcast_to(a["L0_ffn_br"], (P, E)),
        "w_e": np.concatenate([np.concatenate([a["L0_ffn_W1"].reshape(E, FC, P, C, P).transpose(0, 4, 1, 3, 2).reshape(E, P, FC, D),
                                               a["L0_ffn_W2"].transpose(0, 2, 1).reshape(E, FC, P, D).transpose(0, 2, 1, 3)], 3)
                               .reshape(E, P, 2 * FC * D),
                               a["L0_ffn_b1"].reshape(E, FC, P).transpose(0, 2, 1)], 2).reshape(E * P, WROW),
        "b_2": a["L0_ffn_b2"],
        "consts": build_consts(),
    }
    nc = bacc.Bacc("TRN2", target_bir_lowering=False, num_devices=1)
    arrays = {f"{n}_dram": np.ascontiguousarray(v) for n, v in arrays.items()}
    args = [nc.dram_tensor(n, v.shape, F32, kind="ExternalInput").ap() for n, v in arrays.items()]
    args.append(nc.dram_tensor("out_dram", (TOK, D), F32, kind="ExternalOutput").ap())
    perceiver(nc, *args)
    return run(nc, [arrays], core_ids=[0]).results[0]["out_dram"].reshape(B, T, D)
```
